# Optimizing a Trainium2 kernel written in Bass

```python
import numpy as np
import jax
import jax.numpy as jnp

def _softmax(x, axis=-1):
    return jax.nn.softmax(x, axis=axis)

def _gelu(x):
    return jax.nn.gelu(x, approximate=True)

def _silu(x):
    return jax.nn.silu(x)

def _sigmoid(x):
    return jax.nn.sigmoid(x)

def _layernorm(x, axis=-1, eps=1e-05):
    m = jnp.mean(x, axis=axis, keepdims=True)
    v = jnp.var(x, axis=axis, keepdims=True)
    return (x - m) / jnp.sqrt(v + eps)

def _scatter_add(tgt, idx, src, axis=0):
    return tgt.at[idx].add(src)

def _segment_sum(src, seg, n):
    return jax.ops.segment_sum(src, seg, n)
kernel_name = 'mk_flamingo_gated_d2_seqx_r8_1b7cf7'

def setup_inputs(seed: int=0):
    np.random.seed(seed)
    _w = jnp.asarray

    def _rec_inputs():
        import jax
        import jax.numpy as jnp
        _rk = jax.random.key(seed)
        x = 7.22e-05 + 1 * jax.random.normal(jax.random.fold_in(_rk, 1), (16, 128, 256), jnp.float32)
        _lenS = 128 - jax.random.randint(jax.random.fold_in(_rk, 7), (16,), 0, max(1, 128 // 4) + 1, jnp.int32)
        _lenS2 = 128 - jax.random.randint(jax.random.fold_in(_rk, 8), (16,), 0, max(1, 128 // 4) + 1, jnp.int32)
        _ctx_2048P = jax.random.normal(jax.random.fold_in(_rk, 11), (16, 16, 256), jnp.float32)
        _ctx_2048c = jax.random.dirichlet(jax.random.fold_in(_rk, 511), 0.3 * jnp.ones((16,), jnp.float32), (16, 128))
        _ctx_2048t = jnp.einsum('bsk,bkd->bsd', _ctx_2048c, _ctx_2048P)
        _ctx_2048t = _ctx_2048t * jax.lax.rsqrt(jnp.mean(jnp.square(_ctx_2048t)) + 1e-12) * 0.953939
        ctx_2048 = 4.13588e-05 + 0.999923 * (_ctx_2048t + 0.3 * jax.random.normal(jax.random.fold_in(_rk, 611), (16, 128, 256), jnp.float32))
        _validS = jnp.arange(128)[None, :] < _lenS[:, None]
        _validS2 = jnp.arange(128)[None, :] < _lenS2[:, None]
        _causal = jnp.tril(jnp.ones((128, 128), dtype=bool))
        mask_SxS2_bc0 = jnp.logical_not(jnp.broadcast_to(_validS2[0:1, :], (128, 128)))
        mask_BxS2_bk0 = jnp.logical_not(jnp.broadcast_to(_validS2[:, :], (16, 128)))
        _g = jax.random.normal(jax.random.fold_in(_rk, 9001), (2, 2), jnp.float32)
        _g = jnp.sign(_g) * jnp.maximum(jnp.abs(_g), 1.0) + (_g == 0) * 1.0
        g_xattn = _g[0]
        g_ffn = _g[1]
        return (x, ctx_2048, mask_SxS2_bc0, mask_BxS2_bk0, g_xattn, g_ffn)
    x, ctx_2048, mask_SxS2_bc0, mask_BxS2_bk0, g_xattn, g_ffn = _rec_inputs()

    def _L0_xattn_setup():
        import jax, jax.numpy as jnp
        import numpy as np
        B, LQ, LKV = (4, 128, 128)
        HID, H, G = (256, 32, 8)
        HD = HID // H
        HPG = H // G
        key = jax.random.key(seed)
        ks = jax.random.split(key, 10)
        s = 0.02
        inp = {'X': jax.random.normal(ks[0], (B, LQ, HID), jnp.float32), 'encoder_output': jax.random.normal(ks[1], (B, LKV, HID), jnp.float32), 'causal_mask': jnp.triu(jnp.ones((LQ, LKV), bool), 1), 'padding_mask': jnp.zeros((B, LKV), bool).at[B // 2:, LKV - LKV // 4:].set(True), 'Wq': jax.random.normal(ks[2], (HID, HID), jnp.float32) * s, 'bq': jnp.zeros((HID,), jnp.float32), 'Wk': jax.random.normal(ks[3], (G * HD, HID), jnp.float32) * s, 'bk': jnp.zeros((G * HD,), jnp.float32), 'Wv': jax.random.normal(ks[4], (G * HD, HID), jnp.float32) * s, 'bv': jnp.zeros((G * HD,), jnp.float32), 'Wo': jax.random.normal(ks[5], (HID, HID), jnp.float32) * s, 'bo': jnp.zeros((HID,), jnp.float32)}
        return inp
    _L0_xattn_all = _L0_xattn_setup()
    _L0_xattn_in = {k: v for k, v in _L0_xattn_all.items() if k in ('Wq', 'bq', 'Wk', 'bk', 'Wv', 'bv', 'Wo', 'bo')}
    del _L0_xattn_all

    def _L0_ffn_setup():
        import jax, jax.numpy as jnp
        import numpy as np
        ACT_BITS = 8
        HIDDEN = 256
        INTERMEDIATE = 512
        EPS = 1e-05

        def fwht(x):
            shape = x.shape
            n = shape[-1]
            x = x.reshape(-1, n)
            h = 1
            while h < n:
                x = x.reshape(-1, n // (2 * h), 2, h)
                a, b = (x[:, :, 0, :], x[:, :, 1, :])
                x = jnp.stack((a + b, a - b), axis=2).reshape(-1, n)
                h *= 2
            return (x * (1.0 / np.sqrt(n))).reshape(shape)

        def _ste(x, q):
            return x + jax.lax.stop_gradient(q - x)

        def act_quant(x, bits):
            qb = float(2 ** (bits - 1) - 1)
            scale = qb / jnp.clip(jnp.max(jnp.abs(x), axis=-1, keepdims=True), EPS, None)
            q = jnp.clip(jnp.round(x * scale), -qb, qb) / scale
            return _ste(x, q)

        def weight_quant(w):
            scale = jnp.clip(jnp.mean(jnp.abs(w)), EPS, None)
            q = jnp.clip(jnp.round(w / scale), -1.0, 1.0) * scale
            return _ste(w, q)

        def hbitlinear(x, w, bits):
            xq = act_quant(fwht(x), bits)
            wq = weight_quant(w)
            return jnp.einsum('bsd,fd->bsf', xq, wq)
        key = jax.random.key(seed)
        k1, k2, k3 = jax.random.split(key, 3)
        hidden_states = jax.random.normal(k1, (4, 512, HIDDEN), dtype=jnp.float32)
        w_up = jax.random.normal(k2, (INTERMEDIATE, HIDDEN), dtype=jnp.float32) * 0.02
        w_down = jax.random.normal(k3, (HIDDEN, INTERMEDIATE), dtype=jnp.float32) * 0.02
        return {'hidden_states': hidden_states, 'w_up': w_up, 'w_down': w_down}
    _L0_ffn_all = _L0_ffn_setup()
    _L0_ffn_in = {k: v for k, v in _L0_ffn_all.items() if k in ('w_up', 'w_down')}
    del _L0_ffn_all

    def _L1_xattn_setup():
        import jax, jax.numpy as jnp
        import numpy as np
        FP8_MAX = 448.0
        EPS = 1e-05

        def _fp8_roundtrip(x):
            return x.astype(jnp.float8_e4m3fn).astype(jnp.float32)

        def _div_clamp_fp8(x, scale):
            y = jnp.clip(x.astype(jnp.float32) / scale, -FP8_MAX, FP8_MAX)
            y = y.astype(jnp.bfloat16).astype(jnp.float32)
            return _fp8_roundtrip(y)

        def _ln(x, w, b):
            mu = jnp.mean(x, axis=-1, keepdims=True)
            var = jnp.mean(jnp.square(x - mu), axis=-1, keepdims=True)
            return (x - mu) * jax.lax.rsqrt(var + EPS) * w + b

        def _fp8_linear_pertensor(x, wq, w_scale, in_scale):
            xq = _div_clamp_fp8(x, in_scale)
            return jnp.einsum('bsi,oi->bso', xq * in_scale, wq) * w_scale

        def _gqa(q, k, v):
            scale = 1.0 / np.sqrt(q.shape[-1])
            scores = jnp.einsum('bsghd,btgd->bghst', q, k) * scale
            p = jax.nn.softmax(scores, axis=-1)
            return jnp.einsum('bghst,btgd->bsghd', p, v)
        key = jax.random.key(seed)
        ks = jax.random.split(key, 8)
        B, S, SC, H, NH, G, D = (2, 256, 64, 256, 16, 8, 128)

        def qw(k, out_f, in_f):
            w = jax.random.normal(k, (out_f, in_f), jnp.float32) * 0.02
            sc = jnp.max(jnp.abs(w)) / FP8_MAX
            return (_fp8_roundtrip(w / sc), sc.astype(jnp.float32))
        wq, wq_s = qw(ks[0], NH * D, H)
        wqx, wqx_s = qw(ks[1], NH * D, H)
        wk, wk_s = qw(ks[2], G * D, H)
        wv, wv_s = qw(ks[3], G * D, H)
        wproj, wp_s = qw(ks[4], H, 2 * NH * D)
        return {'hidden_states': jax.random.normal(ks[5], (B, S, H), jnp.float32), 'cond': jax.random.normal(ks[6], (B, SC, H), jnp.float32), 'ln_w': jnp.ones((H,), jnp.float32), 'ln_b': jnp.zeros((H,), jnp.float32), 'wq': wq, 'wq_scale': wq_s, 'q_in_scale': jnp.full((H,), 0.05, jnp.float32), 'wqx': wqx, 'wqx_scale': wqx_s, 'qx_in_scale': jnp.full((H,), 0.05, jnp.float32), 'wk': wk, 'wk_scale': wk_s, 'k_in_scale': jnp.full((H,), 0.05, jnp.float32), 'wv': wv, 'wv_scale': wv_s, 'v_in_scale': jnp.full((H,), 0.05, jnp.float32), 'w_kv_x': jax.random.normal(ks[7], (2 * G * D, H), jnp.float32) * 0.02, 'qln_w': jnp.ones((D,), jnp.float32), 'qln_b': jnp.zeros((D,), jnp.float32), 'kln_w': jnp.ones((D,), jnp.float32), 'kln_b': jnp.zeros((D,), jnp.float32), 'qxln_w': jnp.ones((D,), jnp.float32), 'qxln_b': jnp.zeros((D,), jnp.float32), 'kxln_w': jnp.ones((D,), jnp.float32), 'kxln_b': jnp.zeros((D,), jnp.float32), 'wproj': wproj, 'proj_w_scale': wp_s, 'proj_in_scale': jnp.asarray(0.05, jnp.float32), 'proj_smooth': jnp.full((2 * NH * D,), 0.05, jnp.float32)}
    _L1_xattn_all = _L1_xattn_setup()
    _L1_xattn_in = {k: v for k, v in _L1_xattn_all.items() if k in ('ln_w', 'ln_b', 'wq', 'wq_scale', 'q_in_scale', 'wqx', 'wqx_scale', 'qx_in_scale', 'wk', 'wk_scale', 'k_in_scale', 'wv', 'wv_scale', 'v_in_scale', 'w_kv_x', 'qln_w', 'qln_b', 'kln_w', 'kln_b', 'qxln_w', 'qxln_b', 'kxln_w', 'kxln_b', 'wproj', 'proj_w_scale', 'proj_in_scale', 'proj_smooth')}
    del _L1_xattn_all

    def _L1_ffn_setup():
        import jax, jax.numpy as jnp
        import numpy as np
        D_MODEL = 256
        MLP_RATIO = 4
        TOP_K = 2
        N_EXPERTS = 8
        D_INT = D_MODEL * MLP_RATIO // TOP_K
        BATCH, SEQ = (2, 512)
        key = jax.random.key(seed)
        kx, kr, ki, ko = jax.random.split(key, 4)
        x = jax.random.normal(kx, (BATCH, SEQ, D_MODEL), dtype=jnp.float32)
        Wr = jax.random.normal(kr, (N_EXPERTS, D_MODEL), dtype=jnp.float32) * 0.02
        Win = jax.random.normal(ki, (N_EXPERTS, D_INT, D_MODEL), dtype=jnp.float32) * 0.02
        Wout = jax.random.normal(ko, (N_EXPERTS, D_MODEL, D_INT), dtype=jnp.float32) * 0.02
        return {'x': x, 'Wr': Wr, 'Win': Win, 'Wout': Wout}
    _L1_ffn_all = _L1_ffn_setup()
    _L1_ffn_in = {k: v for k, v in _L1_ffn_all.items() if k in ('Wr', 'Win', 'Wout')}
    del _L1_ffn_all
    return {'x': x, 'ctx_2048': ctx_2048, 'mask_SxS2_bc0': mask_SxS2_bc0, 'mask_BxS2_bk0': mask_BxS2_bk0, 'g_xattn': g_xattn, 'g_ffn': g_ffn, 'L0_xattn_Wq': _L0_xattn_in['Wq'], 'L0_xattn_bq': _L0_xattn_in['bq'], 'L0_xattn_Wk': _L0_xattn_in['Wk'], 'L0_xattn_bk': _L0_xattn_in['bk'], 'L0_xattn_Wv': _L0_xattn_in['Wv'], 'L0_xattn_bv': _L0_xattn_in['bv'], 'L0_xattn_Wo': _L0_xattn_in['Wo'], 'L0_xattn_bo': _L0_xattn_in['bo'], 'L0_ffn_w_up': _L0_ffn_in['w_up'], 'L0_ffn_w_down': _L0_ffn_in['w_down'], 'L1_xattn_ln_w': _L1_xattn_in['ln_w'], 'L1_xattn_ln_b': _L1_xattn_in['ln_b'], 'L1_xattn_wq': _L1_xattn_in['wq'], 'L1_xattn_wq_scale': _L1_xattn_in['wq_scale'], 'L1_xattn_q_in_scale': _L1_xattn_in['q_in_scale'], 'L1_xattn_wqx': _L1_xattn_in['wqx'], 'L1_xattn_wqx_scale': _L1_xattn_in['wqx_scale'], 'L1_xattn_qx_in_scale': _L1_xattn_in['qx_in_scale'], 'L1_xattn_wk': _L1_xattn_in['wk'], 'L1_xattn_wk_scale': _L1_xattn_in['wk_scale'], 'L1_xattn_k_in_scale': _L1_xattn_in['k_in_scale'], 'L1_xattn_wv': _L1_xattn_in['wv'], 'L1_xattn_wv_scale': _L1_xattn_in['wv_scale'], 'L1_xattn_v_in_scale': _L1_xattn_in['v_in_scale'], 'L1_xattn_w_kv_x': _L1_xattn_in['w_kv_x'], 'L1_xattn_qln_w': _L1_xattn_in['qln_w'], 'L1_xattn_qln_b': _L1_xattn_in['qln_b'], 'L1_xattn_kln_w': _L1_xattn_in['kln_w'], 'L1_xattn_kln_b': _L1_xattn_in['kln_b'], 'L1_xattn_qxln_w': _L1_xattn_in['qxln_w'], 'L1_xattn_qxln_b': _L1_xattn_in['qxln_b'], 'L1_xattn_kxln_w': _L1_xattn_in['kxln_w'], 'L1_xattn_kxln_b': _L1_xattn_in['kxln_b'], 'L1_xattn_wproj': _L1_xattn_in['wproj'], 'L1_xattn_proj_w_scale': _L1_xattn_in['proj_w_scale'], 'L1_xattn_proj_in_scale': _L1_xattn_in['proj_in_scale'], 'L1_xattn_proj_smooth': _L1_xattn_in['proj_smooth'], 'L1_ffn_Wr': _L1_ffn_in['Wr'], 'L1_ffn_Win': _L1_ffn_in['Win'], 'L1_ffn_Wout': _L1_ffn_in['Wout']}

def reference(x, ctx_2048, mask_SxS2_bc0, mask_BxS2_bk0, g_xattn, g_ffn, L0_xattn_Wq, L0_xattn_bq, L0_xattn_Wk, L0_xattn_bk, L0_xattn_Wv, L0_xattn_bv, L0_xattn_Wo, L0_xattn_bo, L0_ffn_w_up, L0_ffn_w_down, L1_xattn_ln_w, L1_xattn_ln_b, L1_xattn_wq, L1_xattn_wq_scale, L1_xattn_q_in_scale, L1_xattn_wqx, L1_xattn_wqx_scale, L1_xattn_qx_in_scale, L1_xattn_wk, L1_xattn_wk_scale, L1_xattn_k_in_scale, L1_xattn_wv, L1_xattn_wv_scale, L1_xattn_v_in_scale, L1_xattn_w_kv_x, L1_xattn_qln_w, L1_xattn_qln_b, L1_xattn_kln_w, L1_xattn_kln_b, L1_xattn_qxln_w, L1_xattn_qxln_b, L1_xattn_kxln_w, L1_xattn_kxln_b, L1_xattn_wproj, L1_xattn_proj_w_scale, L1_xattn_proj_in_scale, L1_xattn_proj_smooth, L1_ffn_Wr, L1_ffn_Win, L1_ffn_Wout):
    import jax
    import jax.numpy as jnp

    def _L0_xattn_ref(X, encoder_output, causal_mask, padding_mask, Wq, bq, Wk, bk, Wv, bv, Wo, bo):
        import jax, jax.numpy as jnp
        import numpy as np
        B, LQ, LKV = (4, 128, 128)
        HID, H, G = (256, 32, 8)
        HD = HID // H
        HPG = H // G
        b = X.shape[0]
        q = X @ Wq.T + bq
        k = encoder_output @ Wk.T + bk
        v = encoder_output @ Wv.T + bv
        q = q.reshape(b, LQ, G, HPG, HD).transpose(0, 2, 3, 1, 4)
        k = k.reshape(b, LKV, G, HD).transpose(0, 2, 1, 3)
        v = v.reshape(b, LKV, G, HD).transpose(0, 2, 1, 3)
        scores = jnp.einsum('bgrqd,bgkd->bgrqk', q, k) / jnp.sqrt(jnp.float32(HD))
        scores = jnp.where(causal_mask[None, None, None, :, :], -jnp.inf, scores)
        scores = jnp.where(padding_mask[:, None, None, None, :], -jnp.inf, scores)
        w = jax.nn.softmax(scores, axis=-1)
        out = jnp.einsum('bgrqk,bgkd->bgrqd', w, v)
        out = out.reshape(b, H, LQ, HD).transpose(0, 2, 1, 3).reshape(b, LQ, HID)
        return out @ Wo.T + bo

    def _L0_ffn_ref(hidden_states, w_up, w_down):
        import jax, jax.numpy as jnp
        import numpy as np
        ACT_BITS = 8
        HIDDEN = 256
        INTERMEDIATE = 512
        EPS = 1e-05

        def fwht(x):
            shape = x.shape
            n = shape[-1]
            x = x.reshape(-1, n)
            h = 1
            while h < n:
                x = x.reshape(-1, n // (2 * h), 2, h)
                a, b = (x[:, :, 0, :], x[:, :, 1, :])
                x = jnp.stack((a + b, a - b), axis=2).reshape(-1, n)
                h *= 2
            return (x * (1.0 / np.sqrt(n))).reshape(shape)

        def _ste(x, q):
            return x + jax.lax.stop_gradient(q - x)

        def act_quant(x, bits):
            qb = float(2 ** (bits - 1) - 1)
            scale = qb / jnp.clip(jnp.max(jnp.abs(x), axis=-1, keepdims=True), EPS, None)
            q = jnp.clip(jnp.round(x * scale), -qb, qb) / scale
            return _ste(x, q)

        def weight_quant(w):
            scale = jnp.clip(jnp.mean(jnp.abs(w)), EPS, None)
            q = jnp.clip(jnp.round(w / scale), -1.0, 1.0) * scale
            return _ste(w, q)

        def hbitlinear(x, w, bits):
            xq = act_quant(fwht(x), bits)
            wq = weight_quant(w)
            return jnp.einsum('bsd,fd->bsf', xq, wq)
        h = hbitlinear(hidden_states, w_up, ACT_BITS)
        h = jnp.square(jax.nn.relu(h))
        return hbitlinear(h, w_down, ACT_BITS)

    def _L1_xattn_ref(hidden_states, cond, ln_w, ln_b, wq, wq_scale, q_in_scale, wqx, wqx_scale, qx_in_scale, wk, wk_scale, k_in_scale, wv, wv_scale, v_in_scale, w_kv_x, qln_w, qln_b, kln_w, kln_b, qxln_w, qxln_b, kxln_w, kxln_b, wproj, proj_w_scale, proj_in_scale, proj_smooth):
        import jax, jax.numpy as jnp
        import numpy as np
        FP8_MAX = 448.0
        EPS = 1e-05

        def _fp8_roundtrip(x):
            return x.astype(jnp.float8_e4m3fn).astype(jnp.float32)

        def _div_clamp_fp8(x, scale):
            y = jnp.clip(x.astype(jnp.float32) / scale, -FP8_MAX, FP8_MAX)
            y = y.astype(jnp.bfloat16).astype(jnp.float32)
            return _fp8_roundtrip(y)

        def _ln(x, w, b):
            mu = jnp.mean(x, axis=-1, keepdims=True)
            var = jnp.mean(jnp.square(x - mu), axis=-1, keepdims=True)
            return (x - mu) * jax.lax.rsqrt(var + EPS) * w + b

        def _fp8_linear_pertensor(x, wq, w_scale, in_scale):
            xq = _div_clamp_fp8(x, in_scale)
            return jnp.einsum('bsi,oi->bso', xq * in_scale, wq) * w_scale

        def _gqa(q, k, v):
            scale = 1.0 / np.sqrt(q.shape[-1])
            scores = jnp.einsum('bsghd,btgd->bghst', q, k) * scale
            p = jax.nn.softmax(scores, axis=-1)
            return jnp.einsum('bghst,btgd->bsghd', p, v)
        b, s, _ = hidden_states.shape
        sc = cond.shape[1]
        d = qln_w.shape[0]
        nh = wq.shape[0] // d
        g = wk.shape[0] // d
        hpg = nh // g
        ln_out = _ln(hidden_states, ln_w, ln_b)
        q = _fp8_linear_pertensor(ln_out, wq, wq_scale, q_in_scale).reshape(b, s, g, hpg, d)
        q = _ln(q, qln_w, qln_b)
        k = _fp8_linear_pertensor(ln_out, wk, wk_scale, k_in_scale).reshape(b, s, g, d)
        k = _ln(k, kln_w, kln_b)
        v = _fp8_linear_pertensor(ln_out, wv, wv_scale, v_in_scale).reshape(b, s, g, d)
        core = _gqa(q, k, v).reshape(b, s, nh * d)
        qx = _fp8_linear_pertensor(ln_out, wqx, wqx_scale, qx_in_scale).reshape(b, s, g, hpg, d)
        qx = _ln(qx, qxln_w, qxln_b)
        kvx = jnp.einsum('bsi,oi->bso', cond, w_kv_x)
        kx, vx = jnp.split(kvx, 2, axis=-1)
        kx = _ln(kx.reshape(b, sc, g, d), kxln_w, kxln_b)
        vx = vx.reshape(b, sc, g, d)
        xout = _gqa(qx, kx, vx).reshape(b, s, nh * d)
        cat = jnp.concatenate([core, xout], axis=-1)
        catq = _div_clamp_fp8(cat, proj_smooth)
        return jnp.einsum('bsi,oi->bso', catq, wproj) * (proj_in_scale * proj_w_scale)

    def _L1_ffn_ref(x, Wr, Win, Wout):
        import jax, jax.numpy as jnp
        import numpy as np
        D_MODEL = 256
        MLP_RATIO = 4
        TOP_K = 2
        N_EXPERTS = 8
        D_INT = D_MODEL * MLP_RATIO // TOP_K
        BATCH, SEQ = (2, 512)
        orig_shape = x.shape
        xf = x.reshape(-1, orig_shape[-1])
        T = xf.shape[0]
        logits = xf @ Wr.T
        scores, expert = jax.lax.top_k(logits, TOP_K)
        weights = jax.nn.softmax(scores, axis=-1)
        gate = jnp.zeros((T, N_EXPERTS), dtype=xf.dtype)
        gate = gate.at[jnp.arange(T)[:, None], expert].add(weights)
        y = jnp.zeros_like(xf)
        for e in range(N_EXPERTS):
            h = jax.nn.silu(xf @ Win[e].T)
            y = y + gate[:, e:e + 1] * (h @ Wout[e].T)
        return y.reshape(orig_shape)
    x = x + jnp.tanh(g_xattn[0]) * _L0_xattn_ref(_layernorm(x, axis=-1), ctx_2048, mask_SxS2_bc0, mask_BxS2_bk0, L0_xattn_Wq, L0_xattn_bq, L0_xattn_Wk, L0_xattn_bk, L0_xattn_Wv, L0_xattn_bv, L0_xattn_Wo, L0_xattn_bo)
    x = x + jnp.tanh(g_ffn[0]) * _L0_ffn_ref(_layernorm(x, axis=-1), L0_ffn_w_up, L0_ffn_w_down)
    x = x + jnp.tanh(g_xattn[1]) * _L1_xattn_ref(_layernorm(x, axis=-1), ctx_2048, L1_xattn_ln_w, L1_xattn_ln_b, L1_xattn_wq, L1_xattn_wq_scale, L1_xattn_q_in_scale, L1_xattn_wqx, L1_xattn_wqx_scale, L1_xattn_qx_in_scale, L1_xattn_wk, L1_xattn_wk_scale, L1_xattn_k_in_scale, L1_xattn_wv, L1_xattn_wv_scale, L1_xattn_v_in_scale, L1_xattn_w_kv_x, L1_xattn_qln_w, L1_xattn_qln_b, L1_xattn_kln_w, L1_xattn_kln_b, L1_xattn_qxln_w, L1_xattn_qxln_b, L1_xattn_kxln_w, L1_xattn_kxln_b, L1_xattn_wproj, L1_xattn_proj_w_scale, L1_xattn_proj_in_scale, L1_xattn_proj_smooth)
    x = x + jnp.tanh(g_ffn[1]) * _L1_ffn_ref(_layernorm(x, axis=-1), L1_ffn_Wr, L1_ffn_Win, L1_ffn_Wout)
    return x

_drawn_inputs = setup_inputs


def setup_inputs(seed=0):
    import zlib

    import numpy as np

    out = dict(_drawn_inputs(seed))
    spreads = {'g_ffn': (-1.0, 0.6),
     'L0_xattn_bq': (0.0, 0.8),
     'L0_xattn_bk': (0.0, 0.8),
     'L0_xattn_bv': (0.0, 0.27),
     'L0_xattn_bo': (0.0, 0.1),
     'L1_xattn_ln_w': (1.0, 0.6),
     'L1_xattn_ln_b': (0.0, 0.267),
     'L1_xattn_q_in_scale': (0.05000000074505806, 0.6),
     'L1_xattn_qx_in_scale': (0.05000000074505806, 0.6),
     'L1_xattn_k_in_scale': (0.05000000074505806, 0.6),
     'L1_xattn_v_in_scale': (0.05000000074505806, 0.6),
     'L1_xattn_qln_w': (1.0, 0.6),
     'L1_xattn_qln_b': (0.0, 0.8),
     'L1_xattn_kln_w': (1.0, 0.6),
     'L1_xattn_kln_b': (0.0, 0.8),
     'L1_xattn_qxln_w': (1.0, 0.6),
     'L1_xattn_qxln_b': (0.0, 0.8),
     'L1_xattn_kxln_w': (1.0, 0.6),
     'L1_xattn_kxln_b': (0.0, 0.8),
     'L1_xattn_proj_smooth': (0.05000000074505806, 0.2)}
    factors = {'L0_xattn_Wq': 8.0, 'L0_xattn_Wk': 8.0, 'L0_ffn_w_up': 4.591, 'L0_ffn_w_down': 4.247}
    for name, (base, spread) in spreads.items():
        noise = np.random.default_rng([zlib.crc32(name.encode()), seed]).standard_normal(out[name].shape)
        drawn = base * np.exp(spread * noise) if base else spread * noise
        out[name] = jnp.asarray(drawn.astype(out[name].dtype))
    for name, factor in factors.items():
        out[name] = (out[name] * factor).astype(out[name].dtype)
    return out
```

```python
import numpy as np

import concourse.bass as bass
from concourse import mybir
from concourse.alu_op_type import AluOpType as ALU

ACT = mybir.ActivationFunctionType
AX = mybir.AxisListType.X
F32 = mybir.dt.float32
F16 = mybir.dt.float16
BF16 = mybir.dt.bfloat16
U16 = mybir.dt.uint16
U32 = mybir.dt.uint32
U8 = mybir.dt.uint8

P = 128
B = 16
D = 256
KD = D // P
EPS = 1e-5
MAGIC = 1.5 * 2.0**23
MASKED = -1.0e30


class Flag:

    def __init__(self, nc, name, per=1):
        self.sem, self.per = nc.alloc_semaphore(name), per

    def prime(self, engine):
        engine.sem_inc(self.sem, self.per)

    def at(self, i, k=None):
        return (i + 1) * self.per + (self.per if k is None else k)


class Chain:

    def __init__(self, nc, name, per):
        self.sem, self.per, self.name = nc.alloc_semaphore(name), per, name

    def start(self, engine, i):
        self.engine, self.i, self.n = engine, i, 0

    def link(self, instruction):
        instruction.then_inc(self.sem, 1)
        self.n += 1
        self.engine.wait_ge(self.sem, self.i * self.per + self.n)

    def end(self):
        assert self.n == self.per, f"chain {self.name}: {self.n} links"


class Pieces:

    def __init__(self, nc):
        self.nc, self.flags, self.pieces = nc, {}, {}

    def flag(self, name, owner, per=1):
        s = Flag(self.nc, name, per)
        self.flags.setdefault(owner, []).append(s)
        return s

    def piece(self, name, engine):
        def keep(f):
            self.pieces[(name, engine)] = f
            return f
        return keep

    def run(self, block, before, body, after, loop):
        for owner, hook in (("tensor", block.tensor), ("vector", block.vector), ("scalar", block.scalar),
                            ("gpsimd", block.gpsimd), ("sync", block.sync)):
            self.program(owner, hook, before, body, after, loop)

    def program(self, owner, hook, before, body, after, loop):
        @hook
        def _(e):
            def emit(steps):
                for name, i, *more in steps:
                    if (name, owner) in self.pieces:
                        self.pieces[(name, owner)](e, i, *more)
            for s in self.flags.get(owner, []):
                s.prime(e)
            emit(before)
            if loop[1] > loop[0]:
                with e.Fori(*loop) as i:
                    emit(body(i))
            emit(after)


def col(ap):
    return ap.unsqueeze(2)


def spread(ap, n):
    return ap.unsqueeze(2).to_broadcast([ap.shape[0], ap.shape[1], n])


def tiled(ap, n):
    return ap.unsqueeze(1).to_broadcast([ap.shape[0], n, ap.shape[1]])




def prepare_common(nc, a):
    t = {}
    t["x"] = nc.alloc_sbuf_tensor("x_rows", [P, B, D], F32)
    t["gates"] = nc.alloc_sbuf_tensor("gates", [P, 4], F32)
    t["ident"] = nc.alloc_sbuf_tensor("ident", [P, P], F32)
    t["ident_b"] = nc.alloc_sbuf_tensor("ident_b", [P, P], BF16)
    t["ones"] = nc.alloc_sbuf_tensor("ones", [P, P], F32)
    t["half"] = nc.alloc_sbuf_tensor("minus_half", [P, 16], F32)
    t["one_eps"] = nc.alloc_sbuf_tensor("one_eps", [P, 1], F32)
    t["eps_eps"] = nc.alloc_sbuf_tensor("eps_eps", [P, 1], F32)
    t["eps"] = nc.alloc_sbuf_tensor("eps", [P, 16], F32)
    loaded, made, cast, gated = (nc.alloc_semaphore(n) for n in ("common_loaded", "ident_made", "common_cast", "gates_made"))
    with nc.Block() as block:
        @block.sync
        def _(e):
            for q in range(4):
                e.dma_start(t["x"][:, 4 * q:4 * q + 4, :],
                            a["x"][4 * q:4 * q + 4].rearrange("b p d -> p b d")).then_inc(loaded, 16)

        @block.gpsimd
        def _(e):
            e.memset(t["ident"][:, :], 0.0).then_inc(made, 1)
            e.wait_ge(made, 1)
            e.affine_select(out=t["ident"][:, :], in_=t["ident"][:, :], compare_op=ALU.not_equal, fill=1.0,
                            base=0, pattern=[[-1, P]], channel_multiplier=1).then_inc(made, 1)
            e.memset(t["ones"][:, :], 1.0).then_inc(made, 1)
            e.memset(t["half"][:, :], -0.5).then_inc(made, 1)
            e.memset(t["eps"][:, :], EPS).then_inc(made, 1)
            e.memset(t["one_eps"][:, :], 1.0 + EPS).then_inc(made, 1)
            e.memset(t["eps_eps"][:, :], EPS * EPS).then_inc(made, 1)
            e.wait_ge(made, 7)
            e.tensor_copy(t["ident_b"][:, :], t["ident"][:, :]).then_inc(cast, 1)
            e.wait_ge(cast, 1)

        @block.scalar
        def _(e):
            for n, g in enumerate((a["g_xattn"], a["g_ffn"])):
                e.dma_start(t["gates"][:, 2 * n:2 * n + 2],
                            g.unsqueeze(0).to_broadcast([P, 2])).then_inc(loaded, 16)
            e.wait_ge(loaded, 96)
            e.activation(t["gates"][:, :], t["gates"][:, :], ACT.Tanh).then_inc(gated, 1)
            e.wait_ge(gated, 1)
    return t



H0, G0, R0, HD0 = 32, 8, 4, 8
GP = 32
FF = 512
KF = FF // P


def layer0(nc, a, t, ctx):
    def sb(name, shape, dt=F32):
        return ctx.enter_context(nc.sbuf_tensor(name, shape, dt))

    x, gates, ident, ident_b = t["x"], t["gates"], t["ident"], t["ident_b"]
    ctxT = sb("ctxT", [P, KD, B * P])
    wq, wk = sb("wq0", [P, KD, D]), sb("wk0", [P, KD, D])
    wv = sb("wv0", [P, KD, G0 * HD0])
    wo = sb("wo0", [P, 2, R0, D])
    bq, bk = sb("bq0", [P, KD]), sb("bk0", [P, KD])
    bv, bo = sb("bv0", [P, G0 * HD0]), sb("bo0", [P, D])
    had1, had2 = sb("had256", [P, KD, D]), sb("had512", [P, KF, FF])
    pick = sb("pick", [P, R0])
    causal8, pad8 = sb("causal8", [P, P], U8), sb("pad8", [P, B, P], U8)
    causal, pad = sb("causal", [P, P]), sb("pad", [P, B, P])
    minus = sb("minus", [P, P], BF16)
    wup, wdn = sb("wup", [P, KD, FF], BF16), sb("wdn", [P, KF, D], BF16)
    w_scale = sb("w_scale", [P, 2])
    steps = sb("steps", [P, 2, 2])
    psum = [ctx.enter_context(nc.psum_tensor(f"ps0_{n}", [P, 512], F32)) for n in range(8)]

    wraw = ctx.enter_context(nc.sbuf_tensor("ffn_raw", [P, 2, KD * FF], F32))
    wtmp = ctx.enter_context(nc.sbuf_tensor("ffn_tmp", [P, 2, KD * FF], F32))
    wload, wdone, zero, summed = (nc.alloc_semaphore(n) for n in ("w0_loaded", "w0_done", "wo_zero", "w0_sum"))
    with nc.Block() as block:
        @block.sync
        def _(e):
            e.dma_start(wraw[:, 0, :].rearrange("p (k n) -> p k n", k=KD),
                        a["w_upT"].rearrange("(k p) n -> p k n", p=P)).then_inc(wload, 16)
            e.dma_start(wraw[:, 1, :].rearrange("p (k n) -> p k n", k=KF),
                        a["w_downT"].rearrange("(k p) n -> p k n", p=P)).then_inc(wload, 16)
            e.dma_start(causal8[:, :], a["causal"]).then_inc(wload, 16)
            e.dma_start(pad8[:, :, :], a["padding"].unsqueeze(0).to_broadcast([P, B, P])).then_inc(wload, 16)
            for dst, src in ((ctxT, a["ctxT"]), (wq, a["WqT"]), (wk, a["WkT"]), (wv, a["WvT"]),
                             (had1, a["had256"]), (had2, a["had512"])):
                e.dma_start(dst[:, :, :], src.rearrange("(k p) n -> p k n", p=P)).then_inc(wdone, 16)
            e.dma_start(bq[:, :], a["bq"]).then_inc(wdone, 16)
            e.dma_start(bk[:, :], a["bk"]).then_inc(wdone, 16)
            e.dma_start(pick[:, :], a["pick"]).then_inc(wdone, 16)
            e.dma_start(bv[:, :], a["bv"].unsqueeze(0).to_broadcast([P, G0 * HD0])).then_inc(wdone, 16)
            e.dma_start(bo[:, :], a["bo"].unsqueeze(0).to_broadcast([P, D])).then_inc(wdone, 16)
            e.wait_ge(zero, 1)
            for g in range(G0):
                j, half = g % 4, g // 4
                e.dma_start(wo[GP * j:GP * j + HD0, half, :, :], a["WoT"][g]).then_inc(wdone, 16)
            e.wait_ge(wdone, 16 * 19)

        @block.gpsimd
        def _(e):
            e.memset(wo[:, :, :, :], 0.0).then_inc(zero, 1)

        @block.tensor
        def _(e):
            e.wait_ge(summed, 1)
            e.matmul(psum[0][:, 0:2], t["ones"][:, :], steps[:, 0, :], start=True, stop=True).then_inc(summed, 1)

        @block.vector
        def _(e):
            chain = Chain(nc, "w0_chain", 8)
            chain.start(e, 0)
            e.tensor_scalar(minus[:, :], ident[:, :], MASKED, None, ALU.mult)
            e.wait_ge(wload, 16 * 4)
            chain.link(e.tensor_copy(causal[:, :], causal8[:, :]))
            chain.link(e.tensor_copy(pad[:, :, :], pad8[:, :, :]))
            e.tensor_reduce(steps[:, 0, :], wraw[:, :, :], AX, ALU.add, apply_absolute_value=True).then_inc(summed, 1)
            e.wait_ge(summed, 2)
            chain.link(e.tensor_scalar(w_scale[:, :], psum[0][:, 0:2], 1.0 / (D * FF), EPS, ALU.mult, ALU.max))
            chain.link(e.reciprocal(steps[:, 1, :], w_scale[:, :]))
            for n, out in ((0, wup), (1, wdn)):
                chain.link(e.tensor_scalar(wtmp[:, n, :], wraw[:, n, :], steps[:, 1, n:n + 1], MAGIC, ALU.mult, ALU.add))
            for n, out in ((0, wup), (1, wdn)):
                chain.link(e.tensor_scalar(wraw[:, n, :], wtmp[:, n, :], MAGIC, -1.0, ALU.subtract, ALU.max))
            for n, out in ((0, wup), (1, wdn)):
                e.tensor_scalar(out[:, :, :].rearrange("p k n -> p (k n)"), wraw[:, n, :], 1.0, None, ALU.min)
            chain.end()
            e.drain()

    s = Pieces(nc)
    xt_ps, F0, F1 = psum[0], psum[6], psum[7]
    S = psum[1:4]
    O = psum[4:6]
    stats = sb("stats_p", [P, 6])
    mv = sb("mv_p", [P, 2])
    spare = sb("spare", [P, 1])
    rstd = sb("rstd_p", [P, 1])
    xn = sb("xn", [P, D])
    xnT = sb("xnT", [P, KD, P])
    cT = sb("cT", [P, KD, P])
    qT = sb("qT0", [P, KD, P])
    kb = sb("k_blocks", [P, KD, R0, P])
    vp = sb("v_padded", [P, G0, GP])
    mask = sb("mask", [P, P], BF16)
    nmax = sb("nmax", [P, G0, R0])
    nbias = sb("nbias", [P, G0, R0])
    rowsum = sb("rowsum", [P, G0, R0])
    rinv = sb("rinv", [P, G0, R0])
    prob = sb("prob", [P, 4, R0, P])
    probT = sb("probT", [P, 4, R0 * P])
    oT = sb("oT", [P, 2, R0, P])
    stats_f = sb("stats_f", [P, 6])
    mv_f = sb("mv_f", [P, 2])
    rstd_f = sb("rstd_f", [P, 1])
    yn = sb("yn", [P, D])
    ynT = sb("ynT", [P, KD, P])
    quant = sb("quant", [P, 8])
    rnd1, q1 = sb("rnd1", [P, D]), sb("q1", [P, D], BF16)
    q1T = sb("q1T", [P, KD, P], BF16)
    up, hid = sb("up", [P, FF]), sb("hid", [P, FF])
    hidT = sb("hidT", [P, KF, P])
    rnd2, q2 = sb("rnd2", [P, FF]), sb("q2", [P, FF], BF16)
    q2T = sb("q2T", [P, KF, P], BF16)
    gbo = sb("gbo", [P, D])

    sig = s.flag
    p_stat, p_rstd = sig("p_stat", "vector"), sig("p_rstd", "gpsimd")
    p_ctx = sig("p_ctx", "gpsimd")
    p_xn, p_mask, p_qk = sig("p_xn", "vector"), sig("p_mask", "vector"), sig("p_qk", "vector")
    p_v = sig("p_v", "vector")
    p_xT = sig("p_xT", "scalar")
    pe_xT, pe_qk, pe_v = sig("pe_xT", "tensor"), sig("pe_qk", "tensor"), sig("pe_v", "tensor")
    pe_S, pe_T, pe_O = sig("pe_S", "tensor", G0), sig("pe_T", "tensor", G0), sig("pe_O", "tensor", 2)
    v_max, v_inv = sig("v_max", "vector", G0), sig("v_inv", "vector", G0)
    a_exp, g_norm = sig("a_exp", "scalar", G0), sig("g_norm", "gpsimd", G0)
    v_PT, a_PT = sig("v_PT", "vector", G0 // 2), sig("a_PT", "scalar", G0 // 2)
    a_oT, pe_W, v_x1 = sig("a_oT", "scalar", 2), sig("pe_W", "tensor"), sig("v_x1", "vector")
    f_stat, f_rstd, f_yn = sig("f_stat", "vector"), sig("f_rstd", "gpsimd"), sig("f_yn", "vector")
    pe_yT, a_yT, pe_h1 = sig("pe_yT", "tensor"), sig("a_yT", "scalar"), sig("pe_h1", "tensor")
    v_q1, pe_q1, a_q1 = sig("v_q1", "vector"), sig("pe_q1", "tensor"), sig("a_q1", "scalar")
    pe_up, a_hid, pe_hT = sig("pe_up", "tensor"), sig("a_hid", "scalar"), sig("pe_hT", "tensor")
    a_hT, pe_h2, v_q2 = sig("a_hT", "scalar"), sig("pe_h2", "tensor"), sig("v_q2", "vector")
    pe_q2, a_q2, pe_dn, v_x2 = sig("pe_q2", "tensor"), sig("a_q2", "scalar"), sig("pe_dn", "tensor"), sig("v_x2", "vector")

    c_p1 = Chain(nc, "c_p1", 1)

    @s.piece("P1", "vector")
    def _(e, i):
        c_p1.start(e, i)
        c_p1.link(e.bn_stats(stats[:, :], x[:, i, :]))
        e.memset(spare[:, :], 0.0)
        e.bn_aggr(mv[:, :], stats[:, :]).then_inc(p_stat.sem, 1)
        c_p1.end()

    c_p1g = Chain(nc, "c_p1g", 1)

    @s.piece("P1", "gpsimd")
    def _(e, i):
        c_p1g.start(e, i)
        e.wait_ge(p_stat.sem, p_stat.at(i))
        c_p1g.link(e.tensor_tensor(rstd[:, :], mv[:, 1:2], t["eps"][:, 0:1], ALU.add))
        e.tensor_tensor(rstd[:, :], rstd[:, :], t["half"][:, 0:1], ALU.pow).then_inc(p_rstd.sem, 1)
        e.wait_ge(pe_v.sem, pe_v.at(i - 1))
        e.tensor_copy(cT[:, :, :], ctxT[:, :, bass.ds(i * P, P)]).then_inc(p_ctx.sem, 1)
        c_p1g.end()

    @s.piece("P2", "vector")
    def _(e, i):
        e.wait_ge(p_rstd.sem, p_rstd.at(i))
        e.tensor_scalar(xn[:, :], x[:, i, :], mv[:, 0:1], rstd[:, 0:1], ALU.subtract, ALU.mult).then_inc(p_xn.sem, 1)

    @s.piece("P2", "tensor")
    def _(e, i):
        e.wait_ge(p_xn.sem, p_xn.at(i))
        e.wait_ge(p_v.sem, p_v.at(i - 1))
        for k in range(KD):
            last = e.transpose(xt_ps[:, k * P:(k + 1) * P], xn[:, k * P:(k + 1) * P], ident[:, :])
        last.then_inc(pe_xT.sem, 1)

    @s.piece("P2", "scalar")
    def _(e, i):
        e.wait_ge(pe_xT.sem, pe_xT.at(i))
        e.activation(xnT[:, :, :].rearrange("p k t -> p (k t)"), xt_ps[:, 0:D], ACT.Copy).then_inc(p_xT.sem, 1)

    @s.piece("P3", "tensor")
    def _(e, i):
        e.wait_ge(p_xT.sem, p_xT.at(i))
        e.wait_ge(p_ctx.sem, p_ctx.at(i))
        for n, (w, src) in enumerate(((wq, xnT), (wk, cT))):
            for m in range(KD):
                for k in range(KD):
                    last = e.matmul(xt_ps[:, (2 * n + m) * P:(2 * n + m + 1) * P], w[:, k, m * P:(m + 1) * P],
                                    src[:, k, :], start=(k == 0), stop=(k == KD - 1))
        last.then_inc(pe_qk.sem, 1)

    @s.piece("P3", "vector")
    def _(e, i):
        e.wait_ge(pe_qk.sem, pe_qk.at(i))
        e.wait_ge(pe_S.sem, pe_S.at(i - 1))
        e.tensor_tensor(mask[:, :], causal[:, :], pad[:, i, :], ALU.max).then_inc(p_mask.sem, 1)
        for m in range(KD):
            e.tensor_scalar(qT[:, m, :], xt_ps[:, m * P:(m + 1) * P], bq[:, m:m + 1], None, ALU.add)
        for m in range(KD):
            last = e.scalar_tensor_tensor(kb[:, m, :, :], tiled(xt_ps[:, (2 + m) * P:(3 + m) * P], R0),
                                          bk[:, m:m + 1], spread(pick[:, :], P), ALU.add, ALU.mult)
        last.then_inc(p_qk.sem, 1)

    @s.piece("P4", "tensor")
    def _(e, i):
        e.wait_ge(p_qk.sem, p_qk.at(i))
        for k in range(KD):
            last = e.matmul(xt_ps[:, 0:G0 * HD0], cT[:, k, :], wv[:, k, :], start=(k == 0), stop=(k == KD - 1))
        last.then_inc(pe_v.sem, 1)

    @s.piece("P4", "vector")
    def _(e, i):
        e.wait_ge(pe_v.sem, pe_v.at(i))
        e.wait_ge(pe_O.sem, pe_O.at(i - 1))
        e.tensor_tensor(vp[:, :, 0:HD0], xt_ps[:, 0:G0 * HD0].rearrange("p (g d) -> p g d", g=G0),
                        bv[:, :].rearrange("p (g d) -> p g d", g=G0), ALU.add).then_inc(p_v.sem, 1)

    @s.piece("S", "tensor")
    def _(e, i, g):
        if g == 0:
            e.wait_ge(p_qk.sem, p_qk.at(i))
            e.wait_ge(p_mask.sem, p_mask.at(i))
        j, m = g % 4, g // 4
        bank = S[g % 3]
        e.matmul(bank[:, :], minus[:, :], tiled(mask[:, :], R0), start=True, stop=False)
        e.matmul(bank[:, :], qT[GP * j:GP * j + GP, m, :], kb[GP * j:GP * j + GP, m, :, :],
                 start=False, stop=True).then_inc(pe_S.sem, 1)

    c_s = [Chain(nc, f"c_s{g}", 0) for g in range(0)]

    @s.piece("S", "vector")
    def _(e, i, g):
        e.wait_ge(pe_S.sem, pe_S.at(i, g + 1))
        e.tensor_reduce(nmax[:, g, :], S[g % 3][:, :].rearrange("p (r t) -> p r t", r=R0), AX, ALU.max,
                        negate=True).then_inc(v_max.sem, 1)

    @s.piece("S", "scalar")
    def _(e, i, g):
        e.wait_ge(v_max.sem, v_max.at(i, g + 1))
        for r in range(R0):
            last = e.activation(prob[:, g % 4, r, :], S[g % 3][:, r * P:(r + 1) * P], ACT.Exp,
                                bias=nmax[:, g, r:r + 1], accum_out=rowsum[:, g, r:r + 1])
        last.then_inc(a_exp.sem, 1)

    @s.piece("R", "vector")
    def _(e, i, g):
        e.wait_ge(a_exp.sem, a_exp.at(i, g + 1))
        e.reciprocal(rinv[:, g, :], rowsum[:, g, :]).then_inc(v_inv.sem, 1)

    @s.piece("R", "gpsimd")
    def _(e, i, g):
        e.wait_ge(v_inv.sem, v_inv.at(i, g + 1))
        e.tensor_tensor(prob[:, g % 4, :, :], prob[:, g % 4, :, :], spread(rinv[:, g, :], P),
                        ALU.mult).then_inc(g_norm.sem, 1)

    @s.piece("T", "tensor")
    def _(e, i, g):
        e.wait_ge(g_norm.sem, g_norm.at(i, g + 1))
        for r in range(R0):
            last = e.transpose(S[g % 3][:, r * P:(r + 1) * P], prob[:, g % 4, r, :], ident[:, :])
        last.then_inc(pe_T.sem, 1)

    @s.piece("T", "vector")
    def _(e, i, g):
        if g % 2 == 0:
            e.wait_ge(pe_T.sem, pe_T.at(i, g + 1))
            e.tensor_copy(probT[:, g % 4, :], S[g % 3][:, :]).then_inc(v_PT.sem, 1)

    @s.piece("T", "scalar")
    def _(e, i, g):
        if g % 2 == 1:
            e.wait_ge(pe_T.sem, pe_T.at(i, g + 1))
            e.activation(probT[:, g % 4, :], S[g % 3][:, :], ACT.Copy).then_inc(a_PT.sem, 1)

    @s.piece("V", "tensor")
    def _(e, i, g):
        done = a_PT if g % 2 else v_PT
        e.wait_ge(done.sem, done.at(i, g // 2 + 1))
        if g == 0:
            e.wait_ge(p_v.sem, p_v.at(i))
            e.wait_ge(v_x1.sem, v_x1.at(i - 1))
        if g == 4:
            e.wait_ge(a_oT.sem, a_oT.at(i - 1))
        j = g % 4
        m = e.matmul(O[g // 4][GP * j:GP * j + GP, :], vp[:, g, :], probT[:, g % 4, :], start=True, stop=True,
                     tile_position=(0, GP * j))
        if j == 3:
            m.then_inc(pe_O.sem, 1)

    @s.piece("V", "scalar")
    def _(e, i, g):
        if g % 4 == 3:
            e.wait_ge(pe_O.sem, pe_O.at(i, g // 4 + 1))
            e.wait_ge(pe_W.sem, pe_W.at(i - 1))
            e.activation(oT[:, g // 4, :, :].rearrange("p r t -> p (r t)"), O[g // 4][:, :],
                         ACT.Copy).then_inc(a_oT.sem, 1)

    @s.piece("W", "tensor")
    def _(e, i):
        e.wait_ge(a_oT.sem, a_oT.at(i))
        for half in range(2):
            for r in range(R0):
                last = e.matmul(O[0][:, 0:D], oT[:, half, r, :], wo[:, half, r, :],
                                start=(half == 0 and r == 0), stop=(half == 1 and r == R0 - 1))
        last.then_inc(pe_W.sem, 1)

    c_w = Chain(nc, "c_w", 1)

    @s.piece("W", "vector")
    def _(e, i):
        c_w.start(e, i)
        e.wait_ge(pe_W.sem, pe_W.at(i))
        c_w.link(e.scalar_tensor_tensor(x[:, i, :], O[0][:, 0:D], gates[:, 0:1], x[:, i, :], ALU.mult, ALU.add))
        e.tensor_tensor(x[:, i, :], x[:, i, :], gbo[:, :], ALU.add).then_inc(v_x1.sem, 1)
        c_w.end()

    c_f1 = Chain(nc, "c_f1", 1)

    @s.piece("F1", "vector")
    def _(e, i):
        c_f1.start(e, i)
        e.wait_ge(v_x1.sem, v_x1.at(i))
        c_f1.link(e.bn_stats(stats_f[:, :], x[:, i, :]))
        e.memset(spare[:, :], 0.0)
        e.bn_aggr(mv_f[:, :], stats_f[:, :]).then_inc(f_stat.sem, 1)
        c_f1.end()

    c_f1g = Chain(nc, "c_f1g", 1)

    @s.piece("F1", "gpsimd")
    def _(e, i):
        c_f1g.start(e, i)
        e.wait_ge(f_stat.sem, f_stat.at(i))
        c_f1g.link(e.tensor_tensor(rstd_f[:, :], mv_f[:, 1:2], t["eps"][:, 0:1], ALU.add))
        e.tensor_tensor(rstd_f[:, :], rstd_f[:, :], t["half"][:, 0:1], ALU.pow).then_inc(f_rstd.sem, 1)
        c_f1g.end()

    @s.piece("F2", "vector")
    def _(e, i):
        e.wait_ge(f_rstd.sem, f_rstd.at(i))
        e.tensor_scalar(yn[:, :], x[:, i, :], mv_f[:, 0:1], rstd_f[:, 0:1], ALU.subtract,
                        ALU.mult).then_inc(f_yn.sem, 1)

    @s.piece("F2", "tensor")
    def _(e, i):
        e.wait_ge(f_yn.sem, f_yn.at(i))
        for k in range(KD):
            last = e.transpose(F0[:, k * P:(k + 1) * P], yn[:, k * P:(k + 1) * P], ident[:, :])
        last.then_inc(pe_yT.sem, 1)

    @s.piece("F2", "scalar")
    def _(e, i):
        e.wait_ge(pe_yT.sem, pe_yT.at(i))
        e.activation(ynT[:, :, :].rearrange("p k t -> p (k t)"), F0[:, 0:D], ACT.Copy).then_inc(a_yT.sem, 1)

    @s.piece("F3", "tensor")
    def _(e, i):
        e.wait_ge(a_yT.sem, a_yT.at(i))
        e.wait_ge(v_x2.sem, v_x2.at(i - 1))
        for k in range(KD):
            last = e.matmul(F1[:, 0:D], ynT[:, k, :], had1[:, k, :], start=(k == 0), stop=(k == KD - 1))
        last.then_inc(pe_h1.sem, 1)

    def quantise(e, chain, src, width, norm, c, rnd, out, done):
        chain.link(e.tensor_reduce(quant[:, c:c + 1], src, AX, ALU.max, apply_absolute_value=True))
        if c == 4:
            chain.link(e.tensor_tensor(quant[:, c:c + 1], quant[:, c:c + 1], quant[:, 7:8], ALU.mult))
            chain.link(e.tensor_scalar(quant[:, c:c + 1], quant[:, c:c + 1], norm, EPS, ALU.mult, ALU.max))
        else:
            chain.link(e.tensor_scalar(quant[:, c:c + 1], quant[:, c:c + 1], norm, EPS, ALU.mult, ALU.max))
        chain.link(e.reciprocal(quant[:, c + 1:c + 2], quant[:, c:c + 1]))
        if c == 4:
            chain.link(e.tensor_scalar(quant[:, c + 2:c + 3], quant[:, c + 1:c + 2], quant[:, 7:8], 127.0 * norm,
                                       ALU.mult, ALU.mult))
        else:
            chain.link(e.tensor_scalar(quant[:, c + 2:c + 3], quant[:, c + 1:c + 2], 127.0 * norm, None, ALU.mult))
        chain.link(e.tensor_scalar(rnd, src, quant[:, c + 2:c + 3], MAGIC, ALU.mult, ALU.add))
        e.tensor_scalar(out, rnd, MAGIC, None, ALU.subtract).then_inc(done.sem, 1)

    c_f3 = Chain(nc, "c_f3", 5)

    @s.piece("F3", "vector")
    def _(e, i):
        c_f3.start(e, i)
        e.wait_ge(pe_h1.sem, pe_h1.at(i))
        quantise(e, c_f3, F1[:, 0:D], D, D**-0.5, 0, rnd1[:, :], q1[:, :], v_q1)
        c_f3.end()

    @s.piece("F4", "tensor")
    def _(e, i):
        e.wait_ge(v_q1.sem, v_q1.at(i))
        for k in range(KD):
            last = e.transpose(F0[:, k * 64:(k + 1) * 64].bitcast(BF16), q1[:, k * P:(k + 1) * P], ident_b[:, :])
        last.then_inc(pe_q1.sem, 1)
        e.wait_ge(a_q1.sem, a_q1.at(i))
        for k in range(KD):
            last = e.matmul(F1[:, :], q1T[:, k, :], wup[:, k, :], start=(k == 0), stop=(k == KD - 1))
        last.then_inc(pe_up.sem, 1)

    c_f4 = Chain(nc, "c_f4", 1)

    @s.piece("F4", "scalar")
    def _(e, i):
        c_f4.start(e, i)
        e.wait_ge(pe_q1.sem, pe_q1.at(i))
        e.activation(q1T[:, :, :].rearrange("p k t -> p (k t)"), F0[:, 0:P].bitcast(BF16), ACT.Copy).then_inc(a_q1.sem, 1)
        e.wait_ge(pe_up.sem, pe_up.at(i))
        c_f4.link(e.activation(up[:, :], F1[:, :], ACT.Relu))
        e.activation(hid[:, :], up[:, :], ACT.Square).then_inc(a_hid.sem, 1)
        c_f4.end()

    c_f4v = Chain(nc, "c_f4v", 2)

    @s.piece("F4", "vector")
    def _(e, i):
        c_f4v.start(e, i)
        c_f4v.link(e.tensor_scalar(quant[:, 3:4], quant[:, 0:1], w_scale[:, 0:1], 1.0 / 127.0, ALU.mult, ALU.mult))
        c_f4v.link(e.tensor_tensor(quant[:, 7:8], quant[:, 3:4], quant[:, 3:4], ALU.mult))
        c_f4v.end()

    @s.piece("F5", "tensor")
    def _(e, i):
        e.wait_ge(a_hid.sem, a_hid.at(i))
        for k in range(KF):
            last = e.transpose(F0[:, k * P:(k + 1) * P], hid[:, k * P:(k + 1) * P], ident[:, :])
        last.then_inc(pe_hT.sem, 1)

    @s.piece("F5", "scalar")
    def _(e, i):
        e.wait_ge(pe_hT.sem, pe_hT.at(i))
        e.activation(hidT[:, :, :].rearrange("p k t -> p (k t)"), F0[:, :], ACT.Copy).then_inc(a_hT.sem, 1)

    @s.piece("F6", "tensor")
    def _(e, i):
        e.wait_ge(a_hT.sem, a_hT.at(i))
        for k in range(KF):
            last = e.matmul(F1[:, :], hidT[:, k, :], had2[:, k, :], start=(k == 0), stop=(k == KF - 1))
        last.then_inc(pe_h2.sem, 1)

    c_f6 = Chain(nc, "c_f6", 6)

    @s.piece("F6", "vector")
    def _(e, i):
        c_f6.start(e, i)
        e.wait_ge(pe_h2.sem, pe_h2.at(i))
        quantise(e, c_f6, F1[:, :], FF, FF**-0.5, 4, rnd2[:, :], q2[:, :], v_q2)
        c_f6.end()

    @s.piece("F7", "tensor")
    def _(e, i):
        e.wait_ge(v_q2.sem, v_q2.at(i))
        for k in range(KF):
            last = e.transpose(F0[:, k * 64:(k + 1) * 64].bitcast(BF16), q2[:, k * P:(k + 1) * P], ident_b[:, :])
        last.then_inc(pe_q2.sem, 1)
        e.wait_ge(a_q2.sem, a_q2.at(i))
        for k in range(KF):
            last = e.matmul(F1[:, 0:D], q2T[:, k, :], wdn[:, k, :], start=(k == 0), stop=(k == KF - 1))
        last.then_inc(pe_dn.sem, 1)

    @s.piece("F7", "scalar")
    def _(e, i):
        e.wait_ge(pe_q2.sem, pe_q2.at(i))
        e.activation(q2T[:, :, :].rearrange("p k t -> p (k t)"), F0[:, 0:2 * P].bitcast(BF16),
                     ACT.Copy).then_inc(a_q2.sem, 1)

    c_f7 = Chain(nc, "c_f7", 2)

    @s.piece("F7", "vector")
    def _(e, i):
        c_f7.start(e, i)
        c_f7.link(e.tensor_scalar(quant[:, 3:4], quant[:, 4:5], w_scale[:, 1:2], 1.0 / 127.0, ALU.mult, ALU.mult))
        c_f7.link(e.tensor_tensor(quant[:, 3:4], quant[:, 3:4], gates[:, 2:3], ALU.mult))
        e.wait_ge(pe_dn.sem, pe_dn.at(i))
        e.scalar_tensor_tensor(x[:, i, :], F1[:, 0:D], quant[:, 3:4], x[:, i, :], ALU.mult,
                               ALU.add).then_inc(v_x2.sem, 1)
        c_f7.end()

    def body(i, project=True, feed=True):
        p = {3: ["P1"], 4: ["P2"], 6: ["P3"], 7: ["P4"]} if project else {}
        f = {0: ["F2"], 1: ["F3"], 2: ["F4"], 4: ["F5"], 5: ["F6"], 7: ["F7"]} if feed else {}
        steps = [("F1", i - 1)] if feed else []
        steps += [("S", i, 0), ("S", i, 1), ("R", i, 0)]
        for g in range(G0):
            steps.append(("T", i, g))
            steps += [(n, i - 1) for n in f.get(g, [])]
            if g >= 1:
                steps.append(("V", i, g - 1))
            if g + 2 < G0:
                steps.append(("S", i, g + 2))
            steps += [(n, i + 1) for n in p.get(g, []) if n != "P4"]
            if g + 1 < G0:
                steps.append(("R", i, g + 1))
        steps.append(("V", i, G0 - 1))
        steps += [(n, i + 1) for n in p.get(7, [])]
        steps.append(("W", i))
        return steps

    with nc.Block() as block:
        @block.vector
        def _(e):
            e.memset(vp[:, :, :], 0.0)
            e.tensor_scalar(gbo[:, :], bo[:, :], gates[:, 0:1], None, ALU.mult)
            e.drain()

    before = [(n, 0) for n in ("P1", "P2", "P3", "P4")] + body(0, feed=False)
    after = body(B - 1, project=False) + [(n, B - 1) for n in ("F1", "F2", "F3", "F4", "F5", "F6", "F7")]
    with nc.Block() as block:
        s.run(block, before, body, after, (1, B - 1))



G1, HD1 = 8, 128
J = 4
W1 = 8 * D
Q_, QX_, K_, KX_, V_, VX_ = 0, 512, 1024, 1280, 1536, 1792
CTX_UP = 64.0
F8_MAX = 448.0
F8_TINY = 2.0**-6
F8_SHIFT = 1.5 * 2.0**20
EXPONENT = 0x7F80


def split(e, hi, lo, src):
    yield e.tensor_copy(hi, src)
    yield e.tensor_tensor(lo, src, hi, ALU.subtract)


def layer1_attention(nc, a, t, ctx):
    def sb(name, shape, dt=F32):
        return ctx.enter_context(nc.sbuf_tensor(name, shape, dt))

    x, gates, ident = t["x"], t["gates"], t["ident"]
    bank = [ctx.enter_context(nc.psum_tensor(f"ps1_{n}", [P, 512], F32)) for n in range(8)]
    wb = sb("w_proj_in", [P, KD, 2, J * W1], F16)
    wp = sb("w_proj_out", [P, 2, 32, D], F16)
    xq = sb("xq", [P, KD, 4, B * P], BF16)
    cx = sb("ctx_parts", [P, KD, 2, B * P], F16)
    insc = sb("in_scales", [P, KD, 4])
    inv_insc = sb("inv_in_scales", [P, KD, 4])
    lnw, lnb = sb("ln_w", [P, KD]), sb("ln_b", [P, KD])
    wsc = sb("w_scales", [P, 5])
    psc = sb("proj_in_scale", [P, 1])
    hln = sb("head_ln", [P, 8])
    smooth, inv_smooth = sb("smooth", [P, 32]), sb("inv_smooth", [P, 32])
    var_fac, out_fac = sb("var_fac", [P, 12]), sb("out_fac", [P, 12])
    out_gate = sb("out_gate", [P, 1])

    items = []
    for k in range(KD):
        items += [("wqT", k, Q_, 512, 0, True), ("wqxT", k, QX_, 512, 1, True), ("wkT", k, K_, 256, 2, True),
                  ("wvT", k, V_, 256, 3, False), ("wkxT", k, KX_, 256, None, True),
                  ("wvxT", k, VX_, 256, None, False)]
    nproj = 4
    with nc.sbuf_tensor("raw1", [P, 2, 2048], F32) as raw, nc.sbuf_tensor("work1", [P, 2048], F32) as work, \
            nc.sbuf_tensor("head_sum", [P, 16], F32) as head_sum:
        small, got, used = (nc.alloc_semaphore(n) for n in ("w1_small", "w1_got", "w1_used"))
        with nc.Block() as block:
            @block.scalar
            def _(e):
                e.dma_start(insc[:, :, :], a["in_scales"].rearrange("(k p) n -> p k n", p=P)).then_inc(small, 16)
                e.dma_start(lnw[:, :], a["ln_w"]).then_inc(small, 16)
                e.dma_start(lnb[:, :], a["ln_b"]).then_inc(small, 16)
                e.dma_start(wsc[:, :], a["w_scales"].unsqueeze(0).to_broadcast([P, 5])).then_inc(small, 16)
                e.dma_start(psc[:, :], a["proj_in_scale"].unsqueeze(0).to_broadcast([P, 1])).then_inc(small, 16)
                e.dma_start(hln[:, :], a["head_ln"]).then_inc(small, 16)
                e.dma_start(smooth[:, :], a["smooth"]).then_inc(small, 16)

            @block.sync
            def _(e):
                n = 0
                for name, k, _, w, _, _ in items:
                    if n >= 2:
                        e.wait_ge(used, n - 1)
                    e.dma_start(raw[:, n % 2, 0:J * w], a[name].rearrange("(k p) n -> p k n", p=P)[:, k, :]).then_inc(got, 16)
                    n += 1
                    e.wait_ge(got, 16 * n)
                for q in range(nproj):
                    e.wait_ge(used, n - 1)
                    e.dma_start(raw[:, n % 2, :].rearrange("p (h o) -> p h o", h=8),
                                a["wprojT"].rearrange("(h p) o -> p h o", p=P)[:, 8 * q:8 * q + 8, :]).then_inc(got, 16)
                    n += 1
                    e.wait_ge(got, 16 * n)
                for k in range(KD):
                    e.wait_ge(used, n - 1)
                    e.dma_start(raw[:, n % 2, :], a["ctxT"].rearrange("(k p) n -> p k n", p=P)[:, k, :]).then_inc(got, 16)
                    n += 1
                    e.wait_ge(got, 16 * n)

            @block.vector
            def _(e):
                count = sum(5 if c else 2 for *_, c in items) + nproj + KD + 10
                chain = Chain(nc, "w1_chain", count)
                chain.start(e, 0)
                e.wait_ge(small, 16 * 7)
                chain.link(e.reciprocal(inv_insc[:, :, :], insc[:, :, :]))
                chain.link(e.reciprocal(inv_smooth[:, :], smooth[:, :]))
                chain.link(e.tensor_scalar(hln[:, 4:8], hln[:, 4:8], HD1**-0.5, None, ALU.mult))
                chain.link(e.tensor_copy(out_fac[:, 0:4], spread(wsc[:, 0:1], 4)))
                chain.link(e.tensor_copy(out_fac[:, 4:8], spread(wsc[:, 1:2], 4)))
                chain.link(e.tensor_copy(out_fac[:, 8:10], spread(wsc[:, 2:3], 2)))
                chain.link(e.memset(out_fac[:, 10:12], 1.0 / CTX_UP))
                chain.link(e.scalar_tensor_tensor(var_fac[:, :], out_fac[:, :], 1.0 / HD1, out_fac[:, :], ALU.mult, ALU.mult))
                chain.link(e.tensor_tensor(out_gate[:, :], psc[:, :], wsc[:, 4:5], ALU.mult))
                chain.link(e.tensor_tensor(out_gate[:, :], out_gate[:, :], gates[:, 1:2], ALU.mult))
                n = 0
                for name, k, c0, w, sc, centred in items:
                    e.wait_ge(got, 16 * (n + 1))
                    if n:
                        e.wait_ge(used, n)
                    src = raw[:, n % 2, 0:J * w]
                    dst = work[:, 0:J * w]
                    chain.link(e.tensor_scalar(dst, src, CTX_UP if sc is None else insc[:, k, sc:sc + 1], None, ALU.mult))
                    if centred:
                        heads = J * w // HD1
                        byhead = dst.rearrange("p (h d) -> p h d", h=heads)
                        chain.link(e.tensor_reduce(head_sum[:, 0:heads], byhead, AX, ALU.add))
                        chain.link(e.tensor_scalar(head_sum[:, 0:heads], head_sum[:, 0:heads], 1.0 / HD1, None, ALU.mult))
                        chain.link(e.tensor_tensor(byhead, byhead, spread(head_sum[:, 0:heads], HD1), ALU.subtract))
                    parts = [wb[:, k, hl, :].rearrange("p (j c) -> p j c", j=J)[:, :, c0:c0 + w] for hl in range(2)]
                    high, low = split(e, parts[0], parts[1], dst.rearrange("p (j c) -> p j c", j=J)), None
                    chain.link(next(high))
                    next(high).then_inc(used, 1)
                    n += 1
                for q in range(nproj):
                    e.wait_ge(got, 16 * (n + 1))
                    parts = split(e, *(wp[:, hl, 8 * q:8 * q + 8, :].rearrange("p h o -> p (h o)") for hl in range(2)),
                                  raw[:, n % 2, :])
                    chain.link(next(parts))
                    next(parts).then_inc(used, 1)
                    n += 1
                for k in range(KD):
                    e.wait_ge(got, 16 * (n + 1))
                    parts = split(e, cx[:, k, 0, :], cx[:, k, 1, :], raw[:, n % 2, :])
                    chain.link(next(parts))
                    next(parts).then_inc(used, 1)
                    n += 1
                chain.end()
                e.drain()

    r = Pieces(nc)
    stats, mv, rstd, spare = sb("stats_r", [P, 2, 6]), sb("mv_r", [P, 2, 2]), sb("rstd_r", [P, 2]), sb("spare_r", [P, 1])
    rows, u = sb("rows_n", [P, 2, D]), sb("rows_ln", [P, KD, P])
    wide = sb("wide_r", [P, 8, P])
    yb, ye = sb("yb", [P, 8, P], BF16), sb("ye", [P, 8, P], BF16)
    r_stat, r_rstd, r_n = r.flag("r_stat", "vector"), r.flag("r_rstd", "gpsimd"), r.flag("r_n", "vector")
    r_T, r_u, r_q = r.flag("r_T", "tensor"), r.flag("r_u", "scalar"), r.flag("r_q", "vector")
    c_r1, c_r1g = Chain(nc, "c_r1", 1), Chain(nc, "c_r1g", 2)
    c_r3 = Chain(nc, "c_r3", 5)

    def float8(e, chain, y32, b16, e16, dst):
        chain.link(e.tensor_scalar(b16, y32, F8_MAX, -F8_MAX, ALU.min, ALU.max))
        chain.link(e.tensor_scalar(e16.bitcast(U16), b16.bitcast(U16), EXPONENT, None, ALU.bitwise_and))
        chain.link(e.tensor_scalar(e16, e16, F8_TINY, F8_SHIFT, ALU.max, ALU.mult))
        chain.link(e.tensor_tensor(y32, b16, e16, ALU.add))
        return e.tensor_tensor(dst, y32, e16, ALU.subtract)

    @r.piece("1", "vector")
    def _(e, i, b):
        c_r1.start(e, i)
        c_r1.link(e.bn_stats(stats[:, b, :], x[:, i, :]))
        e.memset(spare[:, :], 0.0)
        e.bn_aggr(mv[:, b, :], stats[:, b, :]).then_inc(r_stat.sem, 1)
        c_r1.end()

    @r.piece("1", "gpsimd")
    def _(e, i, b):
        c_r1g.start(e, i)
        e.wait_ge(r_stat.sem, r_stat.at(i))
        c_r1g.link(e.tensor_tensor(rstd[:, b:b + 1], mv[:, b, 1:2], t["one_eps"][:, 0:1], ALU.mult))
        c_r1g.link(e.tensor_tensor(rstd[:, b:b + 1], rstd[:, b:b + 1], t["eps_eps"][:, 0:1], ALU.add))
        e.tensor_tensor(rstd[:, b:b + 1], rstd[:, b:b + 1], t["half"][:, 0:1], ALU.pow).then_inc(r_rstd.sem, 1)
        c_r1g.end()

    @r.piece("2", "vector")
    def _(e, i, b):
        e.wait_ge(r_rstd.sem, r_rstd.at(i))
        e.wait_ge(r_T.sem, r_T.at(i - 1))
        e.tensor_scalar(rows[:, b, :], x[:, i, :], mv[:, b, 0:1], rstd[:, b:b + 1], ALU.subtract,
                        ALU.mult).then_inc(r_n.sem, 1)

    @r.piece("2", "tensor")
    def _(e, i, b):
        e.wait_ge(r_n.sem, r_n.at(i))
        e.wait_ge(r_u.sem, r_u.at(i - 1))
        for k in range(KD):
            last = e.transpose(bank[0][:, k * P:(k + 1) * P], rows[:, b, k * P:(k + 1) * P], ident[:, :])
        last.then_inc(r_T.sem, 1)

    @r.piece("2", "scalar")
    def _(e, i, b):
        e.wait_ge(r_T.sem, r_T.at(i))
        e.wait_ge(r_q.sem, r_q.at(i - 1))
        for k in range(KD):
            last = e.activation(u[:, k, :], bank[0][:, k * P:(k + 1) * P], ACT.Identity, bias=lnb[:, k:k + 1],
                                scale=lnw[:, k:k + 1])
        last.then_inc(r_u.sem, 1)

    @r.piece("3", "vector")
    def _(e, i, b):
        c_r3.start(e, i)
        e.wait_ge(r_u.sem, r_u.at(i))
        for k in range(KD):
            m = e.tensor_tensor(wide[:, 4 * k:4 * k + 4, :], tiled(u[:, k, :], 4), spread(inv_insc[:, k, :], P), ALU.mult)
            if k == KD - 1:
                c_r3.link(m)
        float8(e, c_r3, wide[:, :, :], yb[:, :, :], ye[:, :, :],
               xq[:, :, :, bass.ds(i * P, P)].rearrange("p k s t -> p (k s) t")).then_inc(r_q.sem, 1)
        c_r3.end()

    with nc.Block() as block:
        two = lambda n: [("1", 2 * n, 0), ("1", 2 * n + 1, 1), ("2", 2 * n, 0), ("3", 2 * n, 0),
                         ("2", 2 * n + 1, 1), ("3", 2 * n + 1, 1)]
        r.run(block, [], two, [], (0, B // 2))

    s = Pieces(nc)
    A, S, O = bank[0:4], bank[4:6], bank[6:8]
    hstat = sb("hstat", [P, 12, 6])
    hsq, hsum = sb("hsq", [P, 12, 2]), sb("hsum", [P, 12, 2])
    hr = sb("hr", [P, 12])
    hn = sb("heads_n", [P, 3, 4, HD1])
    hT = sb("headsT", [P, 3, 4, P])
    v = sb("v1", [P, 2, 2, HD1])
    nmax, rowsum, rinv = sb("nmax1", [P, 2, 4]), sb("rowsum1", [P, 2, 4]), sb("rinv1", [P, 2, 4])
    prob, probT = sb("prob1", [P, 2, 4, P]), sb("probT1", [P, 2, 4, P])
    wide2, cb, ce = sb("wide2", [P, 8, P]), sb("cb", [P, 8, P], BF16), sb("ce", [P, 8, P], BF16)
    catq = sb("catq", [P, 8, P], BF16)
    sig = s.flag
    pe_A, v_ss, g_r = sig("pe_A", "tensor", 4), sig("v_ss", "vector"), sig("g_r", "gpsimd")
    v_n, pe_hT = sig("v_n", "vector", 3), sig("pe_headsT", "tensor", 3)
    a_hT, v_hT, a_v = sig("a_headsT", "scalar", 2), sig("v_headsT", "vector"), sig("a_v", "scalar")
    pe_S, v_mx, a_ex = sig("pe_S1", "tensor", 2), sig("v_mx1", "vector", 2), sig("a_ex1", "scalar", 2)
    v_iv, g_p = sig("v_iv1", "vector", 2), sig("g_p1", "gpsimd", 2)
    pe_PT, a_PT, v_PT = sig("pe_PT1", "tensor", 2), sig("a_PT1", "scalar"), sig("v_PT1", "vector")
    pe_O, v_q, pe_out, v_x = sig("pe_O1", "tensor", 2), sig("v_catq", "vector"), sig("pe_out", "tensor"), sig("v_x3", "vector")

    @s.piece("A", "tensor")
    def _(e, i):
        rows_at, w_at = bass.ds((i // J) * P, P), (i % J) * W1

        def project(out, which, c0, n):
            for k in range(KD):
                for hl in range(2):
                    last = e.matmul(out, xq[:, k, which, rows_at], wb[:, k, hl, bass.ds(w_at + c0, n)],
                                    start=(k == 0 and hl == 0), stop=(k == KD - 1 and hl == 1))
            return last

        def project_context(out, c0, n):
            for k in range(KD):
                for part, hl in ((0, 0), (0, 1), (1, 0)):
                    last = e.matmul(out, cx[:, k, part, rows_at], wb[:, k, hl, bass.ds(w_at + c0, n)],
                                    start=(k == 0 and part == hl == 0), stop=(k == KD - 1 and part == 1))
            return last

        project(A[0][:, :], 0, Q_, 512).then_inc(pe_A.sem, 1)
        project(A[1][:, :], 1, QX_, 512).then_inc(pe_A.sem, 1)
        project(A[2][:, 0:256], 2, K_, 256)
        project_context(A[2][:, 256:512], KX_, 256).then_inc(pe_A.sem, 1)
        e.wait_ge(a_v.sem, a_v.at(i - 1))
        project(A[3][:, 0:256], 3, V_, 256)
        project_context(A[3][:, 256:512], VX_, 256).then_inc(pe_A.sem, 1)

    c_st, c_stg = Chain(nc, "c_st", 5), Chain(nc, "c_stg", 1)

    @s.piece("ST", "vector")
    def _(e, i):
        c_st.start(e, i)
        for n in range(3):
            e.wait_ge(pe_A.sem, pe_A.at(i, n + 1))
            for h in range(4):
                last = e.bn_stats(hstat[:, 4 * n + h, :], A[n][:, h * HD1:(h + 1) * HD1])
        c_st.link(last)
        c_st.link(e.tensor_tensor(hsq[:, :, :], hstat[:, :, 1:5:3], hstat[:, :, 1:5:3], ALU.mult))
        c_st.link(e.scalar_tensor_tensor(hsum[:, :, :], hsq[:, :, :], HD1 / 2.0, hstat[:, :, 2:6:3], ALU.mult, ALU.add))
        c_st.link(e.tensor_tensor(hr[:, :], hsum[:, :, 0], hsum[:, :, 1], ALU.add))
        c_st.link(e.tensor_tensor(hr[:, :], hr[:, :], var_fac[:, :], ALU.mult))
        e.tensor_scalar(hr[:, :], hr[:, :], EPS, None, ALU.add).then_inc(v_ss.sem, 1)
        c_st.end()

    @s.piece("ST", "gpsimd")
    def _(e, i):
        c_stg.start(e, i)
        e.wait_ge(v_ss.sem, v_ss.at(i))
        c_stg.link(e.tensor_tensor(hr[:, :], hr[:, :], t["half"][:, 0:12], ALU.pow))
        e.tensor_tensor(hr[:, :], hr[:, :], out_fac[:, :], ALU.mult).then_inc(g_r.sem, 1)
        c_stg.end()

    @s.piece("N", "vector")
    def _(e, i):
        e.wait_ge(g_r.sem, g_r.at(i))
        for n in range(3):
            e.tensor_tensor(hn[:, n, :, :], A[n][:, :].rearrange("p (h d) -> p h d", h=4),
                            spread(hr[:, 4 * n:4 * n + 4], HD1), ALU.mult).then_inc(v_n.sem, 1)

    @s.piece("TQ", "tensor")
    def _(e, i):
        for n in range(3):
            e.wait_ge(v_n.sem, v_n.at(i, n + 1))
            for h in range(4):
                last = e.transpose(A[n][:, h * P:(h + 1) * P], hn[:, n, h, :], ident[:, :])
            last.then_inc(pe_hT.sem, 1)

    @s.piece("TQ", "scalar")
    def _(e, i):
        for n, parts in ((0, ((0, 4, 0),)), (2, ((0, 2, 4), (2, 4, 6)))):
            e.wait_ge(pe_hT.sem, pe_hT.at(i, n + 1))
            for h0, h1, c in parts:
                last = e.activation(hT[:, n, h0:h1, :].rearrange("p h t -> p (h t)"), A[n][:, h0 * P:h1 * P],
                                    ACT.Identity, bias=hln[:, c + 1:c + 2], scale=hln[:, c:c + 1])
            last.then_inc(a_hT.sem, 1)

    @s.piece("TQ", "vector")
    def _(e, i):
        e.wait_ge(pe_hT.sem, pe_hT.at(i, 2))
        e.tensor_scalar(hT[:, 1, :, :].rearrange("p h t -> p (h t)"), A[1][:, :], hln[:, 2:3], hln[:, 3:4],
                        ALU.mult, ALU.add).then_inc(v_hT.sem, 1)

    @s.piece("VE", "scalar")
    def _(e, i):
        e.wait_ge(pe_A.sem, pe_A.at(i))
        e.wait_ge(pe_O.sem, pe_O.at(i - 1))
        e.activation(v[:, 0, :, :].rearrange("p h d -> p (h d)"), A[3][:, 0:256], ACT.Copy, scale=wsc[:, 3:4])
        e.activation(v[:, 1, :, :].rearrange("p h d -> p (h d)"), A[3][:, 256:512], ACT.Copy,
                     scale=1.0 / CTX_UP).then_inc(a_v.sem, 1)

    @s.piece("SC", "tensor")
    def _(e, i):
        e.wait_ge(a_hT.sem, a_hT.at(i))
        e.wait_ge(v_hT.sem, v_hT.at(i))
        for kind in range(2):
            for h in range(4):
                last = e.matmul(S[kind][:, h * P:(h + 1) * P], hT[:, kind, h, :], hT[:, 2, 2 * kind + h // 2, :],
                                start=True, stop=True)
            last.then_inc(pe_S.sem, 1)

    @s.piece("SC", "vector")
    def _(e, i):
        for kind in range(2):
            e.wait_ge(pe_S.sem, pe_S.at(i, kind + 1))
            e.tensor_reduce(nmax[:, kind, :], S[kind][:, :].rearrange("p (h t) -> p h t", h=4), AX, ALU.max,
                            negate=True).then_inc(v_mx.sem, 1)

    @s.piece("SC", "scalar")
    def _(e, i):
        for kind in range(2):
            e.wait_ge(v_mx.sem, v_mx.at(i, kind + 1))
            for h in range(4):
                last = e.activation(prob[:, kind, h, :], S[kind][:, h * P:(h + 1) * P], ACT.Exp,
                                    bias=nmax[:, kind, h:h + 1], accum_out=rowsum[:, kind, h:h + 1])
            last.then_inc(a_ex.sem, 1)

    @s.piece("R", "vector")
    def _(e, i):
        for kind in range(2):
            e.wait_ge(a_ex.sem, a_ex.at(i, kind + 1))
            e.reciprocal(rinv[:, kind, :], rowsum[:, kind, :]).then_inc(v_iv.sem, 1)

    @s.piece("R", "gpsimd")
    def _(e, i):
        for kind in range(2):
            e.wait_ge(v_iv.sem, v_iv.at(i, kind + 1))
            e.tensor_tensor(prob[:, kind, :, :], prob[:, kind, :, :], spread(rinv[:, kind, :], P),
                            ALU.mult).then_inc(g_p.sem, 1)

    @s.piece("PT", "tensor")
    def _(e, i):
        for kind in range(2):
            e.wait_ge(g_p.sem, g_p.at(i, kind + 1))
            for h in range(4):
                last = e.transpose(S[kind][:, h * P:(h + 1) * P], prob[:, kind, h, :], ident[:, :])
            last.then_inc(pe_PT.sem, 1)

    @s.piece("PT", "scalar")
    def _(e, i):
        e.wait_ge(pe_PT.sem, pe_PT.at(i, 1))
        e.activation(probT[:, 0, :, :].rearrange("p h t -> p (h t)"), S[0][:, :], ACT.Copy).then_inc(a_PT.sem, 1)

    @s.piece("PT", "vector")
    def _(e, i):
        e.wait_ge(pe_PT.sem, pe_PT.at(i, 2))
        e.tensor_copy(probT[:, 1, :, :].rearrange("p h t -> p (h t)"), S[1][:, :]).then_inc(v_PT.sem, 1)

    @s.piece("PV", "tensor")
    def _(e, i):
        e.wait_ge(a_v.sem, a_v.at(i))
        e.wait_ge(v_x.sem, v_x.at(i - 1))
        for kind, done in ((0, a_PT), (1, v_PT)):
            e.wait_ge(done.sem, done.at(i))
            for g in range(2):
                last = e.matmul(O[kind][:, g * 2 * P:(g + 1) * 2 * P], v[:, kind, g, :],
                                probT[:, kind, 2 * g:2 * g + 2, :], start=True, stop=True)
            last.then_inc(pe_O.sem, 1)

    c_q = Chain(nc, "c_q", 5)

    @s.piece("Q", "vector")
    def _(e, i):
        c_q.start(e, i)
        for kind in range(2):
            e.wait_ge(pe_O.sem, pe_O.at(i, kind + 1))
            m = e.tensor_tensor(wide2[:, 4 * kind:4 * kind + 4, :], O[kind][:, :].rearrange("p (h t) -> p h t", h=4),
                                spread(inv_smooth[:, bass.ds((i % J) * 4 + 16 * kind, 4)], P), ALU.mult)
        c_q.link(m)
        float8(e, c_q, wide2[:, :, :], cb[:, :, :], ce[:, :, :], catq[:, :, :]).then_inc(v_q.sem, 1)
        c_q.end()

    @s.piece("O", "tensor")
    def _(e, i):
        e.wait_ge(v_q.sem, v_q.at(i))
        n = 0
        for kind in range(2):
            for h in range(4):
                for hl in range(2):
                    w = wp[:, hl, bass.ds((i % J) * 4 + 16 * kind + h, 1), :].rearrange("p h o -> p (h o)")
                    last = e.matmul(O[0][:, 0:D], catq[:, 4 * kind + h, :], w, start=(n == 0), stop=(n == 15))
                    n += 1
        last.then_inc(pe_out.sem, 1)

    @s.piece("O", "vector")
    def _(e, i):
        e.wait_ge(pe_out.sem, pe_out.at(i))
        row = x[:, bass.ds(i // J, 1), :].rearrange("p b d -> p (b d)")
        e.scalar_tensor_tensor(row, O[0][:, 0:D], out_gate[:, 0:1], row, ALU.mult, ALU.add).then_inc(v_x.sem, 1)

    def body(i, nxt=True, last=True):
        steps = [("SC", i)]
        steps += [("A", i + 1)] if nxt else []
        steps += [("O", i - 1)] if last else []
        steps += [("ST", i + 1)] if nxt else []
        steps += [("R", i), ("PT", i), ("PV", i)]
        steps += [("N", i + 1), ("TQ", i + 1), ("VE", i + 1)] if nxt else []
        return steps + [("Q", i)]

    N = B * J
    with nc.Block() as block:
        s.run(block, [("A", 0), ("ST", 0), ("N", 0), ("TQ", 0), ("VE", 0)] + body(0, last=False), body,
              body(N - 1, nxt=False) + [("O", N - 1)], (1, N - 1))



NE = 8
W_UP = 64.0
GROUP = 4
GT = GROUP * P


def layer1_experts(nc, a, t, ctx):
    def sb(name, shape, dt=F32):
        return ctx.enter_context(nc.sbuf_tensor(name, shape, dt))

    x, gates, ident = t["x"], t["gates"], t["ident"]
    bank = [ctx.enter_context(nc.psum_tensor(f"ps2_{n}", [P, 512], F32)) for n in range(8)]
    win = sb("w_in", [P, 2, NE, KD, FF], F16)
    wout = sb("w_out", [P, 2, NE, KF, D], F16)
    wr = sb("w_router", [P, KD, NE])
    rT = sb("rowsT", [P, KD, 2, B * P], F16)
    gate = sb("gate", [P, B, NE])
    order = sb("order", [P, NE])
    top = sb("top", [P, 8])

    got, used, small, made = (nc.alloc_semaphore(n) for n in ("w2_got", "w2_used", "w2_small", "w2_made"))
    with nc.sbuf_tensor("raw2", [P, 2, 2048], F32) as raw, nc.sbuf_tensor("work2", [P, 2, 2048], F32) as work:
        items = [(k, n) for k in ("winT", "woutT") for n in range(4)]
        with nc.Block() as block:
            @block.sync
            def _(e):
                e.dma_start(wr[:, :, :], a["WrT"].rearrange("(k p) n -> p k n", p=P)).then_inc(small, 16)
                for n, (name, q) in enumerate(items):
                    if n >= 2:
                        e.wait_ge(used, n - 1)
                    src = a[name].rearrange("e (k p) n -> p e k n", p=P)[:, 2 * q:2 * q + 2]
                    for h in range(2):
                        e.dma_start(raw[:, n % 2, h * 1024:(h + 1) * 1024].rearrange("p (k n) -> p k n", k=src.shape[2]),
                                    src[:, h]).then_inc(got, 16)
                    e.wait_ge(got, 32 * (n + 1))
                e.wait_ge(small, 16)

            @block.gpsimd
            def _(e):
                for n in range(NE):
                    e.memset(order[:, n:n + 1], float(n))
                e.memset(top[:, :], 0.0).then_inc(made, 1)

            @block.vector
            def _(e):
                chain = Chain(nc, "w2_chain", 2 * len(items))
                chain.start(e, 0)
                for n, (name, q) in enumerate(items):
                    w = (win if name == "winT" else wout)
                    e.wait_ge(got, 32 * (n + 1))
                    if n >= 2:
                        e.wait_ge(used, n - 1)
                    chain.link(e.tensor_scalar(work[:, n % 2, :], raw[:, n % 2, :], W_UP, None, ALU.mult))
                    parts = split(e, *(w[:, hl, 2 * q:2 * q + 2, :, :].rearrange("p e k n -> p (e k n)") for hl in range(2)),
                                  work[:, n % 2, :])
                    chain.link(next(parts))
                    next(parts).then_inc(used, 1)
                chain.end()
                e.drain()

    r = Pieces(nc)
    stats, mv, rstd, spare = sb("stats_m", [P, 2, 6]), sb("mv_m", [P, 2, 2]), sb("rstd_m", [P, 2]), sb("spare_m", [P, 1])
    rows, u = sb("rows_m", [P, 2, D]), sb("rowsT32", [P, 2, KD, P])
    logit, best, found = sb("logit", [P, 2, NE]), sb("best", [P, 2, 8]), sb("found", [P, 2, 8], U32)
    foundf, soft, pick = sb("foundf", [P, 2, 8]), sb("soft", [P, 2, 4]), sb("picked", [P, 2, 2, NE])
    r_stat, r_rstd, r_n = r.flag("m_stat", "vector"), r.flag("m_rstd", "gpsimd"), r.flag("m_n", "vector")
    r_T, r_u, r_hi = r.flag("m_T", "tensor"), r.flag("m_u", "scalar"), r.flag("m_hi", "scalar")
    r_lo, r_lg, r_d = r.flag("m_lo", "vector"), r.flag("m_lg", "tensor"), r.flag("m_d", "vector")
    r_e = r.flag("m_e", "scalar")
    c_1, c_1g, c_3 = Chain(nc, "c_m1", 1), Chain(nc, "c_m1g", 1), Chain(nc, "c_m3", 8)

    @r.piece("1", "vector")
    def _(e, i, b):
        c_1.start(e, i)
        c_1.link(e.bn_stats(stats[:, b, :], x[:, i, :]))
        e.memset(spare[:, :], 0.0)
        e.bn_aggr(mv[:, b, :], stats[:, b, :]).then_inc(r_stat.sem, 1)
        c_1.end()

    @r.piece("1", "gpsimd")
    def _(e, i, b):
        c_1g.start(e, i)
        e.wait_ge(r_stat.sem, r_stat.at(i))
        c_1g.link(e.tensor_tensor(rstd[:, b:b + 1], mv[:, b, 1:2], t["eps"][:, 0:1], ALU.add))
        e.tensor_tensor(rstd[:, b:b + 1], rstd[:, b:b + 1], t["half"][:, 0:1], ALU.pow).then_inc(r_rstd.sem, 1)
        c_1g.end()

    @r.piece("2", "vector")
    def _(e, i, b):
        e.wait_ge(r_rstd.sem, r_rstd.at(i))
        e.wait_ge(r_T.sem, r_T.at(i - 1))
        e.tensor_scalar(rows[:, b, :], x[:, i, :], mv[:, b, 0:1], rstd[:, b:b + 1], ALU.subtract,
                        ALU.mult).then_inc(r_n.sem, 1)

    @r.piece("2", "tensor")
    def _(e, i, b):
        e.wait_ge(r_n.sem, r_n.at(i))
        e.wait_ge(r_hi.sem, r_hi.at(i - 1))
        for k in range(KD):
            last = e.transpose(bank[0][:, k * P:(k + 1) * P], rows[:, b, k * P:(k + 1) * P], ident[:, :])
        last.then_inc(r_T.sem, 1)

    @r.piece("2", "scalar")
    def _(e, i, b):
        e.wait_ge(r_T.sem, r_T.at(i))
        e.wait_ge(r_lg.sem, r_lg.at(i - 1))
        e.wait_ge(r_lo.sem, r_lo.at(i - 1))
        at = bass.ds(i * P, P)
        src = bank[0][:, 0:D].rearrange("p (k t) -> p k t", k=KD)
        e.activation(u[:, b, :, :], src, ACT.Copy).then_inc(r_u.sem, 1)
        e.activation(rT[:, :, 0, at], src, ACT.Copy).then_inc(r_hi.sem, 1)

    @r.piece("2b", "tensor")
    def _(e, i, b):
        e.wait_ge(r_u.sem, r_u.at(i))
        e.wait_ge(r_d.sem, r_d.at(i - 1))
        for k in range(KD):
            last = e.matmul(bank[1][:, 0:NE], u[:, b, k, :], wr[:, k, :], start=(k == 0), stop=(k == KD - 1))
        last.then_inc(r_lg.sem, 1)

    @r.piece("3", "vector")
    def _(e, i, b):
        c_3.start(e, i)
        at = bass.ds(i * P, P)
        e.wait_ge(r_hi.sem, r_hi.at(i))
        e.tensor_tensor(rT[:, :, 1, at], u[:, b, :, :], rT[:, :, 0, at], ALU.subtract).then_inc(r_lo.sem, 1)
        e.wait_ge(r_lg.sem, r_lg.at(i))
        c_3.link(e.tensor_copy(logit[:, b, :], bank[1][:, 0:NE]))
        e.memset(spare[:, :], 0.0)
        c_3.link(e.max(best[:, b, :], logit[:, b, :]))
        e.memset(spare[:, :], 0.0)
        c_3.link(e.max_index(found[:, b, :], best[:, b, :], logit[:, b, :]))
        e.tensor_copy(foundf[:, b, :], found[:, b, :])
        e.tensor_tensor(soft[:, b, 0:1], best[:, b, 1:2], best[:, b, 0:1], ALU.subtract).then_inc(r_d.sem, 1)
        e.wait_ge(r_e.sem, r_e.at(i))
        c_3.link(e.tensor_scalar(soft[:, b, 2:3], soft[:, b, 1:2], 1.0, None, ALU.add))
        c_3.link(e.reciprocal(soft[:, b, 2:3], soft[:, b, 2:3]))
        c_3.link(e.tensor_tensor(soft[:, b, 3:4], soft[:, b, 1:2], soft[:, b, 2:3], ALU.mult))
        for n in range(2):
            m = e.tensor_scalar(pick[:, b, n, :], order[:, :], foundf[:, b, n:n + 1], soft[:, b, 2 + n:3 + n],
                                ALU.is_equal, ALU.mult)
        c_3.link(m)
        c_3.link(e.tensor_tensor(pick[:, b, 0, :], pick[:, b, 0, :], pick[:, b, 1, :], ALU.add))
        e.tensor_scalar(gate[:, i, :], pick[:, b, 0, :], gates[:, 3:4], 1.0 / W_UP, ALU.mult, ALU.mult)
        c_3.end()

    @r.piece("3", "scalar")
    def _(e, i, b):
        e.wait_ge(r_d.sem, r_d.at(i))
        e.activation(soft[:, b, 1:2], soft[:, b, 0:1], ACT.Exp).then_inc(r_e.sem, 1)

    with nc.Block() as block:
        two = lambda n: [("1", 2 * n, 0), ("1", 2 * n + 1, 1), ("2", 2 * n, 0), ("2b", 2 * n, 0),
                         ("2", 2 * n + 1, 1), ("3", 2 * n, 0), ("2b", 2 * n + 1, 1), ("3", 2 * n + 1, 1)]
        r.run(block, [], two, [], (0, B // 2))

    s = Pieces(nc)
    Hb, Y = bank[0:4], bank[4:8]
    h32 = sb("h32", [P, KF, GT])
    hh = sb("hidden", [P, 2, 2, KF, GT], F16)
    pe_H, a_h, v_hi, v_lo = (s.flag("pe_H", "tensor", KF), s.flag("a_h", "scalar", KF),
                             s.flag("v_hi", "vector", KF), s.flag("v_lo", "vector", KF))
    pe_Y, v_Y = s.flag("pe_Y", "tensor", GROUP), s.flag("v_Y", "vector", GROUP)

    @s.piece("H", "tensor")
    def _(e, i, b):
        rows_at = bass.ds((i // NE) * GT, GT)
        for m in range(KF):
            e.wait_ge(a_h.sem, a_h.at(i - 1, m + 1))
            for k in range(KD):
                for part, hl in ((0, 0), (0, 1), (1, 0)):
                    w = win[:, hl, bass.ds(i % NE, 1), k, m * P:(m + 1) * P].rearrange("p e n -> p (e n)")
                    last = e.matmul(Hb[m][:, :], w, rT[:, k, part, rows_at], start=(k == 0 and part == hl == 0),
                                    stop=(k == KD - 1 and part == 1))
            last.then_inc(pe_H.sem, 1)

    @s.piece("H", "scalar")
    def _(e, i, b):
        for m in range(KF):
            e.wait_ge(pe_H.sem, pe_H.at(i, m + 1))
            e.wait_ge(v_lo.sem, v_lo.at(i - 1, m + 1))
            e.activation(h32[:, m, :], Hb[m][:, :], ACT.Silu, scale=1.0 / W_UP).then_inc(a_h.sem, 1)

    @s.piece("H", "vector")
    def _(e, i, b):
        e.wait_ge(pe_Y.sem, pe_Y.at(i - 2))
        for m in range(KF):
            e.wait_ge(a_h.sem, a_h.at(i, m + 1))
            e.tensor_copy(hh[:, b, 0, m, :], h32[:, m, :]).then_inc(v_hi.sem, 1)
            e.wait_ge(v_hi.sem, v_hi.at(i, m + 1))
            e.tensor_tensor(hh[:, b, 1, m, :], h32[:, m, :], hh[:, b, 0, m, :], ALU.subtract).then_inc(v_lo.sem, 1)

    @s.piece("Y", "tensor")
    def _(e, i, b):
        for q in range(GROUP):
            e.wait_ge(v_Y.sem, v_Y.at(i - 1, q + 1))
            for m in range(KF):
                if q == 0:
                    e.wait_ge(v_lo.sem, v_lo.at(i, m + 1))
                for part, hl in ((0, 0), (0, 1), (1, 0)):
                    w = wout[:, hl, bass.ds(i % NE, 1), m, :].rearrange("p e n -> p (e n)")
                    last = e.matmul(Y[q][:, 0:D], hh[:, b, part, m, q * P:(q + 1) * P], w,
                                    start=(m == 0 and part == hl == 0), stop=(m == KF - 1 and part == 1))
            last.then_inc(pe_Y.sem, 1)

    @s.piece("Y", "vector")
    def _(e, i, b):
        for q in range(GROUP):
            e.wait_ge(pe_Y.sem, pe_Y.at(i, q + 1))
            at = (i // NE) * GROUP + q
            row = x[:, bass.ds(at, 1), :].rearrange("p b d -> p (b d)")
            g = gate[:, bass.ds(at, 1), bass.ds(i % NE, 1)].rearrange("p b e -> p (b e)")
            e.scalar_tensor_tensor(row, Y[q][:, 0:D], g, row, ALU.mult, ALU.add).then_inc(v_Y.sem, 1)

    N = NE * B // GROUP

    def pair(n):
        return [("H", 2 * n + 1, 1), ("Y", 2 * n, 0), ("H", 2 * n + 2, 0), ("Y", 2 * n + 1, 1)]

    with nc.Block() as block:
        s.run(block, [("H", 0, 0)], pair, [("H", N - 1, 1), ("Y", N - 2, 0), ("Y", N - 1, 1)], (0, N // 2 - 1))


def store_rows(nc, t, out):
    done = nc.alloc_semaphore("stored")
    with nc.Block() as block:
        @block.sync
        def _(e):
            e.dma_start(out.rearrange("b p d -> p b d"), t["x"][:, :, :]).then_inc(done, 16)
            e.wait_ge(done, 16)


def program(nc, a, out, phases):
    from contextlib import ExitStack

    t = prepare_common(nc, a)
    with ExitStack() as ctx:
        if phases[0]:
            layer0(nc, a, t, ctx)
    with ExitStack() as ctx:
        if phases[1]:
            layer1_attention(nc, a, t, ctx)
    with ExitStack() as ctx:
        if phases[2]:
            layer1_experts(nc, a, t, ctx)
    store_rows(nc, t, out)




def hadamard(n):
    h = np.ones((1, 1), np.float32)
    while h.shape[0] < n:
        h = np.block([[h, h], [h, -h]])
    return np.ascontiguousarray(h, np.float32)


def lay_out(v):
    a = {}
    a["x"] = v["x"]
    a["ctxT"] = v["ctx_2048"].reshape(B * P, D).T
    a["g_xattn"], a["g_ffn"] = v["g_xattn"], v["g_ffn"]
    a["causal"] = v["mask_SxS2_bc0"]
    a["padding"] = v["mask_BxS2_bk0"]
    a["WqT"] = v["L0_xattn_Wq"].T
    a["bq"] = v["L0_xattn_bq"].reshape(KD, P).T
    wk = np.broadcast_to(v["L0_xattn_Wk"].reshape(G0, 1, HD0, D), (G0, R0, HD0, D))
    a["WkT"] = wk.reshape(G0 * R0 * HD0, D).T
    bk = np.broadcast_to(v["L0_xattn_bk"].reshape(G0, 1, HD0), (G0, R0, HD0))
    a["bk"] = bk.reshape(KD, P).T
    a["WvT"] = v["L0_xattn_Wv"].T
    a["bv"] = v["L0_xattn_bv"]
    a["bo"] = v["L0_xattn_bo"]
    a["WoT"] = v["L0_xattn_Wo"].reshape(D, G0, R0, HD0).transpose(1, 3, 2, 0)
    a["w_upT"] = v["L0_ffn_w_up"].T
    a["w_downT"] = v["L0_ffn_w_down"].T
    a["had256"], a["had512"] = hadamard(D), hadamard(FF)
    rows = np.arange(P)
    a["pick"] = ((rows[:, None] // HD0) % R0 == np.arange(R0)[None, :]).astype(np.float32) * np.float32(HD0**-0.5)
    a["in_scales"] = np.stack([v[f"L1_xattn_{n}_in_scale"] for n in ("q", "qx", "k", "v")], axis=1)
    a["ln_w"], a["ln_b"] = v["L1_xattn_ln_w"].reshape(KD, P).T, v["L1_xattn_ln_b"].reshape(KD, P).T
    a["w_scales"] = np.stack([v[f"L1_xattn_{n}_scale"] for n in ("wq", "wqx", "wk", "wv", "proj_w")])
    a["proj_in_scale"] = v["L1_xattn_proj_in_scale"].reshape(1)
    a["head_ln"] = np.stack([v[f"L1_xattn_{n}ln_{c}"] for n in ("q", "qx", "k", "kx") for c in "wb"], axis=1)
    a["smooth"] = v["L1_xattn_proj_smooth"].reshape(32, P).T
    for n in ("wq", "wqx", "wk", "wv"):
        a[n + "T"] = v["L1_xattn_" + n].T
    a["wkxT"], a["wvxT"] = v["L1_xattn_w_kv_x"][:G1 * HD1].T, v["L1_xattn_w_kv_x"][G1 * HD1:].T
    a["WrT"] = v["L1_ffn_Wr"].T
    a["winT"], a["woutT"] = v["L1_ffn_Win"].transpose(0, 2, 1), v["L1_ffn_Wout"].transpose(0, 2, 1)
    a["wprojT"] = v["L1_xattn_wproj"].T
    return {k: np.ascontiguousarray(x) for k, x in a.items()}


PHASES = (1, 1, 1)


def kernel(**inputs):
    import concourse.bacc as bacc
    from concourse.bass_utils import run_bass_kernel_spmd

    nc = bacc.Bacc("TRN2", target_bir_lowering=False, num_devices=1)
    arrays = {f"in_{k}": x for k, x in lay_out(inputs).items()}
    aps = {k[3:]: nc.dram_tensor(k, x.shape, mybir.dt.from_np(x.dtype), kind="ExternalInput").ap()
           for k, x in arrays.items()}
    out = nc.dram_tensor("out_0", (B, P, D), F32, kind="ExternalOutput").ap()
    program(nc, aps, out, PHASES)
    r = run_bass_kernel_spmd(nc, [arrays], core_ids=[0])
    return r.results[0]["out_0"]
```

```python
from contextlib import ExitStack

import numpy as np

import concourse.bass as bass
from concourse import mybir
from concourse.alu_op_type import AluOpType as ALU

ACT = mybir.ActivationFunctionType
AX = mybir.AxisListType.X
F32 = mybir.dt.float32
F16 = mybir.dt.float16
BF16 = mybir.dt.bfloat16
U16 = mybir.dt.uint16
U32 = mybir.dt.uint32
U8 = mybir.dt.uint8

P = 128
B = 16
D = 256
KD = D // P
EPS = 1e-5
MAGIC = 1.5 * 2.0**23
MASKED = -1.0e30


class Flag:

    def __init__(self, nc, name, per=1, lead=1):
        self.sem, self.per, self.lead = nc.alloc_semaphore(name), per, lead

    def prime(self, engine):
        engine.sem_inc(self.sem, self.per * self.lead)

    def at(self, i, k=None):
        return (i + self.lead) * self.per + (self.per if k is None else k)


class Chain:

    def __init__(self, nc, name, per):
        self.sem, self.per, self.name = nc.alloc_semaphore(name), per, name

    def start(self, engine, i):
        self.engine, self.i, self.n = engine, i, 0

    def link(self, instruction):
        instruction.then_inc(self.sem, 1)
        self.n += 1
        self.engine.wait_ge(self.sem, self.i * self.per + self.n)

    def end(self):
        assert self.n == self.per, f"chain {self.name}: {self.n} links"


class Pieces:

    def __init__(self, nc):
        self.nc, self.flags, self.pieces = nc, {}, {}

    def flag(self, name, owner, per=1, lead=1):
        s = Flag(self.nc, name, per, lead)
        self.flags.setdefault(owner, []).append(s)
        return s

    def piece(self, name, engine):
        def keep(f):
            self.pieces[(name, engine)] = f
            return f
        return keep

    def run(self, block, before, body, after, loop):
        for owner, hook in (("tensor", block.tensor), ("vector", block.vector), ("scalar", block.scalar),
                            ("gpsimd", block.gpsimd), ("sync", block.sync)):
            self.program(owner, hook, before, body, after, loop)

    def run_pipelined(self, block, orders, count, ahead, behind):
        def at(owner, i):
            return [(name, i + shift, *item) for name, shift, *item in orders(owner)]

        def some(owner, runs):
            return [step for i in runs for step in at(owner, i) if 0 <= step[1] < count]

        self.run(block, lambda owner: some(owner, range(-ahead, behind)), at,
                 lambda owner: some(owner, range(count - ahead, count + behind)), (behind, count - ahead))

    def run_alike(self, block, before, body, after, loop):
        self.run(block, lambda owner: before, lambda owner, i: body(i), lambda owner: after, loop)

    def program(self, owner, hook, before, body, after, loop):
        @hook
        def _(e):
            def emit(steps):
                for name, i, *more in steps:
                    if (name, owner) in self.pieces:
                        self.pieces[(name, owner)](e, i, *more)
            for s in self.flags.get(owner, []):
                s.prime(e)
            emit(before(owner))
            if loop[1] > loop[0]:
                with e.Fori(*loop) as i:
                    emit(body(owner, i))
            emit(after(owner))


def order(text):
    steps = []
    for word in text.split():
        shift = word.count("+") - word.count("-")
        word = word.rstrip("+-")
        name, _, item = word.partition(":")
        steps.append((name, shift) + ((int(item),) if item else ()))
    return steps


def col(ap):
    return ap.unsqueeze(2)


def spread(ap, n):
    return ap.unsqueeze(2).to_broadcast([ap.shape[0], ap.shape[1], n])


def tiled(ap, n):
    return ap.unsqueeze(1).to_broadcast([ap.shape[0], n, ap.shape[1]])




def prepare_common(nc, a):
    t = {}
    t["x"] = nc.alloc_sbuf_tensor("x_rows", [P, B, D], F32)
    t["gates"] = nc.alloc_sbuf_tensor("gates", [P, 4], F32)
    t["ident"] = nc.alloc_sbuf_tensor("ident", [P, P], F32)
    t["ident_b"] = nc.alloc_sbuf_tensor("ident_b", [P, P], BF16)
    t["ones"] = nc.alloc_sbuf_tensor("ones", [P, P], F32)
    t["half"] = nc.alloc_sbuf_tensor("minus_half", [P, 16], F32)
    t["one_eps"] = nc.alloc_sbuf_tensor("one_eps", [P, 1], F32)
    t["eps_eps"] = nc.alloc_sbuf_tensor("eps_eps", [P, 1], F32)
    t["eps"] = nc.alloc_sbuf_tensor("eps", [P, 16], F32)
    loaded, made, cast, gated = (nc.alloc_semaphore(n) for n in ("common_loaded", "ident_made", "common_cast", "gates_made"))
    with nc.Block() as block:
        @block.sync
        def _(e):
            for q in range(4):
                e.dma_start(t["x"][:, 4 * q:4 * q + 4, :],
                            a["x"][4 * q:4 * q + 4].rearrange("b p d -> p b d")).then_inc(loaded, 16)

        @block.gpsimd
        def _(e):
            e.memset(t["ident"][:, :], 0.0).then_inc(made, 1)
            e.wait_ge(made, 1)
            e.affine_select(out=t["ident"][:, :], in_=t["ident"][:, :], compare_op=ALU.not_equal, fill=1.0,
                            base=0, pattern=[[-1, P]], channel_multiplier=1).then_inc(made, 1)
            e.memset(t["ones"][:, :], 1.0).then_inc(made, 1)
            e.memset(t["half"][:, :], -0.5).then_inc(made, 1)
            e.memset(t["eps"][:, :], EPS).then_inc(made, 1)
            e.memset(t["one_eps"][:, :], 1.0 + EPS).then_inc(made, 1)
            e.memset(t["eps_eps"][:, :], EPS * EPS).then_inc(made, 1)
            e.wait_ge(made, 7)
            e.tensor_copy(t["ident_b"][:, :], t["ident"][:, :]).then_inc(cast, 1)
            e.wait_ge(cast, 1)

        @block.scalar
        def _(e):
            for n, g in enumerate((a["g_xattn"], a["g_ffn"])):
                e.dma_start(t["gates"][:, 2 * n:2 * n + 2],
                            g.unsqueeze(0).to_broadcast([P, 2])).then_inc(loaded, 16)
            e.wait_ge(loaded, 96)
            e.activation(t["gates"][:, :], t["gates"][:, :], ACT.Tanh).then_inc(gated, 1)
            e.wait_ge(gated, 1)
    return t



H0, G0, R0, HD0 = 32, 8, 4, 8
GP = 32
GS = 3 * GP
WO_UP = 64.0
FF = 512
KF = FF // P


ORDER0 = {
    "tensor": (
        "V:7- S:2 T:0 S:3 W- T:1 V:0 V:1 S:4 P2+ P3+ T:2 S:5 T:3 F2- F3- V:2 V:3 T:4 P4+ F4- S:6 "
        "F4u- S:7 V:4 T:5 F5- T:6 F6- S:0+ S:1+ V:5 V:6 T:7 F7- F7d-"
    ),
    "vector": (
        "S:2 R:1 Vs:7- P4w P1+ T:0 P2+ S:3 R:2 Wv- T:1 F1- R:3 S:4 F2- P3v+ T:2 S:5 R:4 T:3 F3q- "
        "F4- R:5 S:6 Vs:3 T:4 F5v- P4v+ S:7 T:5 R:6 P3k+ S:0+ T:6 R:7 F6q- T:7 S:1+ R:0+ F7v-"
    ),
    "scalar": (
        "Vs:7- S:2 T:0 T:1 S:3 P2+ S:4 T:2 F2- T:3 Vs:3 S:5 F4- T:4 F4u- S:6 T:5 F5- S:7 T:6 S:0+ "
        "T:7 F7- S:1+"
    ),
    "gpsimd": "R:1 P1+ R:2 R:3 F1- R:4 R:5 R:6 R:7 R:0+",
    "sync": "P3s+",
}


def layer0(nc, a, t, ctx):
    def sb(name, shape, dt=F32):
        return ctx.enter_context(nc.sbuf_tensor(name, shape, dt))

    x, gates, ident, ident_b = t["x"], t["gates"], t["ident"], t["ident_b"]
    ctxT = sb("ctxT", [P, KD, B * P])
    wq, wk = sb("wq0", [P, KD, D]), sb("wk0", [P, KD, D])
    wv = sb("wv0", [P, KD, G0 * HD0])
    wo = sb("wo0", [P, 2, 2, R0, D], F16)
    bq, bk = sb("bq0", [P, KD]), sb("bk0", [P, KD])
    bv, bo = sb("bv0", [P, G0 * HD0]), sb("bo0", [P, D])
    had1, had2 = sb("had256", [P, KD, D]), sb("had128", [P, P])
    pick = sb("pick", [P, R0])
    low_row, high_row = sb("low_row", [P, 1]), sb("high_row", [P, 1])
    out_gate = sb("out_gate0", [P, 1])
    causal8, pad8 = sb("causal8", [P, P], U8), sb("pad8", [P, B, P], U8)
    causal, pad = sb("causal", [P, P]), sb("pad", [P, B, P])
    minus = sb("minus", [P, P], BF16)
    wup, wdn = sb("wup", [P, KD, FF], BF16), sb("wdn", [P, KF, D], BF16)
    w_scale = sb("w_scale", [P, 2])
    steps = sb("steps", [P, 2, 2])
    psum = [ctx.enter_context(nc.psum_tensor(f"ps0_{n}", [P, 512], F32)) for n in range(8)]

    wraw = ctx.enter_context(nc.sbuf_tensor("ffn_raw", [P, 2, KD * FF], F32))
    wtmp = ctx.enter_context(nc.sbuf_tensor("ffn_tmp", [P, 2, KD * FF], F32))
    woraw = ctx.enter_context(nc.sbuf_tensor("wo_raw", [P, 2, R0 * D], F32))
    wload, wdone, summed = (nc.alloc_semaphore(n) for n in ("w0_loaded", "w0_done", "w0_sum"))
    with nc.Block() as block:
        @block.sync
        def _(e):
            e.dma_start(wraw[:, 0, :].rearrange("p (k n) -> p k n", k=KD),
                        a["w_upT"].rearrange("(k p) n -> p k n", p=P)).then_inc(wload, 16)
            e.dma_start(wraw[:, 1, :].rearrange("p (k n) -> p k n", k=KF),
                        a["w_downT"].rearrange("(k p) n -> p k n", p=P)).then_inc(wload, 16)
            e.dma_start(causal8[:, :], a["causal"]).then_inc(wload, 16)
            e.dma_start(pad8[:, :, :], a["padding"].unsqueeze(0).to_broadcast([P, B, P])).then_inc(wload, 16)
            e.dma_start(woraw[:, :, :].rearrange("p h (r o) -> p h r o", r=R0),
                        a["WoT"].rearrange("h p r o -> p h r o")).then_inc(wload, 16)
            e.dma_start(wq[:, :, :], a["WqT"].rearrange("(k p) n -> p k n", p=P)).then_inc(wload, 16)
            e.dma_start(bq[:, :], a["bq"]).then_inc(wload, 16)
            e.dma_start(low_row[:, :], a["low_row"]).then_inc(wload, 16)
            e.dma_start(high_row[:, :], a["high_row"]).then_inc(wload, 16)
            e.dma_start(had2[:, :], a["had128"]).then_inc(wdone, 16)
            for dst, src in ((ctxT, a["ctxT"]), (wk, a["WkT"]), (wv, a["WvT"]), (had1, a["had256"])):
                e.dma_start(dst[:, :, :], src.rearrange("(k p) n -> p k n", p=P)).then_inc(wdone, 16)
            e.dma_start(bk[:, :], a["bk"]).then_inc(wdone, 16)
            e.dma_start(pick[:, :], a["pick"]).then_inc(wdone, 16)
            e.dma_start(bv[:, :], a["bv"].unsqueeze(0).to_broadcast([P, G0 * HD0])).then_inc(wdone, 16)
            e.dma_start(bo[:, :], a["bo"].unsqueeze(0).to_broadcast([P, D])).then_inc(wdone, 16)
            e.wait_ge(wdone, 16 * 9)

        @block.tensor
        def _(e):
            e.wait_ge(summed, 1)
            e.matmul(psum[0][:, 0:2], t["ones"][:, :], steps[:, 0, :], start=True, stop=True).then_inc(summed, 1)

        @block.vector
        def _(e):
            chain = Chain(nc, "w0_chain", 11)
            chain.start(e, 0)
            e.tensor_scalar(minus[:, :], ident[:, :], MASKED, None, ALU.mult)
            e.wait_ge(wload, 16 * 9)
            e.tensor_scalar(wq[:, :, :], wq[:, :, :], HD0**-0.5, None, ALU.mult)
            e.tensor_scalar(bq[:, :], bq[:, :], HD0**-0.5, None, ALU.mult)
            e.tensor_scalar(out_gate[:, :], gates[:, 0:1], 1.0 / WO_UP, None, ALU.mult)
            parts = [wo[:, n, :, :, :].rearrange("p h r o -> p (h r o)") for n in range(2)]
            flat = woraw[:, :, :].rearrange("p h n -> p (h n)")
            chain.link(e.tensor_scalar(flat, flat, WO_UP, None, ALU.mult))
            chain.link(e.tensor_copy(parts[0], flat))
            chain.link(e.tensor_tensor(flat, flat, parts[0], ALU.subtract))
            e.tensor_scalar(parts[1], flat, high_row[:, 0:1], None, ALU.mult)
            chain.link(e.tensor_copy(causal[:, :], causal8[:, :]))
            chain.link(e.tensor_copy(pad[:, :, :], pad8[:, :, :]))
            e.tensor_reduce(steps[:, 0, :], wraw[:, :, :], AX, ALU.add, apply_absolute_value=True).then_inc(summed, 1)
            e.wait_ge(summed, 2)
            chain.link(e.tensor_scalar(w_scale[:, :], psum[0][:, 0:2], 1.0 / (D * FF), EPS, ALU.mult, ALU.max))
            chain.link(e.reciprocal(steps[:, 1, :], w_scale[:, :]))
            for n, out in ((0, wup), (1, wdn)):
                chain.link(e.tensor_scalar(wtmp[:, n, :], wraw[:, n, :], steps[:, 1, n:n + 1], MAGIC, ALU.mult, ALU.add))
            for n, out in ((0, wup), (1, wdn)):
                chain.link(e.tensor_scalar(wraw[:, n, :], wtmp[:, n, :], MAGIC, -1.0, ALU.subtract, ALU.max))
            for n, out in ((0, wup), (1, wdn)):
                e.tensor_scalar(out[:, :, :].rearrange("p k n -> p (k n)"), wraw[:, n, :], 1.0, None, ALU.min)
            chain.end()
            e.drain()

    s = Pieces(nc)
    xt_ps, F0, F1 = psum[0], psum[6], psum[7]
    S = psum[1:5]
    O = psum[5]
    stats = sb("stats_p", [P, 6])
    mv = sb("mv_p", [P, 2])
    spare = sb("spare", [P, 1])
    rstd = sb("rstd_p", [P, 1])
    xn = sb("xn", [P, D])
    xnT = sb("xnT", [P, KD, P])
    cT = sb("cT", [P, KD, P])
    Q_HI, Q_LO, K_HI, K_LO = range(4)
    qk_part = sb("qk_part", [P, 4, KD, P], F16)
    qk_in = sb("qk_in", [GS, 2, G0, P], F16)
    qs = sb("q_stack", [GS, G0, P], F16)
    kb = sb("k_blocks", [GS, G0, R0, P], F16)
    v32 = sb("v32", [P, G0, 1, HD0])
    vp = sb("v_stack", [P, 2, G0, 2, 2, HD0], F16)
    mask = sb("mask", [P, P], BF16)
    nmax = sb("nmax", [P, G0, R0])
    nbias = sb("nbias", [P, G0, R0])
    rowsum = sb("rowsum", [P, G0, R0])
    rinv = sb("rinv", [P, G0, R0])
    prob = sb("prob", [P, 4, R0, P])
    probT = sb("probT", [P, 2, 4, R0 * P], F16)
    o_hi = sb("o_hi", [P, R0 * P], F16)
    oT = sb("oT", [P, 2, R0, P], F16)
    stats_f = sb("stats_f", [P, 6])
    mv_f = sb("mv_f", [P, 2])
    rstd_f = sb("rstd_f", [P, 1])
    yn = sb("yn", [P, D])
    ynT = sb("ynT", [P, KD, P])
    quant = sb("quant", [P, 8])
    rnd1, q1 = sb("rnd1", [P, D]), sb("q1", [P, D], BF16)
    q1T = sb("q1T", [P, KD, P], BF16)
    up, hid, fly = sb("up", [P, FF]), sb("hid", [P, KF, P]), sb("fly", [P, KF, P])
    hidT = sb("hidT", [P, KF, P])
    rnd2, q2 = sb("rnd2", [P, FF]), sb("q2", [P, FF], BF16)
    q2T = sb("q2T", [P, KF, P], BF16)
    gbo = sb("gbo", [P, D])

    sig = s.flag
    p_stat, p_rstd = sig("p_stat", "vector"), sig("p_rstd", "gpsimd")
    p_ctx = sig("p_ctx", "gpsimd")
    p_xn, p_mask = sig("p_xn", "vector"), sig("p_mask", "vector")
    p_hi = sig("p_hi", "vector", 4)
    p_v32, p_v = sig("p_v32", "vector"), sig("p_v", "vector")
    p_xT = sig("p_xT", "scalar")
    pe_xT, pe_qk, pe_v = sig("pe_xT", "tensor"), sig("pe_qk", "tensor"), sig("pe_v", "tensor")
    pe_S, pe_T, pe_O = sig("pe_S", "tensor", G0), sig("pe_T", "tensor", G0), sig("pe_O", "tensor", 2)
    v_max, v_inv = sig("v_max", "vector", G0), sig("v_inv", "vector", G0)
    a_exp, g_norm = sig("a_exp", "scalar", G0), sig("g_norm", "gpsimd", G0)
    a_PT, v_PT = sig("a_PT", "scalar", G0), sig("v_PT", "vector", G0)
    p_part, d_stack, p_in = sig("p_part", "vector"), sig("d_stack", "sync", 16 * 12), sig("p_in", "vector")
    a_oh, v_oT = sig("a_oh", "scalar", 2), sig("v_oT", "vector", 2)
    pe_W, v_x1 = sig("pe_W", "tensor"), sig("v_x1", "vector")
    f_stat, f_rstd, f_yn = sig("f_stat", "vector"), sig("f_rstd", "gpsimd"), sig("f_yn", "vector")
    pe_yT, a_yT, pe_h1 = sig("pe_yT", "tensor"), sig("a_yT", "scalar"), sig("pe_h1", "tensor")
    v_q1, pe_q1, a_q1 = sig("v_q1", "vector"), sig("pe_q1", "tensor"), sig("a_q1", "scalar")
    pe_up, a_hid, pe_hT = sig("pe_up", "tensor"), sig("a_hid", "scalar"), sig("pe_hT", "tensor")
    v_fly = sig("v_fly", "vector")
    a_hT, pe_h2, v_q2 = sig("a_hT", "scalar"), sig("pe_h2", "tensor"), sig("v_q2", "vector")
    pe_q2, a_q2, pe_dn, v_x2 = sig("pe_q2", "tensor"), sig("a_q2", "scalar"), sig("pe_dn", "tensor"), sig("v_x2", "vector")

    c_p1 = Chain(nc, "c_p1", 1)

    @s.piece("P1", "vector")
    def _(e, i):
        c_p1.start(e, i)
        c_p1.link(e.bn_stats(stats[:, :], x[:, i, :]))
        e.memset(spare[:, :], 0.0)
        e.bn_aggr(mv[:, :], stats[:, :]).then_inc(p_stat.sem, 1)
        c_p1.end()

    c_p1g = Chain(nc, "c_p1g", 1)

    @s.piece("P1", "gpsimd")
    def _(e, i):
        c_p1g.start(e, i)
        e.wait_ge(p_stat.sem, p_stat.at(i))
        c_p1g.link(e.tensor_tensor(rstd[:, :], mv[:, 1:2], t["eps"][:, 0:1], ALU.add))
        e.tensor_tensor(rstd[:, :], rstd[:, :], t["half"][:, 0:1], ALU.pow).then_inc(p_rstd.sem, 1)
        e.wait_ge(pe_v.sem, pe_v.at(i - 1))
        e.tensor_copy(cT[:, :, :], ctxT[:, :, bass.ds(i * P, P)]).then_inc(p_ctx.sem, 1)
        c_p1g.end()

    @s.piece("P2", "vector")
    def _(e, i):
        e.wait_ge(p_rstd.sem, p_rstd.at(i))
        e.tensor_scalar(xn[:, :], x[:, i, :], mv[:, 0:1], rstd[:, 0:1], ALU.subtract, ALU.mult).then_inc(p_xn.sem, 1)

    @s.piece("P2", "tensor")
    def _(e, i):
        e.wait_ge(p_xn.sem, p_xn.at(i))
        e.wait_ge(p_v32.sem, p_v32.at(i - 1))
        for k in range(KD):
            last = e.transpose(xt_ps[:, k * P:(k + 1) * P], xn[:, k * P:(k + 1) * P], ident[:, :])
        last.then_inc(pe_xT.sem, 1)

    @s.piece("P2", "scalar")
    def _(e, i):
        e.wait_ge(pe_xT.sem, pe_xT.at(i))
        e.activation(xnT[:, :, :].rearrange("p k t -> p (k t)"), xt_ps[:, 0:D], ACT.Copy).then_inc(p_xT.sem, 1)

    @s.piece("P3", "tensor")
    def _(e, i):
        e.wait_ge(p_xT.sem, p_xT.at(i))
        e.wait_ge(p_ctx.sem, p_ctx.at(i))
        for n, (w, src) in enumerate(((wq, xnT), (wk, cT))):
            for m in range(KD):
                for k in range(KD):
                    last = e.matmul(xt_ps[:, (2 * n + m) * P:(2 * n + m + 1) * P], w[:, k, m * P:(m + 1) * P],
                                    src[:, k, :], start=(k == 0), stop=(k == KD - 1))
        last.then_inc(pe_qk.sem, 1)

    @s.piece("P3v", "vector")
    def _(e, i):
        e.wait_ge(pe_qk.sem, pe_qk.at(i))
        e.wait_ge(d_stack.sem, d_stack.at(i - 1))
        for hi, bias, n in ((Q_HI, bq, 0), (K_HI, bk, 2)):
            for m in range(KD):
                e.tensor_scalar(qk_part[:, hi, m, :], xt_ps[:, (n + m) * P:(n + m + 1) * P], bias[:, m:m + 1], None,
                                ALU.add).then_inc(p_hi.sem, 1)
        e.wait_ge(p_hi.sem, p_hi.at(i))
        for hi, bias, n in ((Q_HI, bq, 0), (K_HI, bk, 2)):
            for m in range(KD):
                last = e.scalar_tensor_tensor(qk_part[:, hi + 1, m, :], xt_ps[:, (n + m) * P:(n + m + 1) * P],
                                              bias[:, m:m + 1], qk_part[:, hi, m, :], ALU.add, ALU.subtract)
        last.then_inc(p_part.sem, 1)

    def place(g):
        return g % 4 * KD + g // 4

    @s.piece("P3s", "sync")
    def _(e, i):
        e.wait_ge(p_part.sem, p_part.at(i))
        for n, (q, k) in enumerate(((Q_HI, K_HI), (Q_LO, K_HI), (Q_HI, K_LO))):
            for j in range(4):
                e.dma_start(qk_in[n * GP:(n + 1) * GP, :, j * KD:(j + 1) * KD, :],
                            qk_part[j * GP:(j + 1) * GP, q:k + 1:k - q, :, :]).then_inc(d_stack.sem, 16)

    @s.piece("P3k", "vector")
    def _(e, i):
        e.wait_ge(d_stack.sem, d_stack.at(i))
        e.wait_ge(pe_S.sem, pe_S.at(i - 1))
        e.tensor_tensor(mask[:, :], causal[:, :], pad[:, i, :], ALU.max).then_inc(p_mask.sem, 1)
        e.tensor_copy(qs[:, :, :], qk_in[:, 0, :, :])
        for r in range(R0):
            last = e.tensor_scalar(kb[:, :, r, :], qk_in[:, 1, :, :], pick[0:GS, r:r + 1], None, ALU.mult)
        last.then_inc(p_in.sem, 1)

    @s.piece("P4", "tensor")
    def _(e, i):
        e.wait_ge(p_part.sem, p_part.at(i))
        for k in range(KD):
            last = e.matmul(xt_ps[:, 0:G0 * HD0], cT[:, k, :], wv[:, k, :], start=(k == 0), stop=(k == KD - 1))
        last.then_inc(pe_v.sem, 1)

    @s.piece("P4v", "vector")
    def _(e, i):
        e.wait_ge(pe_v.sem, pe_v.at(i))
        e.tensor_tensor(v32[:, :, 0, :], xt_ps[:, 0:G0 * HD0].rearrange("p (g d) -> p g d", g=G0),
                        bv[:, :].rearrange("p (g d) -> p g d", g=G0), ALU.add).then_inc(p_v32.sem, 1)

    c_v = Chain(nc, "c_v0", 1)

    @s.piece("P4w", "vector")
    def _(e, i):
        e.wait_ge(p_v32.sem, p_v32.at(i))
        e.wait_ge(pe_O.sem, pe_O.at(i - 1))
        c_v.start(e, i)
        twice = v32[:, :, :, :].to_broadcast([P, G0, 2, HD0])
        c_v.link(e.tensor_copy(vp[:, 0, :, :, 0, :], twice))
        e.tensor_copy(vp[:, 1, :, :, 0, :], vp[:, 0, :, :, 0, :])
        e.tensor_tensor(vp[:, 0, :, :, 1, :], twice, vp[:, 0, :, :, 0, :], ALU.subtract).then_inc(p_v.sem, 1)
        c_v.end()

    @s.piece("S", "tensor")
    def _(e, i, g):
        if g == 0:
            e.wait_ge(p_in.sem, p_in.at(i))
            e.wait_ge(p_mask.sem, p_mask.at(i))
        bank = S[g % 4]
        e.matmul(bank[:, :], minus[:, :], tiled(mask[:, :], R0), start=True, stop=False)
        e.matmul(bank[:, :], qs[:, place(g), :], kb[:, place(g), :, :], start=False, stop=True).then_inc(pe_S.sem, 1)

    @s.piece("S", "vector")
    def _(e, i, g):
        e.wait_ge(pe_S.sem, pe_S.at(i, g + 1))
        e.tensor_reduce(nmax[:, g, :], S[g % 4][:, :].rearrange("p (r t) -> p r t", r=R0), AX, ALU.max,
                        negate=True).then_inc(v_max.sem, 1)

    @s.piece("S", "scalar")
    def _(e, i, g):
        e.wait_ge(v_max.sem, v_max.at(i, g + 1))
        for r in range(R0):
            last = e.activation(prob[:, g % 4, r, :], S[g % 4][:, r * P:(r + 1) * P], ACT.Exp,
                                bias=nmax[:, g, r:r + 1], accum_out=rowsum[:, g, r:r + 1])
        last.then_inc(a_exp.sem, 1)

    @s.piece("R", "vector")
    def _(e, i, g):
        e.wait_ge(a_exp.sem, a_exp.at(i, g + 1))
        e.reciprocal(rinv[:, g, :], rowsum[:, g, :]).then_inc(v_inv.sem, 1)

    @s.piece("R", "gpsimd")
    def _(e, i, g):
        e.wait_ge(v_inv.sem, v_inv.at(i, g + 1))
        e.tensor_tensor(prob[:, g % 4, :, :], prob[:, g % 4, :, :], spread(rinv[:, g, :], P),
                        ALU.mult).then_inc(g_norm.sem, 1)

    @s.piece("T", "tensor")
    def _(e, i, g):
        e.wait_ge(g_norm.sem, g_norm.at(i, g + 1))
        for r in range(R0):
            last = e.transpose(S[g % 4][:, r * P:(r + 1) * P], prob[:, g % 4, r, :], ident[:, :])
        last.then_inc(pe_T.sem, 1)

    @s.piece("T", "scalar")
    def _(e, i, g):
        e.wait_ge(pe_T.sem, pe_T.at(i, g + 1))
        e.activation(probT[:, 0, g % 4, :], S[g % 4][:, :], ACT.Copy).then_inc(a_PT.sem, 1)

    @s.piece("T", "vector")
    def _(e, i, g):
        e.wait_ge(a_PT.sem, a_PT.at(i, g + 1))
        e.tensor_tensor(probT[:, 1, g % 4, :], S[g % 4][:, :], probT[:, 0, g % 4, :], ALU.subtract).then_inc(v_PT.sem, 1)

    @s.piece("V", "tensor")
    def _(e, i, g):
        e.wait_ge(v_PT.sem, v_PT.at(i, g + 1))
        if g == 0:
            e.wait_ge(p_v.sem, p_v.at(i))
            e.wait_ge(v_oT.sem, v_oT.at(i - 1))
        if g == 4:
            e.wait_ge(v_oT.sem, v_oT.at(i, 1))
        j = g % 4
        for part in range(2):
            m = e.matmul(O[GP * j:GP * j + GP, :], vp[:, part, g, :, :, :].rearrange("p a b d -> p (a b d)"),
                         probT[:, part, g % 4, :], start=(part == 0), stop=(part == 1), tile_position=(0, GP * j))
        if j == 3:
            m.then_inc(pe_O.sem, 1)

    @s.piece("Vs", "scalar")
    def _(e, i, g):
        if g % 4 == 3:
            e.wait_ge(pe_O.sem, pe_O.at(i, g // 4 + 1))
            n = g // 4
            e.wait_ge(v_oT.sem, v_oT.at(i - 1) if n == 0 else v_oT.at(i, 1))
            e.activation(o_hi[:, :], O[:, :], ACT.Copy).then_inc(a_oh.sem, 1)

    @s.piece("Vs", "vector")
    def _(e, i, g):
        if g % 4 == 3:
            n = g // 4
            e.wait_ge(a_oh.sem, a_oh.at(i, n + 1))
            e.wait_ge(pe_W.sem, pe_W.at(i - 1))
            e.scalar_tensor_tensor(oT[:, n, :, :].rearrange("p r t -> p (r t)"), o_hi[:, :], low_row[:, 0:1],
                                   O[:, :], ALU.mult, ALU.add).then_inc(v_oT.sem, 1)

    @s.piece("W", "tensor")
    def _(e, i):
        e.wait_ge(v_oT.sem, v_oT.at(i))
        e.wait_ge(a_q2.sem, a_q2.at(i - 1))
        for half in range(2):
            for r in range(R0):
                for part in range(2):
                    last = e.matmul(F0[:, 0:D], oT[:, half, r, :], wo[:, part, half, r, :],
                                    start=(half == r == part == 0), stop=(half == 1 and r == R0 - 1 and part == 1))
        last.then_inc(pe_W.sem, 1)

    c_w = Chain(nc, "c_w", 1)

    @s.piece("Wv", "vector")
    def _(e, i):
        c_w.start(e, i)
        e.wait_ge(pe_W.sem, pe_W.at(i))
        c_w.link(e.scalar_tensor_tensor(x[:, i, :], F0[:, 0:D], out_gate[:, 0:1], x[:, i, :], ALU.mult, ALU.add))
        e.tensor_tensor(x[:, i, :], x[:, i, :], gbo[:, :], ALU.add).then_inc(v_x1.sem, 1)
        c_w.end()

    c_f1 = Chain(nc, "c_f1", 1)

    @s.piece("F1", "vector")
    def _(e, i):
        c_f1.start(e, i)
        e.wait_ge(v_x1.sem, v_x1.at(i))
        e.memset(spare[:, :], 0.0)
        c_f1.link(e.bn_stats(stats_f[:, :], x[:, i, :]))
        e.memset(spare[:, :], 0.0)
        e.bn_aggr(mv_f[:, :], stats_f[:, :]).then_inc(f_stat.sem, 1)
        c_f1.end()

    c_f1g = Chain(nc, "c_f1g", 1)

    @s.piece("F1", "gpsimd")
    def _(e, i):
        c_f1g.start(e, i)
        e.wait_ge(f_stat.sem, f_stat.at(i))
        c_f1g.link(e.tensor_tensor(rstd_f[:, :], mv_f[:, 1:2], t["eps"][:, 0:1], ALU.add))
        e.tensor_tensor(rstd_f[:, :], rstd_f[:, :], t["half"][:, 0:1], ALU.pow).then_inc(f_rstd.sem, 1)
        c_f1g.end()

    @s.piece("F2", "vector")
    def _(e, i):
        e.wait_ge(f_rstd.sem, f_rstd.at(i))
        e.tensor_scalar(yn[:, :], x[:, i, :], mv_f[:, 0:1], rstd_f[:, 0:1], ALU.subtract,
                        ALU.mult).then_inc(f_yn.sem, 1)

    @s.piece("F2", "tensor")
    def _(e, i):
        e.wait_ge(f_yn.sem, f_yn.at(i))
        for k in range(KD):
            last = e.transpose(F0[:, k * P:(k + 1) * P], yn[:, k * P:(k + 1) * P], ident[:, :])
        last.then_inc(pe_yT.sem, 1)

    @s.piece("F2", "scalar")
    def _(e, i):
        e.wait_ge(pe_yT.sem, pe_yT.at(i))
        e.activation(ynT[:, :, :].rearrange("p k t -> p (k t)"), F0[:, 0:D], ACT.Copy).then_inc(a_yT.sem, 1)

    @s.piece("F3", "tensor")
    def _(e, i):
        e.wait_ge(a_yT.sem, a_yT.at(i))
        e.wait_ge(v_x2.sem, v_x2.at(i - 1))
        for k in range(KD):
            last = e.matmul(F1[:, 0:D], ynT[:, k, :], had1[:, k, :], start=(k == 0), stop=(k == KD - 1))
        last.then_inc(pe_h1.sem, 1)

    def quantise(e, chain, src, width, norm, c, rnd, out, done):
        chain.link(e.tensor_reduce(quant[:, c:c + 1], src, AX, ALU.max, apply_absolute_value=True))
        if c == 4:
            chain.link(e.tensor_tensor(quant[:, c:c + 1], quant[:, c:c + 1], quant[:, 7:8], ALU.mult))
            chain.link(e.tensor_scalar(quant[:, c:c + 1], quant[:, c:c + 1], norm, EPS, ALU.mult, ALU.max))
        else:
            chain.link(e.tensor_scalar(quant[:, c:c + 1], quant[:, c:c + 1], norm, EPS, ALU.mult, ALU.max))
        chain.link(e.reciprocal(quant[:, c + 1:c + 2], quant[:, c:c + 1]))
        if c == 4:
            chain.link(e.tensor_scalar(quant[:, c + 2:c + 3], quant[:, c + 1:c + 2], quant[:, 7:8], 127.0 * norm,
                                       ALU.mult, ALU.mult))
        else:
            chain.link(e.tensor_scalar(quant[:, c + 2:c + 3], quant[:, c + 1:c + 2], 127.0 * norm, None, ALU.mult))
        chain.link(e.tensor_scalar(rnd, src, quant[:, c + 2:c + 3], MAGIC, ALU.mult, ALU.add))
        e.tensor_scalar(out, rnd, MAGIC, None, ALU.subtract).then_inc(done.sem, 1)

    c_f3 = Chain(nc, "c_f3", 5)

    @s.piece("F3q", "vector")
    def _(e, i):
        c_f3.start(e, i)
        e.wait_ge(pe_h1.sem, pe_h1.at(i))
        quantise(e, c_f3, F1[:, 0:D], D, D**-0.5, 0, rnd1[:, :], q1[:, :], v_q1)
        c_f3.end()

    @s.piece("F4", "tensor")
    def _(e, i):
        e.wait_ge(v_q1.sem, v_q1.at(i))
        for k in range(KD):
            last = e.transpose(F0[:, k * 64:(k + 1) * 64].bitcast(BF16), q1[:, k * P:(k + 1) * P], ident_b[:, :])
        last.then_inc(pe_q1.sem, 1)

    @s.piece("F4u", "tensor")
    def _(e, i):
        e.wait_ge(a_q1.sem, a_q1.at(i))
        for k in range(KD):
            last = e.matmul(F1[:, :], q1T[:, k, :], wup[:, k, :], start=(k == 0), stop=(k == KD - 1))
        last.then_inc(pe_up.sem, 1)

    c_f4 = Chain(nc, "c_f4", 1)

    @s.piece("F4", "scalar")
    def _(e, i):
        e.wait_ge(pe_q1.sem, pe_q1.at(i))
        e.activation(q1T[:, :, :].rearrange("p k t -> p (k t)"), F0[:, 0:P].bitcast(BF16), ACT.Copy).then_inc(a_q1.sem, 1)

    @s.piece("F4u", "scalar")
    def _(e, i):
        c_f4.start(e, i)
        e.wait_ge(pe_up.sem, pe_up.at(i))
        c_f4.link(e.activation(up[:, :], F1[:, :], ACT.Relu))
        e.activation(hid[:, :, :].rearrange("p k n -> p (k n)"), up[:, :], ACT.Square).then_inc(a_hid.sem, 1)
        c_f4.end()

    c_f4v = Chain(nc, "c_f4v", 2)

    @s.piece("F4", "vector")
    def _(e, i):
        c_f4v.start(e, i)
        c_f4v.link(e.tensor_scalar(quant[:, 3:4], quant[:, 0:1], w_scale[:, 0:1], 1.0 / 127.0, ALU.mult, ALU.mult))
        c_f4v.link(e.tensor_tensor(quant[:, 7:8], quant[:, 3:4], quant[:, 3:4], ALU.mult))
        c_f4v.end()

    c_f5 = Chain(nc, "c_f5", 1)

    @s.piece("F5v", "vector")
    def _(e, i):
        c_f5.start(e, i)
        e.wait_ge(a_hid.sem, a_hid.at(i))
        e.wait_ge(pe_hT.sem, pe_hT.at(i - 1))
        e.tensor_tensor(fly[:, 0:4:2, :], hid[:, 0:4:2, :], hid[:, 1:4:2, :], ALU.add)
        c_f5.link(e.tensor_tensor(fly[:, 1:4:2, :], hid[:, 0:4:2, :], hid[:, 1:4:2, :], ALU.subtract))
        e.tensor_tensor(hid[:, 0:2, :], fly[:, 0:2, :], fly[:, 2:4, :], ALU.add)
        e.tensor_tensor(hid[:, 2:4, :], fly[:, 0:2, :], fly[:, 2:4, :], ALU.subtract).then_inc(v_fly.sem, 1)
        c_f5.end()

    @s.piece("F5", "tensor")
    def _(e, i):
        e.wait_ge(v_fly.sem, v_fly.at(i))
        for k in range(KF):
            last = e.transpose(F0[:, k * P:(k + 1) * P], hid[:, k, :], ident[:, :])
        last.then_inc(pe_hT.sem, 1)

    @s.piece("F5", "scalar")
    def _(e, i):
        e.wait_ge(pe_hT.sem, pe_hT.at(i))
        e.activation(hidT[:, :, :].rearrange("p k t -> p (k t)"), F0[:, :], ACT.Copy).then_inc(a_hT.sem, 1)

    @s.piece("F6", "tensor")
    def _(e, i):
        e.wait_ge(a_hT.sem, a_hT.at(i))
        for k in range(KF):
            last = e.matmul(F1[:, k * P:(k + 1) * P], hidT[:, k, :], had2[:, :], start=True, stop=True)
        last.then_inc(pe_h2.sem, 1)

    c_f6 = Chain(nc, "c_f6", 6)

    @s.piece("F6q", "vector")
    def _(e, i):
        c_f6.start(e, i)
        e.wait_ge(pe_h2.sem, pe_h2.at(i))
        quantise(e, c_f6, F1[:, :], FF, FF**-0.5, 4, rnd2[:, :], q2[:, :], v_q2)
        c_f6.end()

    @s.piece("F7", "tensor")
    def _(e, i):
        e.wait_ge(v_q2.sem, v_q2.at(i))
        for k in range(KF):
            last = e.transpose(F0[:, k * 64:(k + 1) * 64].bitcast(BF16), q2[:, k * P:(k + 1) * P], ident_b[:, :])
        last.then_inc(pe_q2.sem, 1)

    @s.piece("F7d", "tensor")
    def _(e, i):
        e.wait_ge(a_q2.sem, a_q2.at(i))
        for k in range(KF):
            last = e.matmul(F1[:, 0:D], q2T[:, k, :], wdn[:, k, :], start=(k == 0), stop=(k == KF - 1))
        last.then_inc(pe_dn.sem, 1)

    @s.piece("F7", "scalar")
    def _(e, i):
        e.wait_ge(pe_q2.sem, pe_q2.at(i))
        e.activation(q2T[:, :, :].rearrange("p k t -> p (k t)"), F0[:, 0:2 * P].bitcast(BF16),
                     ACT.Copy).then_inc(a_q2.sem, 1)

    c_f7 = Chain(nc, "c_f7", 2)

    @s.piece("F7v", "vector")
    def _(e, i):
        c_f7.start(e, i)
        c_f7.link(e.tensor_scalar(quant[:, 3:4], quant[:, 4:5], w_scale[:, 1:2], 1.0 / 127.0, ALU.mult, ALU.mult))
        c_f7.link(e.tensor_tensor(quant[:, 3:4], quant[:, 3:4], gates[:, 2:3], ALU.mult))
        e.wait_ge(pe_dn.sem, pe_dn.at(i))
        e.scalar_tensor_tensor(x[:, i, :], F1[:, 0:D], quant[:, 3:4], x[:, i, :], ALU.mult,
                               ALU.add).then_inc(v_x2.sem, 1)
        c_f7.end()

    def body(owner, i, nxt=True, prev=True):
        return [(name, i + shift, *item) for name, shift, *item in order(ORDER0[owner])
                if shift == 0 or (nxt if shift == 1 else prev)]

    with nc.Block() as block:
        @block.vector
        def _(e):
            e.memset(vp[:, :, :, :, :, :].rearrange("p n g a b d -> p (n g a b d)"), 0.0)
            e.tensor_scalar(gbo[:, :], bo[:, :], gates[:, 0:1], None, ALU.mult)
            e.drain()

    def before(owner):
        return [(n, 0) for n in ("P1", "P2", "P3", "P3v", "P3s", "P4", "P4v", "P3k")] + [
            ("S", 0, 0), ("S", 0, 1), ("R", 0, 0)] + body(owner, 0, prev=False)

    def after(owner):
        return body(owner, B - 1, nxt=False) + [("V", B - 1, G0 - 1), ("Vs", B - 1, G0 - 1)] + [(n, B - 1) for n in (
            "W", "Wv", "F1", "F2", "F3", "F3q", "F4", "F4u", "F5v", "F5", "F6", "F6q", "F7", "F7d", "F7v")]

    with nc.Block() as block:
        s.run(block, before, body, after, (1, B - 1))



G1, HD1 = 8, 128
J = 4
W1 = 8 * D
Q_, QX_, K_, KX_, V_, VX_ = 0, 512, 1024, 1280, 1536, 1792
CTX_UP = 64.0
F8_MAX = 448.0
F8_TINY = 2.0**-6
F8_SHIFT = 1.5 * 2.0**20
EXPONENT = 0x7F80


def split(e, hi, lo, src):
    yield e.tensor_copy(hi, src)
    yield e.tensor_tensor(lo, src, hi, ALU.subtract)


ORDER1 = {
    "tensor": "PT:1- A:0+ SC:0 SC:1 A:1+ O-- PV:1- A:2+ PT:0 TQ:0+ A:3+ PV:0 TQ:1+ TQ:2+",
    "vector": "PT:1- QS-- SC:0 SC:1 R:0 O-- R:1 N:0+ QM:1- N:1+ PT:0 Q- N:2+ QM:0",
    "scalar": "ST:0+ SC:0 ST:1+ SC:1 VE ST:2+ TQ:0+ TQ:1+ TQ:2+",
    "gpsimd": "R:0 SU:0+ SU:1+ R:1 SU:2+ QA-",
    "sync": "",
}


def layer1_attention(nc, a, t, ctx):
    def sb(name, shape, dt=F32):
        return ctx.enter_context(nc.sbuf_tensor(name, shape, dt))

    x, gates, ident = t["x"], t["gates"], t["ident"]
    bank = [ctx.enter_context(nc.psum_tensor(f"ps1_{n}", [P, 512], F32)) for n in range(8)]
    wb = sb("w_proj_in", [P, KD, 2, J * W1], F16)
    wp = sb("w_proj_out", [P, 2, 32, D], F16)
    cx = sb("ctx_parts", [P, KD, 2, B * P], F16)
    insc = sb("in_scales", [P, KD, 4])
    inv_insc = sb("inv_in_scales", [P, KD, 4])
    row_w, row_b = sb("row_w", [P, KD, 4]), sb("row_b", [P, KD, 4])
    lnw, lnb = sb("ln_w", [P, KD]), sb("ln_b", [P, KD])
    wsc = sb("w_scales", [P, 5])
    psc = sb("proj_in_scale", [P, 1])
    hln = sb("head_ln", [P, 8])
    smooth, inv_smooth = sb("smooth", [P, 32]), sb("inv_smooth", [P, 32])
    head_eps, sign = sb("head_eps", [P, 12]), sb("sign", [P, 3])
    out_gate = sb("out_gate", [P, 1])

    items = []
    for k in range(KD):
        items += [("wqT", k, Q_, 512, 0, True), ("wqxT", k, QX_, 512, 1, True), ("wkT", k, K_, 256, 2, True),
                  ("wvT", k, V_, 256, 3, False), ("wkxT", k, KX_, 256, None, True),
                  ("wvxT", k, VX_, 256, None, False)]
    nproj = 4
    NRAW, NWORK = 2, 4
    work_items = []
    for name, k, c0, w, sc, centred in items:
        parts = [wb[:, k, hl, :].rearrange("p (j c) -> p j c", j=J)[:, :, c0:c0 + w] for hl in range(2)]
        work_items.append((a[name].rearrange("(k p) n -> p k n", p=P)[:, k, :], J * w, parts, (k, sc), centred))
    for q in range(nproj):
        parts = [wp[:, hl, 8 * q:8 * q + 8, :] for hl in range(2)]
        work_items.append((a["wprojT"].rearrange("(h p) o -> p h o", p=P)[:, 8 * q:8 * q + 8, :], 2048, parts, None, False))
    for k in range(KD):
        parts = [cx[:, k, hl, :] for hl in range(2)]
        work_items.append((a["ctxT"].rearrange("(k p) n -> p k n", p=P)[:, k, :], 2048, parts, None, False))

    def like(ap, part):
        if len(part.shape) == 2:
            return ap
        return ap.rearrange("p (m c) -> p m c", m=part.shape[1])

    with nc.sbuf_tensor("raw1", [P, NRAW, 2048], F32) as raw, nc.sbuf_tensor("work1", [P, NWORK, 2048], F32) as work, \
            nc.sbuf_tensor("head_sum", [P, NWORK, 16], F32) as head_sum:
        small, ready = nc.alloc_semaphore("w1_small"), nc.alloc_semaphore("w1_ready")
        got = [nc.alloc_semaphore(f"w1_got{n}") for n in range(NRAW)]
        scaled, meant, centred_, high, low = (nc.alloc_semaphore(f"w1_{n}") for n in (
            "scaled", "mean", "centred", "high", "low"))

        def count(n, which):
            return sum(1 for it in work_items[:n + 1] if which(it))

        is_scaled, is_centred, always = (lambda it: it[3] is not None), (lambda it: it[4]), (lambda it: True)

        def source(n):
            width = work_items[n][1]
            return work[:, n % NWORK, 0:width] if is_scaled(work_items[n]) else raw[:, n % NRAW, 0:width]

        def wait_source(e, n):
            if is_centred(work_items[n]):
                e.wait_ge(centred_, count(n, is_centred))
            elif is_scaled(work_items[n]):
                e.wait_ge(scaled, count(n, is_scaled))
            else:
                e.wait_ge(got[n % NRAW], 16 * (n // NRAW + 1))

        with nc.Block() as block:
            @block.sync
            def _(e):
                for n, (src, width, parts, sc, centred) in enumerate(work_items):
                    if n >= NRAW:
                        if is_scaled(work_items[n - NRAW]):
                            e.wait_ge(scaled, count(n - NRAW, is_scaled))
                        else:
                            e.wait_ge(low, n - NRAW + 1)
                    dst = raw[:, n % NRAW, 0:width]
                    if len(src.shape) == 3:
                        dst = dst.rearrange("p (h o) -> p h o", h=8)
                    e.dma_start(dst, src).then_inc(got[n % NRAW], 16)

            @block.scalar
            def _(e):
                e.dma_start(insc[:, :, :], a["in_scales"].rearrange("(k p) n -> p k n", p=P)).then_inc(small, 16)
                e.dma_start(lnw[:, :], a["ln_w"]).then_inc(small, 16)
                e.dma_start(lnb[:, :], a["ln_b"]).then_inc(small, 16)
                e.dma_start(wsc[:, :], a["w_scales"].unsqueeze(0).to_broadcast([P, 5])).then_inc(small, 16)
                e.dma_start(psc[:, :], a["proj_in_scale"].unsqueeze(0).to_broadcast([P, 1])).then_inc(small, 16)
                e.dma_start(hln[:, :], a["head_ln"]).then_inc(small, 16)
                e.dma_start(smooth[:, :], a["smooth"]).then_inc(small, 16)
                e.wait_ge(small, 16 * 7)

                def scale(n):
                    _, width, _, sc, _ = work_items[n]
                    e.wait_ge(got[n % NRAW], 16 * (n // NRAW + 1))
                    if n >= NWORK:
                        e.wait_ge(low, n - NWORK + 1)
                    k, c = sc
                    e.activation(work[:, n % NWORK, 0:width], raw[:, n % NRAW, 0:width], ACT.Copy,
                                 scale=CTX_UP if c is None else insc[:, k, c:c + 1]).then_inc(scaled, 1)

                for n in range(-2, len(work_items)):
                    if n + 2 < len(work_items) and is_scaled(work_items[n + 2]):
                        scale(n + 2)
                    if n >= 0:
                        wait_source(e, n)
                        part = work_items[n][2][0]
                        e.activation(part, like(source(n), part), ACT.Copy).then_inc(high, 1)
                e.wait_ge(high, len(work_items))

            @block.gpsimd
            def _(e):
                for n, (_, width, _, _, centred) in enumerate(work_items):
                    if centred:
                        heads = width // HD1
                        byhead = source(n).rearrange("p (h d) -> p h d", h=heads)
                        e.wait_ge(meant, count(n, is_centred))
                        e.tensor_tensor(byhead, byhead, spread(head_sum[:, n % NWORK, 0:heads], HD1),
                                        ALU.subtract).then_inc(centred_, 1)
                e.wait_ge(centred_, count(len(work_items), is_centred))

            @block.vector
            def _(e):
                chain = Chain(nc, "w1_chain", 15 + count(len(work_items), is_centred))
                chain.start(e, 0)
                e.wait_ge(small, 16 * 7)
                chain.link(e.reciprocal(inv_insc[:, :, :], insc[:, :, :]))
                for k in range(KD):
                    e.tensor_scalar(row_w[:, k, :], inv_insc[:, k, :], lnw[:, k:k + 1], None, ALU.mult)
                    e.tensor_scalar(row_b[:, k, :], inv_insc[:, k, :], lnb[:, k:k + 1], None, ALU.mult)
                chain.link(e.reciprocal(inv_smooth[:, :], smooth[:, :]))
                chain.link(e.tensor_scalar(hln[:, 4:8], hln[:, 4:8], HD1**-0.5, None, ALU.mult))
                chain.link(e.tensor_copy(head_eps[:, 0:4], spread(wsc[:, 0:1], 4)))
                chain.link(e.tensor_copy(head_eps[:, 4:8], spread(wsc[:, 1:2], 4)))
                chain.link(e.tensor_copy(head_eps[:, 8:10], spread(wsc[:, 2:3], 2)))
                chain.link(e.memset(head_eps[:, 10:12], 1.0 / CTX_UP))
                chain.link(e.tensor_tensor(head_eps[:, :], head_eps[:, :], head_eps[:, :], ALU.mult))
                chain.link(e.reciprocal(head_eps[:, :], head_eps[:, :]))
                chain.link(e.tensor_scalar(head_eps[:, :], head_eps[:, :], EPS, None, ALU.mult))
                chain.link(e.tensor_scalar(sign[:, :], wsc[:, 0:3], 0.0, 2.0, ALU.is_ge, ALU.mult))
                chain.link(e.tensor_scalar(sign[:, :], sign[:, :], -1.0, None, ALU.add))
                chain.link(e.tensor_tensor(hln[:, 0:6:2], hln[:, 0:6:2], sign[:, :], ALU.mult))
                chain.link(e.tensor_tensor(out_gate[:, :], psc[:, :], wsc[:, 4:5], ALU.mult))
                chain.link(e.tensor_tensor(out_gate[:, :], out_gate[:, :], gates[:, 1:2], ALU.mult))

                def mean(n):
                    heads = work_items[n][1] // HD1
                    e.wait_ge(scaled, count(n, is_scaled))
                    m = head_sum[:, n % NWORK, 0:heads]
                    chain.link(e.tensor_reduce(m, source(n).rearrange("p (h d) -> p h d", h=heads), AX, ALU.add))
                    e.tensor_scalar(m, m, 1.0 / HD1, None, ALU.mult).then_inc(meant, 1)

                for n in range(-2, len(work_items)):
                    if n >= 0:
                        e.wait_ge(high, n + 1)
                        parts = work_items[n][2]
                        e.tensor_tensor(parts[1], like(source(n), parts[1]), parts[0], ALU.subtract).then_inc(low, 1)
                    if n + 2 < len(work_items) and is_centred(work_items[n + 2]):
                        mean(n + 2)
                chain.end()
                e.wait_ge(low, len(work_items))

    r = Pieces(nc)
    xq = sb("xq", [P, KD, 4, B * P], BF16)
    only_here = ExitStack()

    def rb(name, shape, dt=F32):
        return only_here.enter_context(nc.sbuf_tensor(name, shape, dt))

    stats, mv, rstd, spare = rb("stats_r", [P, 2, 6]), rb("mv_r", [P, 2, 2]), rb("rstd_r", [P, 2]), rb("spare_r", [P, 1])
    rows = rb("rows_n", [P, 2, D])
    wide, total = rb("wide_r", [P, 2, 8, P]), rb("total_r", [P, 2, 8, P])
    yb, ye = rb("yb", [P, 2, 8, P], BF16), rb("ye", [P, 2, 8, P], BF16)
    r_stat, r_rstd, r_n = r.flag("r_stat", "vector"), r.flag("r_rstd", "gpsimd"), r.flag("r_n", "vector")
    r_T, r_u = r.flag("r_T", "tensor", 1, 2), r.flag("r_u", "scalar", 1, 2)
    r_grid, r_add = r.flag("r_grid", "vector", 1, 2), r.flag("r_add", "gpsimd")
    c_r1, c_r1g, c_r3 = Chain(nc, "c_r1", 1), Chain(nc, "c_r1g", 2), Chain(nc, "c_r3", 2)

    def float8_grid(e, chain, y32, b16, e16):
        chain.link(e.tensor_scalar(b16, y32, F8_MAX, -F8_MAX, ALU.min, ALU.max))
        chain.link(e.tensor_scalar(e16.bitcast(U16), b16.bitcast(U16), EXPONENT, None, ALU.bitwise_and))
        return e.tensor_scalar(e16, e16, F8_TINY, F8_SHIFT, ALU.max, ALU.mult)

    @r.piece("1", "vector")
    def _(e, n, b):
        i = 2 * n + b
        c_r1.start(e, i)
        c_r1.link(e.bn_stats(stats[:, b, :], x[:, i, :]))
        e.memset(spare[:, :], 0.0)
        e.bn_aggr(mv[:, b, :], stats[:, b, :]).then_inc(r_stat.sem, 1)
        c_r1.end()

    @r.piece("1", "gpsimd")
    def _(e, n, b):
        i = 2 * n + b
        c_r1g.start(e, i)
        e.wait_ge(r_stat.sem, r_stat.at(i))
        c_r1g.link(e.tensor_tensor(rstd[:, b:b + 1], mv[:, b, 1:2], t["one_eps"][:, 0:1], ALU.mult))
        c_r1g.link(e.tensor_tensor(rstd[:, b:b + 1], rstd[:, b:b + 1], t["eps_eps"][:, 0:1], ALU.add))
        e.tensor_tensor(rstd[:, b:b + 1], rstd[:, b:b + 1], t["half"][:, 0:1], ALU.pow).then_inc(r_rstd.sem, 1)
        c_r1g.end()

    @r.piece("2", "vector")
    def _(e, n, b):
        i = 2 * n + b
        e.wait_ge(r_rstd.sem, r_rstd.at(i))
        e.wait_ge(r_T.sem, r_T.at(i - 2))
        e.tensor_scalar(rows[:, b, :], x[:, i, :], mv[:, b, 0:1], rstd[:, b:b + 1], ALU.subtract,
                        ALU.mult).then_inc(r_n.sem, 1)

    @r.piece("2", "tensor")
    def _(e, n, b):
        i = 2 * n + b
        e.wait_ge(r_n.sem, r_n.at(i))
        e.wait_ge(r_u.sem, r_u.at(i - 2))
        for k in range(KD):
            last = e.transpose(bank[b][:, k * P:(k + 1) * P], rows[:, b, k * P:(k + 1) * P], ident[:, :])
        last.then_inc(r_T.sem, 1)

    @r.piece("2", "scalar")
    def _(e, n, b):
        i = 2 * n + b
        e.wait_ge(r_T.sem, r_T.at(i))
        e.wait_ge(r_grid.sem, r_grid.at(i - 2))
        for k in range(KD):
            for c in range(4):
                last = e.activation(wide[:, b, 4 * k + c, :], bank[b][:, k * P:(k + 1) * P], ACT.Identity,
                                    bias=row_b[:, k, c:c + 1], scale=row_w[:, k, c:c + 1])
        last.then_inc(r_u.sem, 1)

    @r.piece("3", "vector")
    def _(e, n, b):
        i = 2 * n + b
        c_r3.start(e, i)
        e.wait_ge(r_u.sem, r_u.at(i))
        float8_grid(e, c_r3, wide[:, b, :, :], yb[:, b, :, :], ye[:, b, :, :]).then_inc(r_grid.sem, 1)
        c_r3.end()

    @r.piece("3A", "gpsimd")
    def _(e, n, b):
        i = 2 * n + b
        e.wait_ge(r_grid.sem, r_grid.at(i))
        e.tensor_tensor(total[:, b, :, :], yb[:, b, :, :], ye[:, b, :, :], ALU.add).then_inc(r_add.sem, 1)

    @r.piece("3S", "vector")
    def _(e, n, b):
        i = 2 * n + b
        e.wait_ge(r_add.sem, r_add.at(i))
        e.tensor_tensor(xq[:, :, :, bass.ds(i * P, P)].rearrange("p k s t -> p (k s) t"), total[:, b, :, :],
                        ye[:, b, :, :], ALU.subtract)

    rows_order = order("2:1 1:0+ 3:0 3A:0 3S:1- 2:0+ 1:1+ 3:1 3A:1 3S:0")

    def rows_body(owner, n, nxt=True, prev=True):
        return [(name, n + shift, item) for name, shift, item in rows_order
                if shift == 0 or (nxt if shift == 1 else prev)]

    with nc.Block() as block:
        last = B // 2 - 1
        r.run(block, lambda owner: order("1:0 1:1 2:0") + rows_body(owner, 0, prev=False), rows_body,
              lambda owner: rows_body(owner, last, nxt=False) + [("3S", last, 1)], (1, last))
    only_here.close()

    s = Pieces(nc)
    A, S, O = bank[0:4], bank[4:6], bank[6:8]
    squares, hss, hr = sb("squares", [P, 12, HD1], BF16), sb("head_squares", [P, 12]), sb("head_rstd", [P, 12])
    hn = sb("heads_n", [P, 3, 4, HD1])
    hT = sb("headsT", [P, 3, 4, P])
    v = sb("v1", [P, 2, 2, HD1])
    nmax, rowsum, rinv = sb("nmax1", [P, 2, 4]), sb("rowsum1", [P, 2, 4]), sb("rinv1", [P, 2, 4])
    prob, probT = sb("prob1", [P, 2, 4, P]), sb("probT1", [P, 2, 4, P])
    wide2, cb, ce = sb("wide2", [P, 8, P]), sb("cb", [P, 8, P], BF16), sb("ce", [P, 8, P], BF16)
    total2 = sb("total2", [P, 8, P])
    catq = sb("catq", [P, 8, P], BF16)
    sig = s.flag
    pe_A, a_st, g_r = sig("pe_A", "tensor", 4), sig("a_st", "scalar", 3), sig("g_r", "gpsimd", 3)
    v_n, pe_hT = sig("v_n", "vector", 3), sig("pe_headsT", "tensor", 3)
    a_hT, a_v = sig("a_headsT", "scalar", 3), sig("a_v", "scalar")
    pe_S, v_mx, a_ex = sig("pe_S1", "tensor", 2), sig("v_mx1", "vector", 2), sig("a_ex1", "scalar", 2)
    v_iv, g_p = sig("v_iv1", "vector", 2), sig("g_p1", "gpsimd", 2)
    pe_PT, v_PT = sig("pe_PT1", "tensor", 2), sig("v_PT1", "vector", 2)
    v_qm = sig("v_qm", "vector", 2)
    v_grid, g_add = sig("v_grid", "vector"), sig("g_add", "gpsimd")
    pe_O, v_q, pe_out, v_x = sig("pe_O1", "tensor", 2), sig("v_catq", "vector"), sig("pe_out", "tensor"), sig("v_x3", "vector")

    @s.piece("A", "tensor")
    def _(e, i, n):
        rows_at, w_at = bass.ds((i // J) * P, P), (i % J) * W1

        def project(out, which, c0, n):
            for k in range(KD):
                for hl in range(2):
                    last = e.matmul(out, xq[:, k, which, rows_at], wb[:, k, hl, bass.ds(w_at + c0, n)],
                                    start=(k == 0 and hl == 0), stop=(k == KD - 1 and hl == 1))
            return last

        def project_context(out, c0, n):
            for k in range(KD):
                for part, hl in ((0, 0), (0, 1), (1, 0)):
                    last = e.matmul(out, cx[:, k, part, rows_at], wb[:, k, hl, bass.ds(w_at + c0, n)],
                                    start=(k == 0 and part == hl == 0), stop=(k == KD - 1 and part == 1))
            return last

        if n < 3:
            e.wait_ge(a_hT.sem, a_hT.at(i - 1, n + 1))
        else:
            e.wait_ge(a_v.sem, a_v.at(i - 1))
        if n < 2:
            project(A[n][:, :], n, (Q_, QX_)[n], 512).then_inc(pe_A.sem, 1)
        else:
            project(A[n][:, 0:256], n, (K_, V_)[n - 2], 256)
            project_context(A[n][:, 256:512], (KX_, VX_)[n - 2], 256).then_inc(pe_A.sem, 1)

    @s.piece("ST", "scalar")
    def _(e, i, n):
        e.wait_ge(pe_A.sem, pe_A.at(i, n + 1))
        for h in range(4):
            last = e.activation(squares[:, 4 * n + h, :], A[n][:, h * HD1:(h + 1) * HD1], ACT.Square, scale=HD1**-0.5,
                                accum_out=hss[:, 4 * n + h:4 * n + h + 1])
        last.then_inc(a_st.sem, 1)

    c_su = [Chain(nc, f"c_su{n}", 1) for n in range(3)]

    @s.piece("SU", "gpsimd")
    def _(e, i, n):
        c_su[n].start(e, i)
        four = slice(4 * n, 4 * n + 4)
        e.wait_ge(a_st.sem, a_st.at(i, n + 1))
        c_su[n].link(e.tensor_tensor(hr[:, four], hss[:, four], head_eps[:, four], ALU.add))
        e.tensor_tensor(hr[:, four], hr[:, four], t["half"][:, four], ALU.pow).then_inc(g_r.sem, 1)
        c_su[n].end()

    @s.piece("N", "vector")
    def _(e, i, n):
        e.wait_ge(g_r.sem, g_r.at(i, n + 1))
        e.tensor_tensor(hn[:, n, :, :], A[n][:, :].rearrange("p (h d) -> p h d", h=4),
                        spread(hr[:, 4 * n:4 * n + 4], HD1), ALU.mult).then_inc(v_n.sem, 1)

    @s.piece("TQ", "tensor")
    def _(e, i, n):
        e.wait_ge(v_n.sem, v_n.at(i, n + 1))
        for h in range(4):
            last = e.transpose(A[n][:, h * P:(h + 1) * P], hn[:, n, h, :], ident[:, :])
        last.then_inc(pe_hT.sem, 1)

    @s.piece("TQ", "scalar")
    def _(e, i, n):
        e.wait_ge(pe_hT.sem, pe_hT.at(i, n + 1))
        for h0, h1, c in (((0, 4, 0),), ((0, 4, 2),), ((0, 2, 4), (2, 4, 6)))[n]:
            last = e.activation(hT[:, n, h0:h1, :].rearrange("p h t -> p (h t)"), A[n][:, h0 * P:h1 * P],
                                ACT.Identity, bias=hln[:, c + 1:c + 2], scale=hln[:, c:c + 1])
        last.then_inc(a_hT.sem, 1)

    @s.piece("VE", "scalar")
    def _(e, i):
        e.wait_ge(pe_A.sem, pe_A.at(i))
        e.wait_ge(pe_O.sem, pe_O.at(i - 1))
        e.activation(v[:, 0, :, :].rearrange("p h d -> p (h d)"), A[3][:, 0:256], ACT.Copy, scale=wsc[:, 3:4])
        e.activation(v[:, 1, :, :].rearrange("p h d -> p (h d)"), A[3][:, 256:512], ACT.Copy,
                     scale=1.0 / CTX_UP).then_inc(a_v.sem, 1)

    @s.piece("SC", "tensor")
    def _(e, i, kind):
        e.wait_ge(a_hT.sem, a_hT.at(i))
        e.wait_ge(v_PT.sem, v_PT.at(i - 1, kind + 1))
        for h in range(4):
            last = e.matmul(S[kind][:, h * P:(h + 1) * P], hT[:, kind, h, :], hT[:, 2, 2 * kind + h // 2, :],
                            start=True, stop=True)
        last.then_inc(pe_S.sem, 1)

    @s.piece("SC", "vector")
    def _(e, i, kind):
        e.wait_ge(pe_S.sem, pe_S.at(i, kind + 1))
        e.tensor_reduce(nmax[:, kind, :], S[kind][:, :].rearrange("p (h t) -> p h t", h=4), AX, ALU.max,
                        negate=True).then_inc(v_mx.sem, 1)

    @s.piece("SC", "scalar")
    def _(e, i, kind):
        e.wait_ge(v_mx.sem, v_mx.at(i, kind + 1))
        for h in range(4):
            last = e.activation(prob[:, kind, h, :], S[kind][:, h * P:(h + 1) * P], ACT.Exp,
                                bias=nmax[:, kind, h:h + 1], accum_out=rowsum[:, kind, h:h + 1])
        last.then_inc(a_ex.sem, 1)

    @s.piece("R", "vector")
    def _(e, i, kind):
        e.wait_ge(a_ex.sem, a_ex.at(i, kind + 1))
        e.reciprocal(rinv[:, kind, :], rowsum[:, kind, :]).then_inc(v_iv.sem, 1)

    @s.piece("R", "gpsimd")
    def _(e, i, kind):
        e.wait_ge(v_iv.sem, v_iv.at(i, kind + 1))
        e.tensor_tensor(prob[:, kind, :, :], prob[:, kind, :, :], spread(rinv[:, kind, :], P),
                        ALU.mult).then_inc(g_p.sem, 1)

    @s.piece("PT", "tensor")
    def _(e, i, kind):
        e.wait_ge(g_p.sem, g_p.at(i, kind + 1))
        for h in range(4):
            last = e.transpose(S[kind][:, h * P:(h + 1) * P], prob[:, kind, h, :], ident[:, :])
        last.then_inc(pe_PT.sem, 1)

    @s.piece("PT", "vector")
    def _(e, i, kind):
        e.wait_ge(pe_PT.sem, pe_PT.at(i, kind + 1))
        e.tensor_copy(probT[:, kind, :, :].rearrange("p h t -> p (h t)"), S[kind][:, :]).then_inc(v_PT.sem, 1)

    @s.piece("PV", "tensor")
    def _(e, i, kind):
        e.wait_ge(a_v.sem, a_v.at(i))
        if kind == 1:
            e.wait_ge(v_x.sem, v_x.at(i - 1))
        e.wait_ge(v_PT.sem, v_PT.at(i, kind + 1))
        for g in range(2):
            last = e.matmul(O[kind][:, g * 2 * P:(g + 1) * 2 * P], v[:, kind, g, :],
                            probT[:, kind, 2 * g:2 * g + 2, :], start=True, stop=True)
        last.then_inc(pe_O.sem, 1)

    c_q = Chain(nc, "c_q", 2)

    @s.piece("QM", "vector")
    def _(e, i, kind):
        e.wait_ge(pe_O.sem, pe_O.at(i, kind + 1))
        e.tensor_tensor(wide2[:, 4 * kind:4 * kind + 4, :], O[kind][:, :].rearrange("p (h t) -> p h t", h=4),
                        spread(inv_smooth[:, bass.ds((i % J) * 4 + 16 * kind, 4)], P), ALU.mult).then_inc(v_qm.sem, 1)

    @s.piece("Q", "vector")
    def _(e, i):
        c_q.start(e, i)
        e.wait_ge(v_qm.sem, v_qm.at(i))
        float8_grid(e, c_q, wide2[:, :, :], cb[:, :, :], ce[:, :, :]).then_inc(v_grid.sem, 1)
        c_q.end()

    @s.piece("QA", "gpsimd")
    def _(e, i):
        e.wait_ge(v_grid.sem, v_grid.at(i))
        e.tensor_tensor(total2[:, :, :], cb[:, :, :], ce[:, :, :], ALU.add).then_inc(g_add.sem, 1)

    @s.piece("QS", "vector")
    def _(e, i):
        e.wait_ge(g_add.sem, g_add.at(i))
        e.tensor_tensor(catq[:, :, :], total2[:, :, :], ce[:, :, :], ALU.subtract).then_inc(v_q.sem, 1)

    @s.piece("O", "tensor")
    def _(e, i):
        e.wait_ge(v_q.sem, v_q.at(i))
        n = 0
        for kind in range(2):
            for h in range(4):
                for hl in range(2):
                    w = wp[:, hl, bass.ds((i % J) * 4 + 16 * kind + h, 1), :].rearrange("p h o -> p (h o)")
                    last = e.matmul(O[1][:, 0:D], catq[:, 4 * kind + h, :], w, start=(n == 0), stop=(n == 15))
                    n += 1
        last.then_inc(pe_out.sem, 1)

    @s.piece("O", "vector")
    def _(e, i):
        e.wait_ge(pe_out.sem, pe_out.at(i))
        row = x[:, bass.ds(i // J, 1), :].rearrange("p b d -> p (b d)")
        e.scalar_tensor_tensor(row, O[1][:, 0:D], out_gate[:, 0:1], row, ALU.mult, ALU.add).then_inc(v_x.sem, 1)

    N = B * J
    with nc.Block() as block:
        s.run_pipelined(block, lambda owner: order(ORDER1[owner]), N, 1, 2)



NE = 8
W_UP = 64.0
GROUP = 4
GT = GROUP * P


def layer1_experts(nc, a, t, ctx):
    def sb(name, shape, dt=F32):
        return ctx.enter_context(nc.sbuf_tensor(name, shape, dt))

    x, gates, ident = t["x"], t["gates"], t["ident"]
    bank = [ctx.enter_context(nc.psum_tensor(f"ps2_{n}", [P, 512], F32)) for n in range(8)]
    win = sb("w_in", [P, 2, NE, KD, FF], F16)
    wout = sb("w_out", [P, 2, NE, KF, D], F16)
    wr = sb("w_router", [P, KD, NE])
    rT = sb("rowsT", [P, KD, 2, B * P], F16)
    gate = sb("gate", [P, B, NE])
    order = sb("order", [P, NE])
    top = sb("top", [P, 8])

    got, used, small, made = (nc.alloc_semaphore(n) for n in ("w2_got", "w2_used", "w2_small", "w2_made"))
    with nc.sbuf_tensor("raw2", [P, 2, 2048], F32) as raw, nc.sbuf_tensor("work2", [P, 2, 2048], F32) as work:
        items = [(k, n) for k in ("winT", "woutT") for n in range(4)]
        with nc.Block() as block:
            @block.sync
            def _(e):
                e.dma_start(wr[:, :, :], a["WrT"].rearrange("(k p) n -> p k n", p=P)).then_inc(small, 16)
                for n, (name, q) in enumerate(items):
                    if n >= 2:
                        e.wait_ge(used, n - 1)
                    src = a[name].rearrange("e (k p) n -> p e k n", p=P)[:, 2 * q:2 * q + 2]
                    for h in range(2):
                        e.dma_start(raw[:, n % 2, h * 1024:(h + 1) * 1024].rearrange("p (k n) -> p k n", k=src.shape[2]),
                                    src[:, h]).then_inc(got, 16)
                    e.wait_ge(got, 32 * (n + 1))
                e.wait_ge(small, 16)

            @block.gpsimd
            def _(e):
                for n in range(NE):
                    e.memset(order[:, n:n + 1], float(n))
                e.memset(top[:, :], 0.0).then_inc(made, 1)

            @block.vector
            def _(e):
                chain = Chain(nc, "w2_chain", 2 * len(items))
                chain.start(e, 0)
                for n, (name, q) in enumerate(items):
                    w = (win if name == "winT" else wout)
                    e.wait_ge(got, 32 * (n + 1))
                    if n >= 2:
                        e.wait_ge(used, n - 1)
                    chain.link(e.tensor_scalar(work[:, n % 2, :], raw[:, n % 2, :], W_UP, None, ALU.mult))
                    parts = split(e, *(w[:, hl, 2 * q:2 * q + 2, :, :].rearrange("p e k n -> p (e k n)") for hl in range(2)),
                                  work[:, n % 2, :])
                    chain.link(next(parts))
                    next(parts).then_inc(used, 1)
                chain.end()
                e.drain()

    r = Pieces(nc)
    stats, mv, rstd, spare = sb("stats_m", [P, 2, 6]), sb("mv_m", [P, 2, 2]), sb("rstd_m", [P, 2]), sb("spare_m", [P, 1])
    rows, u = sb("rows_m", [P, 2, D]), sb("rowsT32", [P, 2, KD, P])
    logit, best, found = sb("logit", [P, 2, NE]), sb("best", [P, 2, 8]), sb("found", [P, 2, 8], U32)
    foundf, soft, pick = sb("foundf", [P, 2, 8]), sb("soft", [P, 2, 4]), sb("picked", [P, 2, 2, NE])
    r_stat, r_rstd, r_n = r.flag("m_stat", "vector"), r.flag("m_rstd", "gpsimd"), r.flag("m_n", "vector")
    r_T, r_u, r_hi = r.flag("m_T", "tensor"), r.flag("m_u", "scalar"), r.flag("m_hi", "scalar")
    r_lo, r_lg, r_d = r.flag("m_lo", "vector"), r.flag("m_lg", "tensor"), r.flag("m_d", "vector")
    r_e = r.flag("m_e", "scalar")
    c_1, c_1g, c_3 = Chain(nc, "c_m1", 1), Chain(nc, "c_m1g", 1), Chain(nc, "c_m3", 8)

    @r.piece("1", "vector")
    def _(e, i, b):
        c_1.start(e, i)
        c_1.link(e.bn_stats(stats[:, b, :], x[:, i, :]))
        e.memset(spare[:, :], 0.0)
        e.bn_aggr(mv[:, b, :], stats[:, b, :]).then_inc(r_stat.sem, 1)
        c_1.end()

    @r.piece("1", "gpsimd")
    def _(e, i, b):
        c_1g.start(e, i)
        e.wait_ge(r_stat.sem, r_stat.at(i))
        c_1g.link(e.tensor_tensor(rstd[:, b:b + 1], mv[:, b, 1:2], t["eps"][:, 0:1], ALU.add))
        e.tensor_tensor(rstd[:, b:b + 1], rstd[:, b:b + 1], t["half"][:, 0:1], ALU.pow).then_inc(r_rstd.sem, 1)
        c_1g.end()

    @r.piece("2", "vector")
    def _(e, i, b):
        e.wait_ge(r_rstd.sem, r_rstd.at(i))
        e.wait_ge(r_T.sem, r_T.at(i - 1))
        e.tensor_scalar(rows[:, b, :], x[:, i, :], mv[:, b, 0:1], rstd[:, b:b + 1], ALU.subtract,
                        ALU.mult).then_inc(r_n.sem, 1)

    @r.piece("2", "tensor")
    def _(e, i, b):
        e.wait_ge(r_n.sem, r_n.at(i))
        e.wait_ge(r_hi.sem, r_hi.at(i - 1))
        for k in range(KD):
            last = e.transpose(bank[0][:, k * P:(k + 1) * P], rows[:, b, k * P:(k + 1) * P], ident[:, :])
        last.then_inc(r_T.sem, 1)

    @r.piece("2", "scalar")
    def _(e, i, b):
        e.wait_ge(r_T.sem, r_T.at(i))
        e.wait_ge(r_lg.sem, r_lg.at(i - 1))
        e.wait_ge(r_lo.sem, r_lo.at(i - 1))
        at = bass.ds(i * P, P)
        src = bank[0][:, 0:D].rearrange("p (k t) -> p k t", k=KD)
        e.activation(u[:, b, :, :], src, ACT.Copy).then_inc(r_u.sem, 1)
        e.activation(rT[:, :, 0, at], src, ACT.Copy).then_inc(r_hi.sem, 1)

    @r.piece("2b", "tensor")
    def _(e, i, b):
        e.wait_ge(r_u.sem, r_u.at(i))
        e.wait_ge(r_d.sem, r_d.at(i - 1))
        for k in range(KD):
            last = e.matmul(bank[1][:, 0:NE], u[:, b, k, :], wr[:, k, :], start=(k == 0), stop=(k == KD - 1))
        last.then_inc(r_lg.sem, 1)

    @r.piece("3", "vector")
    def _(e, i, b):
        c_3.start(e, i)
        at = bass.ds(i * P, P)
        e.wait_ge(r_hi.sem, r_hi.at(i))
        e.tensor_tensor(rT[:, :, 1, at], u[:, b, :, :], rT[:, :, 0, at], ALU.subtract).then_inc(r_lo.sem, 1)
        e.wait_ge(r_lg.sem, r_lg.at(i))
        c_3.link(e.tensor_copy(logit[:, b, :], bank[1][:, 0:NE]))
        e.memset(spare[:, :], 0.0)
        c_3.link(e.max(best[:, b, :], logit[:, b, :]))
        e.memset(spare[:, :], 0.0)
        c_3.link(e.max_index(found[:, b, :], best[:, b, :], logit[:, b, :]))
        e.tensor_copy(foundf[:, b, :], found[:, b, :])
        e.tensor_tensor(soft[:, b, 0:1], best[:, b, 1:2], best[:, b, 0:1], ALU.subtract).then_inc(r_d.sem, 1)
        e.wait_ge(r_e.sem, r_e.at(i))
        c_3.link(e.tensor_scalar(soft[:, b, 2:3], soft[:, b, 1:2], 1.0, None, ALU.add))
        c_3.link(e.reciprocal(soft[:, b, 2:3], soft[:, b, 2:3]))
        c_3.link(e.tensor_tensor(soft[:, b, 3:4], soft[:, b, 1:2], soft[:, b, 2:3], ALU.mult))
        for n in range(2):
            m = e.tensor_scalar(pick[:, b, n, :], order[:, :], foundf[:, b, n:n + 1], soft[:, b, 2 + n:3 + n],
                                ALU.is_equal, ALU.mult)
        c_3.link(m)
        c_3.link(e.tensor_tensor(pick[:, b, 0, :], pick[:, b, 0, :], pick[:, b, 1, :], ALU.add))
        e.tensor_scalar(gate[:, i, :], pick[:, b, 0, :], gates[:, 3:4], 1.0 / W_UP, ALU.mult, ALU.mult)
        c_3.end()

    @r.piece("3", "scalar")
    def _(e, i, b):
        e.wait_ge(r_d.sem, r_d.at(i))
        e.activation(soft[:, b, 1:2], soft[:, b, 0:1], ACT.Exp).then_inc(r_e.sem, 1)

    with nc.Block() as block:
        two = lambda n: [("1", 2 * n, 0), ("1", 2 * n + 1, 1), ("2", 2 * n, 0), ("2b", 2 * n, 0),
                         ("2", 2 * n + 1, 1), ("3", 2 * n, 0), ("2b", 2 * n + 1, 1), ("3", 2 * n + 1, 1)]
        r.run_alike(block, [], two, [], (0, B // 2))

    s = Pieces(nc)
    Hb, Y = bank[0:4], bank[4:8]
    h32 = sb("h32", [P, KF, GT])
    hh = sb("hidden", [P, 2, 2, KF, GT], F16)
    pe_H, a_h, v_hi, v_lo = (s.flag("pe_H", "tensor", KF), s.flag("a_h", "scalar", KF),
                             s.flag("v_hi", "vector", KF), s.flag("v_lo", "vector", KF))
    pe_Y, v_Y = s.flag("pe_Y", "tensor", GROUP, 2), s.flag("v_Y", "vector", GROUP)

    @s.piece("H", "tensor")
    def _(e, i, b):
        rows_at = bass.ds((i // NE) * GT, GT)
        for m in range(KF):
            e.wait_ge(a_h.sem, a_h.at(i - 1, m + 1))
            for k in range(KD):
                for part, hl in ((0, 0), (0, 1), (1, 0)):
                    w = win[:, hl, bass.ds(i % NE, 1), k, m * P:(m + 1) * P].rearrange("p e n -> p (e n)")
                    last = e.matmul(Hb[m][:, :], w, rT[:, k, part, rows_at], start=(k == 0 and part == hl == 0),
                                    stop=(k == KD - 1 and part == 1))
            last.then_inc(pe_H.sem, 1)

    @s.piece("H", "scalar")
    def _(e, i, b):
        for m in range(KF):
            e.wait_ge(pe_H.sem, pe_H.at(i, m + 1))
            e.wait_ge(v_lo.sem, v_lo.at(i - 1, m + 1))
            e.activation(h32[:, m, :], Hb[m][:, :], ACT.Silu, scale=1.0 / W_UP).then_inc(a_h.sem, 1)

    @s.piece("H", "vector")
    def _(e, i, b):
        e.wait_ge(pe_Y.sem, pe_Y.at(i - 2))
        for m in range(KF):
            e.wait_ge(a_h.sem, a_h.at(i, m + 1))
            e.tensor_copy(hh[:, b, 0, m, :], h32[:, m, :]).then_inc(v_hi.sem, 1)
            e.wait_ge(v_hi.sem, v_hi.at(i, m + 1))
            e.tensor_tensor(hh[:, b, 1, m, :], h32[:, m, :], hh[:, b, 0, m, :], ALU.subtract).then_inc(v_lo.sem, 1)

    @s.piece("Y", "tensor")
    def _(e, i, b):
        for q in range(GROUP):
            e.wait_ge(v_Y.sem, v_Y.at(i - 1, q + 1))
            for m in range(KF):
                if q == 0:
                    e.wait_ge(v_lo.sem, v_lo.at(i, m + 1))
                for part, hl in ((0, 0), (0, 1), (1, 0)):
                    w = wout[:, hl, bass.ds(i % NE, 1), m, :].rearrange("p e n -> p (e n)")
                    last = e.matmul(Y[q][:, 0:D], hh[:, b, part, m, q * P:(q + 1) * P], w,
                                    start=(m == 0 and part == hl == 0), stop=(m == KF - 1 and part == 1))
            last.then_inc(pe_Y.sem, 1)

    @s.piece("Y", "vector")
    def _(e, i, b):
        for q in range(GROUP):
            e.wait_ge(pe_Y.sem, pe_Y.at(i, q + 1))
            at = (i // NE) * GROUP + q
            row = x[:, bass.ds(at, 1), :].rearrange("p b d -> p (b d)")
            g = gate[:, bass.ds(at, 1), bass.ds(i % NE, 1)].rearrange("p b e -> p (b e)")
            e.scalar_tensor_tensor(row, Y[q][:, 0:D], g, row, ALU.mult, ALU.add).then_inc(v_Y.sem, 1)

    N = NE * B // GROUP

    def pair(n):
        return [("H", 2 * n + 1, 1), ("Y", 2 * n, 0), ("H", 2 * n + 2, 0), ("Y", 2 * n + 1, 1)]

    with nc.Block() as block:
        s.run_alike(block, [("H", 0, 0)], pair, [("H", N - 1, 1), ("Y", N - 2, 0), ("Y", N - 1, 1)], (0, N // 2 - 1))


def store_rows(nc, t, out):
    done = nc.alloc_semaphore("stored")
    with nc.Block() as block:
        @block.sync
        def _(e):
            e.dma_start(out.rearrange("b p d -> p b d"), t["x"][:, :, :]).then_inc(done, 16)
            e.wait_ge(done, 16)


def program(nc, a, out, phases):
    t = prepare_common(nc, a)
    with ExitStack() as ctx:
        if phases[0]:
            layer0(nc, a, t, ctx)
    with ExitStack() as ctx:
        if phases[1]:
            layer1_attention(nc, a, t, ctx)
    with ExitStack() as ctx:
        if phases[2]:
            layer1_experts(nc, a, t, ctx)
    store_rows(nc, t, out)




def hadamard(n):
    h = np.ones((1, 1), np.float32)
    while h.shape[0] < n:
        h = np.block([[h, h], [h, -h]])
    return np.ascontiguousarray(h, np.float32)


def lay_out(v):
    a = {}
    a["x"] = v["x"]
    a["ctxT"] = v["ctx_2048"].reshape(B * P, D).T
    a["g_xattn"], a["g_ffn"] = v["g_xattn"], v["g_ffn"]
    a["causal"] = v["mask_SxS2_bc0"]
    a["padding"] = v["mask_BxS2_bk0"]
    a["WqT"] = v["L0_xattn_Wq"].T
    a["bq"] = v["L0_xattn_bq"].reshape(KD, P).T
    wk = np.broadcast_to(v["L0_xattn_Wk"].reshape(G0, 1, HD0, D), (G0, R0, HD0, D))
    a["WkT"] = wk.reshape(G0 * R0 * HD0, D).T
    bk = np.broadcast_to(v["L0_xattn_bk"].reshape(G0, 1, HD0), (G0, R0, HD0))
    a["bk"] = bk.reshape(KD, P).T
    a["WvT"] = v["L0_xattn_Wv"].T
    a["bv"] = v["L0_xattn_bv"]
    a["bo"] = v["L0_xattn_bo"]
    wo = v["L0_xattn_Wo"].reshape(D, 2, 4, 1, R0, HD0).transpose(1, 2, 3, 5, 4, 0)
    a["WoT"] = np.broadcast_to(wo, (2, 4, 4, HD0, R0, D)).reshape(2, P, R0, D)
    a["w_upT"] = v["L0_ffn_w_up"].T
    a["w_downT"] = v["L0_ffn_w_down"].T
    a["had256"], a["had128"] = hadamard(D), hadamard(P)
    rows = np.arange(P)
    a["low_row"] = -(rows[:, None] % GP >= GP // 2).astype(np.float32)
    a["high_row"] = (rows[:, None] % GP < GP // 2).astype(np.float32)
    a["pick"] = ((rows[:, None] // HD0) % R0 == np.arange(R0)[None, :]).astype(np.float32)
    a["in_scales"] = np.stack([v[f"L1_xattn_{n}_in_scale"] for n in ("q", "qx", "k", "v")], axis=1)
    a["ln_w"], a["ln_b"] = v["L1_xattn_ln_w"].reshape(KD, P).T, v["L1_xattn_ln_b"].reshape(KD, P).T
    a["w_scales"] = np.stack([v[f"L1_xattn_{n}_scale"] for n in ("wq", "wqx", "wk", "wv", "proj_w")])
    a["proj_in_scale"] = v["L1_xattn_proj_in_scale"].reshape(1)
    a["head_ln"] = np.stack([v[f"L1_xattn_{n}ln_{c}"] for n in ("q", "qx", "k", "kx") for c in "wb"], axis=1)
    a["smooth"] = v["L1_xattn_proj_smooth"].reshape(32, P).T
    for n in ("wq", "wqx", "wk", "wv"):
        a[n + "T"] = v["L1_xattn_" + n].T
    a["wkxT"], a["wvxT"] = v["L1_xattn_w_kv_x"][:G1 * HD1].T, v["L1_xattn_w_kv_x"][G1 * HD1:].T
    a["WrT"] = v["L1_ffn_Wr"].T
    a["winT"], a["woutT"] = v["L1_ffn_Win"].transpose(0, 2, 1), v["L1_ffn_Wout"].transpose(0, 2, 1)
    a["wprojT"] = v["L1_xattn_wproj"].T
    return {k: np.ascontiguousarray(x) for k, x in a.items()}


PHASES = (1, 1, 1)


def kernel(**inputs):
    import concourse.bacc as bacc
    from concourse.bass_utils import run_bass_kernel_spmd

    nc = bacc.Bacc("TRN2", target_bir_lowering=False, num_devices=1)
    arrays = {f"in_{k}": x for k, x in lay_out(inputs).items()}
    aps = {k[3:]: nc.dram_tensor(k, x.shape, mybir.dt.from_np(x.dtype), kind="ExternalInput").ap()
           for k, x in arrays.items()}
    out = nc.dram_tensor("out_0", (B, P, D), F32, kind="ExternalOutput").ap()
    program(nc, aps, out, PHASES)
    r = run_bass_kernel_spmd(nc, [arrays], core_ids=[0])
    return r.results[0]["out_0"]
```

```python
from contextlib import ExitStack

import numpy as np

import concourse.bass as bass
from concourse import mybir
from concourse.alu_op_type import AluOpType as ALU

ACT = mybir.ActivationFunctionType
AX = mybir.AxisListType.X
F32 = mybir.dt.float32
F16 = mybir.dt.float16
BF16 = mybir.dt.bfloat16
U16 = mybir.dt.uint16
U8 = mybir.dt.uint8

P = 128
B = 16
D = 256
KD = D // P
EPS = 1e-5
MAGIC = 1.5 * 2.0**23
MASKED = -1.0e30


class Flag:

    def __init__(self, nc, name, per=1, lead=1):
        self.sem, self.per, self.lead = nc.alloc_semaphore(name), per, lead

    def prime(self, engine):
        engine.sem_inc(self.sem, self.per * self.lead)

    def at(self, i, k=None):
        return (i + self.lead) * self.per + (self.per if k is None else k)


class Chain:

    def __init__(self, nc, name, per):
        self.sem, self.per, self.name = nc.alloc_semaphore(name), per, name

    def start(self, engine, i):
        self.engine, self.i, self.n = engine, i, 0

    def link(self, instruction):
        instruction.then_inc(self.sem, 1)
        self.n += 1
        self.engine.wait_ge(self.sem, self.i * self.per + self.n)

    def end(self):
        assert self.n == self.per, f"chain {self.name}: {self.n} links"


class Pieces:

    def __init__(self, nc):
        self.nc, self.flags, self.pieces = nc, {}, {}

    def flag(self, name, owner, per=1, lead=1):
        s = Flag(self.nc, name, per, lead)
        self.flags.setdefault(owner, []).append(s)
        return s

    def piece(self, name, engine):
        def keep(f):
            self.pieces[(name, engine)] = f
            return f
        return keep

    def run(self, block, before, body, after, loop):
        for owner, hook in (("tensor", block.tensor), ("vector", block.vector), ("scalar", block.scalar),
                            ("gpsimd", block.gpsimd), ("sync", block.sync)):
            self.program(owner, hook, before, body, after, loop)

    def run_pipelined(self, block, orders, count, ahead, behind):
        def at(owner, i):
            return [(name, i + shift, *item) for name, shift, *item in orders(owner)]

        def some(owner, runs):
            return [step for i in runs for step in at(owner, i) if 0 <= step[1] < count]

        self.run(block, lambda owner: some(owner, range(-ahead, behind)), at,
                 lambda owner: some(owner, range(count - ahead, count + behind)), (behind, count - ahead))

    def run_alike(self, block, before, body, after, loop):
        self.run(block, lambda owner: before, lambda owner, i: body(i), lambda owner: after, loop)

    def program(self, owner, hook, before, body, after, loop):
        @hook
        def _(e):
            def emit(steps):
                for name, i, *more in steps:
                    if (name, owner) in self.pieces:
                        self.pieces[(name, owner)](e, i, *more)
            for s in self.flags.get(owner, []):
                s.prime(e)
            emit(before(owner))
            if loop[1] > loop[0]:
                with e.Fori(*loop) as i:
                    emit(body(owner, i))
            emit(after(owner))


def order(text):
    steps = []
    for word in text.split():
        shift = word.count("+") - word.count("-")
        word = word.rstrip("+-")
        name, _, item = word.partition(":")
        steps.append((name, shift) + ((int(item),) if item else ()))
    return steps


def spread(ap, n):
    return ap.unsqueeze(2).to_broadcast([ap.shape[0], ap.shape[1], n])


def tiled(ap, n):
    return ap.unsqueeze(1).to_broadcast([ap.shape[0], n, ap.shape[1]])




def prepare_common(nc, a):
    t = {}
    t["x"] = nc.alloc_sbuf_tensor("x_rows", [P, B, D], F32)
    t["gates"] = nc.alloc_sbuf_tensor("gates", [P, 4], F32)
    t["ident"] = nc.alloc_sbuf_tensor("ident", [P, P], F32)
    t["ident_b"] = nc.alloc_sbuf_tensor("ident_b", [P, P], BF16)
    t["ones"] = nc.alloc_sbuf_tensor("ones", [P, P], F32)
    t["half"] = nc.alloc_sbuf_tensor("minus_half", [P, 16], F32)
    t["one_eps"] = nc.alloc_sbuf_tensor("one_eps", [P, 1], F32)
    t["eps_eps"] = nc.alloc_sbuf_tensor("eps_eps", [P, 1], F32)
    t["eps"] = nc.alloc_sbuf_tensor("eps", [P, 16], F32)
    loaded, made, cast, gated = (nc.alloc_semaphore(n) for n in ("common_loaded", "ident_made", "common_cast", "gates_made"))
    with nc.Block() as block:
        @block.sync
        def _(e):
            for q in range(4):
                e.dma_start(t["x"][:, 4 * q:4 * q + 4, :],
                            a["x"][4 * q:4 * q + 4].rearrange("b p d -> p b d")).then_inc(loaded, 16)

        @block.gpsimd
        def _(e):
            e.memset(t["ident"][:, :], 0.0).then_inc(made, 1)
            e.wait_ge(made, 1)
            e.affine_select(out=t["ident"][:, :], in_=t["ident"][:, :], compare_op=ALU.not_equal, fill=1.0,
                            base=0, pattern=[[-1, P]], channel_multiplier=1).then_inc(made, 1)
            e.memset(t["ones"][:, :], 1.0).then_inc(made, 1)
            e.memset(t["half"][:, :], -0.5).then_inc(made, 1)
            e.memset(t["eps"][:, :], EPS).then_inc(made, 1)
            e.memset(t["one_eps"][:, :], 1.0 + EPS).then_inc(made, 1)
            e.memset(t["eps_eps"][:, :], EPS * EPS).then_inc(made, 1)
            e.wait_ge(made, 7)
            e.tensor_copy(t["ident_b"][:, :], t["ident"][:, :]).then_inc(cast, 1)
            e.wait_ge(cast, 1)

        @block.scalar
        def _(e):
            for n, g in enumerate((a["g_xattn"], a["g_ffn"])):
                e.dma_start(t["gates"][:, 2 * n:2 * n + 2],
                            g.unsqueeze(0).to_broadcast([P, 2])).then_inc(loaded, 16)
            e.wait_ge(loaded, 96)
            e.activation(t["gates"][:, :], t["gates"][:, :], ACT.Tanh).then_inc(gated, 1)
            e.wait_ge(gated, 1)
    return t



G0, R0, HD0 = 8, 4, 8
GP = 32
GS = 3 * GP
WO_UP = 64.0
FF = 512
KF = FF // P


ORDER0 = {
    "tensor": (
        "V:7- S:2 T:0 S:3 P2+ T:1 P3+ V:0 F5-- S:4 T:2 W- V:1 S:5 P4+ T:3 V:2 F6-- T:4 S:6 V:3 "
        "F7-- S:7 F2- T:5 F7d-- V:4 T:6 F3- S:0+ T:7 V:6 V:5 S:1+ F4- F4u-"
    ),
    "vector": (
        "P1+ R:1 S:2 P2+ Vs:7- T:0 P4w S:3 R:2 R:3 S:4 T:1 P3v+ R:4 Wv- S:5 T:2 F1- T:3 R:5 F6q-- "
        "S:6 F2- T:4 S:7 Vs:3 R:6 F7v-- T:5 P3k+ R:7 P4v+ F3q- S:0+ T:6 F4- R:0+ S:1+ T:7"
    ),
    "scalar": (
        "Vs:7- T:0 P2+ S:2 T:1 S:3 F5-- P3h+ T:2 S:4 T:3 S:5 T:4 Vs:3 F7-- S:6 T:5 F2- S:7 P3k+ "
        "T:6 T:7 S:0+ F4- S:1+ F4u-"
    ),
    "gpsimd": "P1+ R:1 F5v-- R:2 XB+ R:3 R:4 F1- R:5 R:6 R:7 R:0+",
    "sync": "P3s+",
}


def layer0(nc, a, t, ctx):
    def sb(name, shape, dt=F32):
        return ctx.enter_context(nc.sbuf_tensor(name, shape, dt))

    x, gates, ident, ident_b = t["x"], t["gates"], t["ident"], t["ident_b"]
    ctxT = sb("ctxT", [P, KD, B * P])
    wq, wk = sb("wq0", [P, KD, D]), sb("wk0", [P, KD, D])
    wv = sb("wv0", [P, KD, G0 * HD0])
    wo = sb("wo0", [P, 2, 2, R0, D], F16)
    bq, bk = sb("bq0", [P, KD]), sb("bk0", [P, KD])
    bv, bo = sb("bv0", [P, G0 * HD0]), sb("bo0", [P, D])
    had1, had2 = sb("had256", [P, KD, D]), sb("had128", [P, P])
    pick = sb("pick", [P, R0])
    low_row, high_row = sb("low_row", [P, 1]), sb("high_row", [P, 1])
    out_gate = sb("out_gate0", [P, 1])
    causal8, pad8 = sb("causal8", [P, P], U8), sb("pad8", [P, B, P], U8)
    causal, pad = sb("causal", [P, P]), sb("pad", [P, B, P])
    minus = sb("minus", [P, P], BF16)
    wup, wdn = sb("wup", [P, KD, FF], BF16), sb("wdn", [P, KF, D], BF16)
    w_scale = sb("w_scale", [P, 2])
    steps = sb("steps", [P, 2, 2])
    psum = [ctx.enter_context(nc.psum_tensor(f"ps0_{n}", [P, 512], F32)) for n in range(8)]

    wraw = ctx.enter_context(nc.sbuf_tensor("ffn_raw", [P, 2, KD * FF], F32))
    wtmp = ctx.enter_context(nc.sbuf_tensor("ffn_tmp", [P, 2, KD * FF], F32))
    woraw = ctx.enter_context(nc.sbuf_tensor("wo_raw", [P, 2, R0 * D], F32))
    early, late, wdone, summed = (nc.alloc_semaphore(n) for n in ("w0_early", "w0_late", "w0_done", "w0_sum"))
    gbo = sb("gbo", [P, D])
    vp = sb("v_stack", [P, 2, G0, 2, 2, HD0], F16)
    with nc.Block() as block:
        @block.sync
        def _(e):
            e.dma_start(bq[:, :], a["bq"]).then_inc(early, 16)
            e.dma_start(bo[:, :], a["bo"].unsqueeze(0).to_broadcast([P, D])).then_inc(early, 16)
            e.dma_start(wq[:, :, :], a["WqT"].rearrange("(k p) n -> p k n", p=P)).then_inc(early, 16)
            e.dma_start(causal8[:, :], a["causal"]).then_inc(early, 16)
            e.dma_start(pad8[:, :, :], a["padding"].unsqueeze(0).to_broadcast([P, B, P])).then_inc(early, 16)
            for dst, src in ((wk, a["WkT"]), (wv, a["WvT"]), (ctxT, a["ctxT"])):
                e.dma_start(dst[:, :, :], src.rearrange("(k p) n -> p k n", p=P)).then_inc(wdone, 16)
            e.dma_start(bk[:, :], a["bk"]).then_inc(wdone, 16)
            e.dma_start(pick[:, :], a["pick"]).then_inc(wdone, 16)
            e.dma_start(bv[:, :], a["bv"].unsqueeze(0).to_broadcast([P, G0 * HD0])).then_inc(wdone, 16)
            e.dma_start(low_row[:, :], a["low_row"]).then_inc(late, 16)
            e.dma_start(high_row[:, :], a["high_row"]).then_inc(late, 16)
            e.dma_start(woraw[:, :, :].rearrange("p h (r o) -> p h r o", r=R0),
                        a["WoT"].rearrange("h p r o -> p h r o")).then_inc(late, 16)
            e.dma_start(wraw[:, 0, :].rearrange("p (k n) -> p k n", k=KD),
                        a["w_upT"].rearrange("(k p) n -> p k n", p=P)).then_inc(late, 16)
            e.dma_start(wraw[:, 1, :].rearrange("p (k n) -> p k n", k=KF),
                        a["w_downT"].rearrange("(k p) n -> p k n", p=P)).then_inc(late, 16)
            e.dma_start(had1[:, :, :], a["had256"].rearrange("(k p) n -> p k n", p=P)).then_inc(late, 16)
            e.dma_start(had2[:, :], a["had128"]).then_inc(late, 16)
            e.wait_ge(wdone, 16 * 6)

        @block.vector
        def _(e):
            e.tensor_scalar(minus[:, :], ident[:, :], MASKED, None, ALU.mult)
            e.memset(vp[:, :, :, :, :, :].rearrange("p n g a b d -> p (n g a b d)"), 0.0)
            e.tensor_scalar(out_gate[:, :], gates[:, 0:1], 1.0 / WO_UP, None, ALU.mult)
            e.wait_ge(early, 16 * 5)
            e.tensor_scalar(wq[:, :, :], wq[:, :, :], HD0**-0.5, None, ALU.mult)
            e.tensor_scalar(bq[:, :], bq[:, :], HD0**-0.5, None, ALU.mult)
            e.tensor_scalar(gbo[:, :], bo[:, :], gates[:, 0:1], None, ALU.mult)
            e.tensor_copy(causal[:, :], causal8[:, :])
            e.tensor_copy(pad[:, :, :], pad8[:, :, :])
            e.drain()

    s = Pieces(nc)
    xt_ps, F0, F1 = psum[0], psum[6], psum[7]

    @s.piece("late", "tensor")
    def _(e, i):
        e.wait_ge(summed, 1)
        e.matmul(F1[:, 0:2], t["ones"][:, :], steps[:, 0, :], start=True, stop=True).then_inc(summed, 1)

    @s.piece("made", "tensor")
    def _(e, i):
        e.wait_ge(summed, 3)
        e.wait_ge(late, 16 * 7)

    @s.piece("late", "vector")
    def _(e, i):
        chain = Chain(nc, "w0_chain", 10)
        chain.start(e, 0)
        e.wait_ge(late, 16 * 7)
        e.tensor_reduce(steps[:, 0, :], wraw[:, :, :], AX, ALU.add, apply_absolute_value=True).then_inc(summed, 1)
        parts = [wo[:, n, :, :, :].rearrange("p h r o -> p (h r o)") for n in range(2)]
        flat = woraw[:, :, :].rearrange("p h n -> p (h n)")
        chain.link(e.tensor_scalar(flat, flat, WO_UP, None, ALU.mult))
        chain.link(e.tensor_copy(parts[0], flat))
        chain.link(e.tensor_tensor(flat, flat, parts[0], ALU.subtract))
        e.tensor_scalar(parts[1], flat, high_row[:, 0:1], None, ALU.mult)
        e.wait_ge(summed, 2)
        chain.link(e.tensor_scalar(w_scale[:, :], F1[:, 0:2], 1.0 / (D * FF), EPS, ALU.mult, ALU.max))
        chain.link(e.reciprocal(steps[:, 1, :], w_scale[:, :]))
        for n in range(2):
            chain.link(e.tensor_scalar(wtmp[:, n, :], wraw[:, n, :], steps[:, 1, n:n + 1], MAGIC, ALU.mult, ALU.add))
        for n in range(2):
            chain.link(e.tensor_scalar(wraw[:, n, :], wtmp[:, n, :], MAGIC, -1.0, ALU.subtract, ALU.max))
        chain.link(e.tensor_scalar(wup[:, :, :].rearrange("p k n -> p (k n)"), wraw[:, 0, :], 1.0, None, ALU.min))
        e.tensor_scalar(wdn[:, :, :].rearrange("p k n -> p (k n)"), wraw[:, 1, :], 1.0, None, ALU.min).then_inc(summed, 1)
        chain.end()
    S = psum[1:5]
    O = psum[5]
    stats = sb("stats_p", [P, 6])
    mv = sb("mv_p", [P, 2])
    spare = sb("spare", [P, 1])
    rstd = sb("rstd_p", [P, 1])
    xn = sb("xn", [P, D])
    xnT = sb("xnT", [P, KD, P])
    cT = sb("cT", [P, KD, P])
    Q_HI, Q_LO, K_HI, K_LO = range(4)
    qk_part = sb("qk_part", [P, 4, KD, P], F16)
    qk_in = sb("qk_in", [GS, 2, G0, P], F16)
    qs = sb("q_stack", [GS, G0, P], F16)
    kb = sb("k_blocks", [GS, G0, R0, P], F16)
    v32 = sb("v32", [P, G0, 1, HD0])
    mask = sb("mask", [P, P], BF16)
    nmax = sb("nmax", [P, G0, R0])
    nbias = sb("nbias", [P, G0, R0])
    rowsum = sb("rowsum", [P, G0, R0])
    rinv = sb("rinv", [P, G0, R0])
    prob = sb("prob", [P, 4, R0, P])
    probT = sb("probT", [P, 2, 4, R0 * P], F16)
    o_hi = sb("o_hi", [P, R0 * P], F16)
    oT = sb("oT", [P, 2, R0, P], F16)
    stats_f = sb("stats_f", [P, 6])
    mv_f = sb("mv_f", [P, 2])
    rstd_f = sb("rstd_f", [P, 1])
    yn = sb("yn", [P, D])
    ynT = sb("ynT", [P, KD, P])
    quant = sb("quant", [P, 8])
    rnd1, q1 = sb("rnd1", [P, D]), sb("q1", [P, D], BF16)
    q1T = sb("q1T", [P, KD, P], BF16)
    up, hid, fly = sb("up", [P, FF]), sb("hid", [P, KF, P]), sb("fly", [P, KF, P])
    hidT = sb("hidT", [P, KF, P])
    rnd2, q2 = sb("rnd2", [P, FF]), sb("q2", [P, FF], BF16)
    q2T = sb("q2T", [P, KF, P], BF16)

    sig = s.flag
    p_stat, p_rstd = sig("p_stat", "vector"), sig("p_rstd", "gpsimd")
    p_ctx = sig("p_ctx", "gpsimd")
    p_xn, p_mask = sig("p_xn", "vector"), sig("p_mask", "vector")
    a_part, a_in, g_bias = sig("a_part", "scalar"), sig("a_in", "scalar"), sig("g_bias", "gpsimd")
    p_v32, p_v = sig("p_v32", "vector"), sig("p_v", "vector")
    p_xT = sig("p_xT", "scalar")
    pe_xT, pe_qk, pe_v = sig("pe_xT", "tensor"), sig("pe_qk", "tensor"), sig("pe_v", "tensor")
    pe_S, pe_T, pe_O = sig("pe_S", "tensor", G0), sig("pe_T", "tensor", G0), sig("pe_O", "tensor", 2)
    v_max, v_inv = sig("v_max", "vector", G0), sig("v_inv", "vector", G0)
    a_exp, g_norm = sig("a_exp", "scalar", G0), sig("g_norm", "gpsimd", G0)
    a_PT, v_PT = sig("a_PT", "scalar", G0), sig("v_PT", "vector", G0)
    p_part, d_stack, p_in = sig("p_part", "vector"), sig("d_stack", "sync", 16 * 12), sig("p_in", "vector")
    a_oh, v_oT = sig("a_oh", "scalar", 2), sig("v_oT", "vector", 2)
    pe_W, v_x1 = sig("pe_W", "tensor"), sig("v_x1", "vector")
    f_stat, f_rstd, f_yn = sig("f_stat", "vector"), sig("f_rstd", "gpsimd"), sig("f_yn", "vector")
    pe_yT, a_yT, pe_h1 = sig("pe_yT", "tensor"), sig("a_yT", "scalar"), sig("pe_h1", "tensor")
    v_q1, pe_q1, a_q1 = sig("v_q1", "vector"), sig("pe_q1", "tensor"), sig("a_q1", "scalar")
    pe_up, a_hid, pe_hT = sig("pe_up", "tensor"), sig("a_hid", "scalar"), sig("pe_hT", "tensor")
    g_fly = sig("g_fly", "gpsimd")
    a_hT, pe_h2, v_q2 = sig("a_hT", "scalar"), sig("pe_h2", "tensor"), sig("v_q2", "vector")
    pe_q2, a_q2, pe_dn, v_x2 = sig("pe_q2", "tensor"), sig("a_q2", "scalar"), sig("pe_dn", "tensor"), sig("v_x2", "vector")

    c_p1 = Chain(nc, "c_p1", 1)

    @s.piece("P1", "vector")
    def _(e, i):
        c_p1.start(e, i)
        c_p1.link(e.bn_stats(stats[:, :], x[:, i, :]))
        e.memset(spare[:, :], 0.0)
        e.bn_aggr(mv[:, :], stats[:, :]).then_inc(p_stat.sem, 1)
        c_p1.end()

    c_p1g = Chain(nc, "c_p1g", 1)

    @s.piece("P1", "gpsimd")
    def _(e, i):
        c_p1g.start(e, i)
        e.wait_ge(p_stat.sem, p_stat.at(i))
        c_p1g.link(e.tensor_tensor(rstd[:, :], mv[:, 1:2], t["eps"][:, 0:1], ALU.add))
        e.tensor_tensor(rstd[:, :], rstd[:, :], t["half"][:, 0:1], ALU.pow).then_inc(p_rstd.sem, 1)
        e.wait_ge(pe_v.sem, pe_v.at(i - 1))
        e.tensor_copy(cT[:, :, :], ctxT[:, :, bass.ds(i * P, P)]).then_inc(p_ctx.sem, 1)
        c_p1g.end()

    @s.piece("XB", "gpsimd")
    def _(e, i):
        e.wait_ge(p_xn.sem, p_xn.at(i))
        e.tensor_tensor(x[:, i, :], x[:, i, :], gbo[:, :], ALU.add).then_inc(g_bias.sem, 1)

    @s.piece("P2", "vector")
    def _(e, i):
        e.wait_ge(p_rstd.sem, p_rstd.at(i))
        e.tensor_scalar(xn[:, :], x[:, i, :], mv[:, 0:1], rstd[:, 0:1], ALU.subtract, ALU.mult).then_inc(p_xn.sem, 1)

    @s.piece("P2", "tensor")
    def _(e, i):
        e.wait_ge(p_xn.sem, p_xn.at(i))
        e.wait_ge(p_v32.sem, p_v32.at(i - 1))
        for k in range(KD):
            last = e.transpose(xt_ps[:, k * P:(k + 1) * P], xn[:, k * P:(k + 1) * P], ident[:, :])
        last.then_inc(pe_xT.sem, 1)

    @s.piece("P2", "scalar")
    def _(e, i):
        e.wait_ge(pe_xT.sem, pe_xT.at(i))
        e.activation(xnT[:, :, :].rearrange("p k t -> p (k t)"), xt_ps[:, 0:D], ACT.Copy).then_inc(p_xT.sem, 1)

    @s.piece("P3", "tensor")
    def _(e, i):
        e.wait_ge(p_xT.sem, p_xT.at(i))
        e.wait_ge(p_ctx.sem, p_ctx.at(i))
        for n, (w, src) in enumerate(((wq, xnT), (wk, cT))):
            for m in range(KD):
                for k in range(KD):
                    last = e.matmul(xt_ps[:, (2 * n + m) * P:(2 * n + m + 1) * P], w[:, k, m * P:(m + 1) * P],
                                    src[:, k, :], start=(k == 0), stop=(k == KD - 1))
        last.then_inc(pe_qk.sem, 1)

    @s.piece("P3h", "scalar")
    def _(e, i):
        e.wait_ge(pe_qk.sem, pe_qk.at(i))
        e.wait_ge(d_stack.sem, d_stack.at(i - 1))
        for hi, bias, n in ((Q_HI, bq, 0), (K_HI, bk, 2)):
            for m in range(KD):
                last = e.activation(qk_part[:, hi, m, :], xt_ps[:, (n + m) * P:(n + m + 1) * P], ACT.Identity,
                                    bias=bias[:, m:m + 1])
        last.then_inc(a_part.sem, 1)

    @s.piece("P3v", "vector")
    def _(e, i):
        e.wait_ge(a_part.sem, a_part.at(i))
        for hi, bias, n in ((Q_HI, bq, 0), (K_HI, bk, 2)):
            for m in range(KD):
                last = e.scalar_tensor_tensor(qk_part[:, hi + 1, m, :], xt_ps[:, (n + m) * P:(n + m + 1) * P],
                                              bias[:, m:m + 1], qk_part[:, hi, m, :], ALU.add, ALU.subtract)
        last.then_inc(p_part.sem, 1)

    def place(g):
        return g % 4 * KD + g // 4

    @s.piece("P3s", "sync")
    def _(e, i):
        e.wait_ge(p_part.sem, p_part.at(i))
        for n, (q, k) in enumerate(((Q_HI, K_HI), (Q_LO, K_HI), (Q_HI, K_LO))):
            for j in range(4):
                e.dma_start(qk_in[n * GP:(n + 1) * GP, :, j * KD:(j + 1) * KD, :],
                            qk_part[j * GP:(j + 1) * GP, q:k + 1:k - q, :, :]).then_inc(d_stack.sem, 16)

    @s.piece("P3k", "vector")
    def _(e, i):
        e.wait_ge(d_stack.sem, d_stack.at(i))
        e.wait_ge(pe_S.sem, pe_S.at(i - 1))
        e.tensor_tensor(mask[:, :], causal[:, :], pad[:, i, :], ALU.max).then_inc(p_mask.sem, 1)
        e.tensor_copy(qs[:, :, :], qk_in[:, 0, :, :])
        for r in range(R0 // 2):
            last = e.tensor_scalar(kb[:, :, r, :], qk_in[:, 1, :, :], pick[0:GS, r:r + 1], None, ALU.mult)
        last.then_inc(p_in.sem, 1)

    @s.piece("P3k", "scalar")
    def _(e, i):
        e.wait_ge(d_stack.sem, d_stack.at(i))
        e.wait_ge(pe_S.sem, pe_S.at(i - 1))
        for r in range(R0 // 2, R0):
            last = e.activation(kb[:, :, r, :], qk_in[:, 1, :, :], ACT.Copy, scale=pick[0:GS, r:r + 1])
        last.then_inc(a_in.sem, 1)

    @s.piece("P4", "tensor")
    def _(e, i):
        e.wait_ge(p_part.sem, p_part.at(i))
        for k in range(KD):
            last = e.matmul(xt_ps[:, 0:G0 * HD0], cT[:, k, :], wv[:, k, :], start=(k == 0), stop=(k == KD - 1))
        last.then_inc(pe_v.sem, 1)

    @s.piece("P4v", "vector")
    def _(e, i):
        e.wait_ge(pe_v.sem, pe_v.at(i))
        e.tensor_tensor(v32[:, :, 0, :], xt_ps[:, 0:G0 * HD0].rearrange("p (g d) -> p g d", g=G0),
                        bv[:, :].rearrange("p (g d) -> p g d", g=G0), ALU.add).then_inc(p_v32.sem, 1)

    c_v = Chain(nc, "c_v0", 1)

    @s.piece("P4w", "vector")
    def _(e, i):
        e.wait_ge(p_v32.sem, p_v32.at(i))
        e.wait_ge(pe_O.sem, pe_O.at(i - 1))
        c_v.start(e, i)
        twice = v32[:, :, :, :].to_broadcast([P, G0, 2, HD0])
        c_v.link(e.tensor_copy(vp[:, 0, :, :, 0, :], twice))
        e.tensor_copy(vp[:, 1, :, :, 0, :], vp[:, 0, :, :, 0, :])
        e.tensor_tensor(vp[:, 0, :, :, 1, :], twice, vp[:, 0, :, :, 0, :], ALU.subtract).then_inc(p_v.sem, 1)
        c_v.end()

    @s.piece("S", "tensor")
    def _(e, i, g):
        if g == 0:
            e.wait_ge(p_in.sem, p_in.at(i))
            e.wait_ge(a_in.sem, a_in.at(i))
            e.wait_ge(p_mask.sem, p_mask.at(i))
        bank = S[g % 4]
        e.matmul(bank[:, :], minus[:, :], tiled(mask[:, :], R0), start=True, stop=False)
        e.matmul(bank[:, :], qs[:, place(g), :], kb[:, place(g), :, :], start=False, stop=True).then_inc(pe_S.sem, 1)

    @s.piece("S", "vector")
    def _(e, i, g):
        e.wait_ge(pe_S.sem, pe_S.at(i, g + 1))
        e.tensor_reduce(nmax[:, g, :], S[g % 4][:, :].rearrange("p (r t) -> p r t", r=R0), AX, ALU.max,
                        negate=True).then_inc(v_max.sem, 1)

    @s.piece("S", "scalar")
    def _(e, i, g):
        e.wait_ge(v_max.sem, v_max.at(i, g + 1))
        for r in range(R0):
            last = e.activation(prob[:, g % 4, r, :], S[g % 4][:, r * P:(r + 1) * P], ACT.Exp,
                                bias=nmax[:, g, r:r + 1], accum_out=rowsum[:, g, r:r + 1])
        last.then_inc(a_exp.sem, 1)

    @s.piece("R", "vector")
    def _(e, i, g):
        e.wait_ge(a_exp.sem, a_exp.at(i, g + 1))
        e.reciprocal(rinv[:, g, :], rowsum[:, g, :]).then_inc(v_inv.sem, 1)

    @s.piece("R", "gpsimd")
    def _(e, i, g):
        e.wait_ge(v_inv.sem, v_inv.at(i, g + 1))
        e.tensor_tensor(prob[:, g % 4, :, :], prob[:, g % 4, :, :], spread(rinv[:, g, :], P),
                        ALU.mult).then_inc(g_norm.sem, 1)

    @s.piece("T", "tensor")
    def _(e, i, g):
        e.wait_ge(g_norm.sem, g_norm.at(i, g + 1))
        for r in range(R0):
            last = e.transpose(S[g % 4][:, r * P:(r + 1) * P], prob[:, g % 4, r, :], ident[:, :])
        last.then_inc(pe_T.sem, 1)

    @s.piece("T", "scalar")
    def _(e, i, g):
        e.wait_ge(pe_T.sem, pe_T.at(i, g + 1))
        e.activation(probT[:, 0, g % 4, :], S[g % 4][:, :], ACT.Copy).then_inc(a_PT.sem, 1)

    @s.piece("T", "vector")
    def _(e, i, g):
        e.wait_ge(a_PT.sem, a_PT.at(i, g + 1))
        e.tensor_tensor(probT[:, 1, g % 4, :], S[g % 4][:, :], probT[:, 0, g % 4, :], ALU.subtract).then_inc(v_PT.sem, 1)

    @s.piece("V", "tensor")
    def _(e, i, g):
        e.wait_ge(v_PT.sem, v_PT.at(i, g + 1))
        if g == 0:
            e.wait_ge(p_v.sem, p_v.at(i))
            e.wait_ge(v_oT.sem, v_oT.at(i - 1))
        if g == 4:
            e.wait_ge(v_oT.sem, v_oT.at(i, 1))
        j = g % 4
        for part in range(2):
            m = e.matmul(O[GP * j:GP * j + GP, :], vp[:, part, g, :, :, :].rearrange("p a b d -> p (a b d)"),
                         probT[:, part, g % 4, :], start=(part == 0), stop=(part == 1), tile_position=(0, GP * j))
        if j == 3:
            m.then_inc(pe_O.sem, 1)

    @s.piece("Vs", "scalar")
    def _(e, i, g):
        if g % 4 == 3:
            e.wait_ge(pe_O.sem, pe_O.at(i, g // 4 + 1))
            n = g // 4
            e.wait_ge(v_oT.sem, v_oT.at(i - 1) if n == 0 else v_oT.at(i, 1))
            e.activation(o_hi[:, :], O[:, :], ACT.Copy).then_inc(a_oh.sem, 1)

    @s.piece("Vs", "vector")
    def _(e, i, g):
        if g % 4 == 3:
            n = g // 4
            e.wait_ge(a_oh.sem, a_oh.at(i, n + 1))
            e.wait_ge(pe_W.sem, pe_W.at(i - 1))
            e.scalar_tensor_tensor(oT[:, n, :, :].rearrange("p r t -> p (r t)"), o_hi[:, :], low_row[:, 0:1],
                                   O[:, :], ALU.mult, ALU.add).then_inc(v_oT.sem, 1)

    @s.piece("W", "tensor")
    def _(e, i):
        e.wait_ge(v_oT.sem, v_oT.at(i))
        e.wait_ge(a_hT.sem, a_hT.at(i - 1))
        for half in range(2):
            for r in range(R0):
                for part in range(2):
                    last = e.matmul(F0[:, 0:D], oT[:, half, r, :], wo[:, part, half, r, :],
                                    start=(half == r == part == 0), stop=(half == 1 and r == R0 - 1 and part == 1))
        last.then_inc(pe_W.sem, 1)

    @s.piece("Wv", "vector")
    def _(e, i):
        e.wait_ge(pe_W.sem, pe_W.at(i))
        e.wait_ge(g_bias.sem, g_bias.at(i))
        e.scalar_tensor_tensor(x[:, i, :], F0[:, 0:D], out_gate[:, 0:1], x[:, i, :], ALU.mult, ALU.add).then_inc(v_x1.sem, 1)

    c_f1 = Chain(nc, "c_f1", 1)

    @s.piece("F1", "vector")
    def _(e, i):
        c_f1.start(e, i)
        e.wait_ge(v_x1.sem, v_x1.at(i))
        e.memset(spare[:, :], 0.0)
        c_f1.link(e.bn_stats(stats_f[:, :], x[:, i, :]))
        e.memset(spare[:, :], 0.0)
        e.bn_aggr(mv_f[:, :], stats_f[:, :]).then_inc(f_stat.sem, 1)
        c_f1.end()

    c_f1g = Chain(nc, "c_f1g", 1)

    @s.piece("F1", "gpsimd")
    def _(e, i):
        c_f1g.start(e, i)
        e.wait_ge(f_stat.sem, f_stat.at(i))
        c_f1g.link(e.tensor_tensor(rstd_f[:, :], mv_f[:, 1:2], t["eps"][:, 0:1], ALU.add))
        e.tensor_tensor(rstd_f[:, :], rstd_f[:, :], t["half"][:, 0:1], ALU.pow).then_inc(f_rstd.sem, 1)
        c_f1g.end()

    @s.piece("F2", "vector")
    def _(e, i):
        e.wait_ge(f_rstd.sem, f_rstd.at(i))
        e.tensor_scalar(yn[:, :], x[:, i, :], mv_f[:, 0:1], rstd_f[:, 0:1], ALU.subtract,
                        ALU.mult).then_inc(f_yn.sem, 1)

    @s.piece("F2", "tensor")
    def _(e, i):
        e.wait_ge(f_yn.sem, f_yn.at(i))
        for k in range(KD):
            last = e.transpose(F0[:, k * P:(k + 1) * P], yn[:, k * P:(k + 1) * P], ident[:, :])
        last.then_inc(pe_yT.sem, 1)

    @s.piece("F2", "scalar")
    def _(e, i):
        e.wait_ge(pe_yT.sem, pe_yT.at(i))
        e.activation(ynT[:, :, :].rearrange("p k t -> p (k t)"), F0[:, 0:D], ACT.Copy).then_inc(a_yT.sem, 1)

    @s.piece("F3", "tensor")
    def _(e, i):
        e.wait_ge(a_yT.sem, a_yT.at(i))
        e.wait_ge(v_x2.sem, v_x2.at(i - 1))
        for k in range(KD):
            last = e.matmul(F1[:, 0:D], ynT[:, k, :], had1[:, k, :], start=(k == 0), stop=(k == KD - 1))
        last.then_inc(pe_h1.sem, 1)

    def quantise(e, chain, src, width, norm, c, rnd, out, done):
        chain.link(e.tensor_reduce(quant[:, c:c + 1], src, AX, ALU.max, apply_absolute_value=True))
        if c == 4:
            chain.link(e.tensor_tensor(quant[:, c:c + 1], quant[:, c:c + 1], quant[:, 7:8], ALU.mult))
            chain.link(e.tensor_scalar(quant[:, c:c + 1], quant[:, c:c + 1], norm, EPS, ALU.mult, ALU.max))
        else:
            chain.link(e.tensor_scalar(quant[:, c:c + 1], quant[:, c:c + 1], norm, EPS, ALU.mult, ALU.max))
        chain.link(e.reciprocal(quant[:, c + 1:c + 2], quant[:, c:c + 1]))
        if c == 4:
            chain.link(e.tensor_scalar(quant[:, c + 2:c + 3], quant[:, c + 1:c + 2], quant[:, 7:8], 127.0 * norm,
                                       ALU.mult, ALU.mult))
        else:
            chain.link(e.tensor_scalar(quant[:, c + 2:c + 3], quant[:, c + 1:c + 2], 127.0 * norm, None, ALU.mult))
        chain.link(e.tensor_scalar(rnd, src, quant[:, c + 2:c + 3], MAGIC, ALU.mult, ALU.add))
        e.tensor_scalar(out, rnd, MAGIC, None, ALU.subtract).then_inc(done.sem, 1)

    c_f3 = Chain(nc, "c_f3", 5)

    @s.piece("F3q", "vector")
    def _(e, i):
        c_f3.start(e, i)
        e.wait_ge(pe_h1.sem, pe_h1.at(i))
        quantise(e, c_f3, F1[:, 0:D], D, D**-0.5, 0, rnd1[:, :], q1[:, :], v_q1)
        c_f3.end()

    @s.piece("F4", "tensor")
    def _(e, i):
        e.wait_ge(v_q1.sem, v_q1.at(i))
        for k in range(KD):
            last = e.transpose(F0[:, k * 64:(k + 1) * 64].bitcast(BF16), q1[:, k * P:(k + 1) * P], ident_b[:, :])
        last.then_inc(pe_q1.sem, 1)

    @s.piece("F4u", "tensor")
    def _(e, i):
        e.wait_ge(a_q1.sem, a_q1.at(i))
        for k in range(KD):
            last = e.matmul(F1[:, :], q1T[:, k, :], wup[:, k, :], start=(k == 0), stop=(k == KD - 1))
        last.then_inc(pe_up.sem, 1)

    c_f4 = Chain(nc, "c_f4", 1)

    @s.piece("F4", "scalar")
    def _(e, i):
        e.wait_ge(pe_q1.sem, pe_q1.at(i))
        e.activation(q1T[:, :, :].rearrange("p k t -> p (k t)"), F0[:, 0:P].bitcast(BF16), ACT.Copy).then_inc(a_q1.sem, 1)

    @s.piece("F4u", "scalar")
    def _(e, i):
        c_f4.start(e, i)
        e.wait_ge(pe_up.sem, pe_up.at(i))
        c_f4.link(e.activation(up[:, :], F1[:, :], ACT.Relu))
        e.activation(hid[:, :, :].rearrange("p k n -> p (k n)"), up[:, :], ACT.Square).then_inc(a_hid.sem, 1)
        c_f4.end()

    c_f4v = Chain(nc, "c_f4v", 2)

    @s.piece("F4", "vector")
    def _(e, i):
        c_f4v.start(e, i)
        c_f4v.link(e.tensor_scalar(quant[:, 3:4], quant[:, 0:1], w_scale[:, 0:1], 1.0 / 127.0, ALU.mult, ALU.mult))
        c_f4v.link(e.tensor_tensor(quant[:, 7:8], quant[:, 3:4], quant[:, 3:4], ALU.mult))
        c_f4v.end()

    c_f5 = Chain(nc, "c_f5", 1)

    @s.piece("F5v", "gpsimd")
    def _(e, i):
        c_f5.start(e, i)
        e.wait_ge(a_hid.sem, a_hid.at(i))
        e.wait_ge(pe_hT.sem, pe_hT.at(i - 1))
        e.tensor_tensor(fly[:, 0:4:2, :], hid[:, 0:4:2, :], hid[:, 1:4:2, :], ALU.add)
        c_f5.link(e.tensor_tensor(fly[:, 1:4:2, :], hid[:, 0:4:2, :], hid[:, 1:4:2, :], ALU.subtract))
        e.tensor_tensor(hid[:, 0:2, :], fly[:, 0:2, :], fly[:, 2:4, :], ALU.add)
        e.tensor_tensor(hid[:, 2:4, :], fly[:, 0:2, :], fly[:, 2:4, :], ALU.subtract).then_inc(g_fly.sem, 1)
        c_f5.end()

    @s.piece("F5", "tensor")
    def _(e, i):
        e.wait_ge(g_fly.sem, g_fly.at(i))
        for k in range(KF):
            last = e.transpose(F0[:, k * P:(k + 1) * P], hid[:, k, :], ident[:, :])
        last.then_inc(pe_hT.sem, 1)

    @s.piece("F5", "scalar")
    def _(e, i):
        e.wait_ge(pe_hT.sem, pe_hT.at(i))
        e.wait_ge(pe_h2.sem, pe_h2.at(i - 1))
        e.activation(hidT[:, :, :].rearrange("p k t -> p (k t)"), F0[:, :], ACT.Copy).then_inc(a_hT.sem, 1)

    @s.piece("F6", "tensor")
    def _(e, i):
        e.wait_ge(a_hT.sem, a_hT.at(i))
        for k in range(KF):
            last = e.matmul(F1[:, k * P:(k + 1) * P], hidT[:, k, :], had2[:, :], start=True, stop=True)
        last.then_inc(pe_h2.sem, 1)

    c_f6 = Chain(nc, "c_f6", 6)

    @s.piece("F6q", "vector")
    def _(e, i):
        c_f6.start(e, i)
        e.wait_ge(pe_h2.sem, pe_h2.at(i))
        quantise(e, c_f6, F1[:, :], FF, FF**-0.5, 4, rnd2[:, :], q2[:, :], v_q2)
        c_f6.end()

    @s.piece("F7", "tensor")
    def _(e, i):
        e.wait_ge(v_q2.sem, v_q2.at(i))
        for k in range(KF):
            last = e.transpose(F1[:, k * 64:(k + 1) * 64].bitcast(BF16), q2[:, k * P:(k + 1) * P], ident_b[:, :])
        last.then_inc(pe_q2.sem, 1)

    @s.piece("F7d", "tensor")
    def _(e, i):
        e.wait_ge(a_q2.sem, a_q2.at(i))
        for k in range(KF):
            last = e.matmul(F1[:, 0:D], q2T[:, k, :], wdn[:, k, :], start=(k == 0), stop=(k == KF - 1))
        last.then_inc(pe_dn.sem, 1)

    @s.piece("F7", "scalar")
    def _(e, i):
        e.wait_ge(pe_q2.sem, pe_q2.at(i))
        e.activation(q2T[:, :, :].rearrange("p k t -> p (k t)"), F1[:, 0:2 * P].bitcast(BF16),
                     ACT.Copy).then_inc(a_q2.sem, 1)

    c_f7 = Chain(nc, "c_f7", 2)

    @s.piece("F7v", "vector")
    def _(e, i):
        c_f7.start(e, i)
        c_f7.link(e.tensor_scalar(quant[:, 3:4], quant[:, 4:5], w_scale[:, 1:2], 1.0 / 127.0, ALU.mult, ALU.mult))
        c_f7.link(e.tensor_tensor(quant[:, 3:4], quant[:, 3:4], gates[:, 2:3], ALU.mult))
        e.wait_ge(pe_dn.sem, pe_dn.at(i))
        e.scalar_tensor_tensor(x[:, i, :], F1[:, 0:D], quant[:, 3:4], x[:, i, :], ALU.mult,
                               ALU.add).then_inc(v_x2.sem, 1)
        c_f7.end()

    def body(owner, i):
        return [(name, i + shift, *item) for name, shift, *item in order(ORDER0[owner])]

    def some(owner, i):
        return [step for step in body(owner, i) if 0 <= step[1] < B]

    def before(owner):
        return [(n, 0) for n in ("P1", "P2", "XB", "P3", "P3h", "P3v", "P3s", "P4", "P4v", "late", "P3k")] + [
            ("S", 0, 0), ("S", 0, 1), ("R", 0, 0)] + some(owner, 0) + [("made", 0)] + some(owner, 1)

    def after(owner):
        return some(owner, B - 1) + some(owner, B) + some(owner, B + 1)

    with nc.Block() as block:
        s.run(block, before, body, after, (2, B - 1))



G1, HD1 = 8, 128
J = 4
W1 = 8 * D
Q_, QX_, K_, KX_, V_, VX_ = 0, 512, 1024, 1280, 1536, 1792
CTX_UP = 64.0
F8_MAX = 448.0
F8_TINY = 2.0**-6
F8_SHIFT = 1.5 * 2.0**20
EXPONENT = 0x7F80


class Parting:

    def __init__(self, nc, name, raw, items):
        self.raw, self.items, self.ring = raw, items, raw.shape[1]
        self.got = [nc.alloc_semaphore(f"{name}_got{n}") for n in range(self.ring)]
        self.high, self.low = nc.alloc_semaphore(f"{name}_high"), nc.alloc_semaphore(f"{name}_low")

    def source(self, n):
        return self.raw[:, n % self.ring, 0:self.items[n][1]]

    def like(self, n, ap):
        if len(ap.shape) == 2:
            return self.source(n)
        if len(ap.shape) == 3:
            return self.source(n).rearrange("p (m c) -> p m c", m=ap.shape[1])
        return self.source(n).rearrange("p (l m c) -> p l m c", l=ap.shape[1], m=ap.shape[2])

    def load(self, e):
        for n, (src, *_) in enumerate(self.items):
            if n >= self.ring:
                self.wait_low(e, n - self.ring)
            e.dma_start(self.like(n, src), src).then_inc(self.got[n % self.ring], 16)

    def wait_load(self, e, n):
        e.wait_ge(self.got[n % self.ring], 16 * (n // self.ring + 1))

    def wait_high(self, e, n):
        e.wait_ge(self.high, n + 1)

    def wait_low(self, e, n):
        e.wait_ge(self.low, n + 1)

    def high_part(self, scalar, n):
        part, factor = self.items[n][2][0], self.items[n][3]
        scalar.activation(part, self.like(n, part), ACT.Copy, scale=factor).then_inc(self.high, 1)

    def low_part(self, vector, n):
        (high, low), factor = self.items[n][2], self.items[n][3]
        vector.scalar_tensor_tensor(low, self.like(n, low), factor, high, ALU.mult, ALU.subtract).then_inc(self.low, 1)


ORDER1 = {
    "tensor": "PT:1- A:0+ SC:0 SC:1 A:1+ O-- PV:1- A:2+ PT:0 TQ:0+ A:3+ PV:0 TQ:1+ TQ:2+",
    "vector": "PT:1- QS-- SC:0 SC:1 R:0 O-- R:1 N:0+ QM:1- N:1+ PT:0 Q- N:2+ QM:0",
    "scalar": "ST:0+ SC:0 ST:1+ SC:1 VE ST:2+ TQ:0+ TQ:1+ TQ:2+",
    "gpsimd": "R:0 SU:0+ SU:1+ R:1 SU:2+ QA-",
    "sync": "",
}


def layer1_attention(nc, a, t, ctx):
    def sb(name, shape, dt=F32):
        return ctx.enter_context(nc.sbuf_tensor(name, shape, dt))

    x, gates, ident = t["x"], t["gates"], t["ident"]
    bank = [ctx.enter_context(nc.psum_tensor(f"ps1_{n}", [P, 512], F32)) for n in range(8)]
    wb = sb("w_proj_in", [P, KD, 2, J * W1], F16)
    wp = sb("w_proj_out", [P, 2, 32, D], F16)
    cx = sb("ctx_parts", [P, KD, 2, B * P], F16)
    insc = sb("in_scales", [P, KD, 4])
    inv_insc = sb("inv_in_scales", [P, KD, 4])
    row_w, row_b = sb("row_w", [P, KD, 4]), sb("row_b", [P, KD, 4])
    lnw, lnb = sb("ln_w", [P, KD]), sb("ln_b", [P, KD])
    wsc = sb("w_scales", [P, 5])
    psc = sb("proj_in_scale", [P, 1])
    hln = sb("head_ln", [P, 8])
    smooth, inv_smooth = sb("smooth", [P, 32]), sb("inv_smooth", [P, 32])
    head_eps, sign = sb("head_eps", [P, 12]), sb("sign", [P, 3])
    out_gate = sb("out_gate", [P, 1])

    items = []
    for k in range(KD):
        items += [("wqT", k, Q_, 512, 0, True), ("wqxT", k, QX_, 512, 1, True), ("wkT", k, K_, 256, 2, True),
                  ("wvT", k, V_, 256, 3, False), ("wkxT", k, KX_, 256, None, True),
                  ("wvxT", k, VX_, 256, None, False)]
    nproj = 4
    NRAW = 5
    work_items = []
    for name, k, c0, w, sc, centred in items:
        parts = [wb[:, k, hl, :].rearrange("p (j c) -> p j c", j=J)[:, :, c0:c0 + w] for hl in range(2)]
        work_items.append((a[name].rearrange("(k p) n -> p k n", p=P)[:, k, :], J * w, parts,
                           CTX_UP if sc is None else insc[:, k, sc:sc + 1], centred))
    for q in range(nproj):
        parts = [wp[:, hl, 8 * q:8 * q + 8, :] for hl in range(2)]
        work_items.append((a["wprojT"].rearrange("(h p) o -> p h o", p=P)[:, 8 * q:8 * q + 8, :], 2048, parts, 1.0, False))
    for k in range(KD):
        parts = [cx[:, k, hl, :] for hl in range(2)]
        work_items.append((a["ctxT"].rearrange("(k p) n -> p k n", p=P)[:, k, :], 2048, parts, 1.0, False))

    with nc.sbuf_tensor("raw1", [P, NRAW, 2048], F32) as raw, nc.sbuf_tensor("head_sum", [P, NRAW, 16], F32) as head_sum:
        small = nc.alloc_semaphore("w1_small")
        meant, centred_ = nc.alloc_semaphore("w1_mean"), nc.alloc_semaphore("w1_centred")
        parting = Parting(nc, "w1", raw, work_items)

        def centred_before(n):
            return sum(1 for it in work_items[:n + 1] if it[4])

        def wait_source(e, n):
            if work_items[n][4]:
                e.wait_ge(centred_, centred_before(n))
            else:
                parting.wait_load(e, n)

        with nc.Block() as block:
            @block.sync
            def _(e):
                e.dma_start(insc[:, :, :], a["in_scales"].rearrange("(k p) n -> p k n", p=P)).then_inc(small, 16)
                e.dma_start(lnw[:, :], a["ln_w"]).then_inc(small, 16)
                e.dma_start(lnb[:, :], a["ln_b"]).then_inc(small, 16)
                e.dma_start(wsc[:, :], a["w_scales"].unsqueeze(0).to_broadcast([P, 5])).then_inc(small, 16)
                e.dma_start(psc[:, :], a["proj_in_scale"].unsqueeze(0).to_broadcast([P, 1])).then_inc(small, 16)
                e.dma_start(hln[:, :], a["head_ln"]).then_inc(small, 16)
                e.dma_start(smooth[:, :], a["smooth"]).then_inc(small, 16)
                parting.load(e)

            @block.scalar
            def _(e):
                e.wait_ge(small, 16 * 7)
                for n in range(len(work_items)):
                    wait_source(e, n)
                    parting.high_part(e, n)
                parting.wait_high(e, len(work_items) - 1)

            @block.gpsimd
            def _(e):
                for n, (_, width, _, _, centred) in enumerate(work_items):
                    if centred:
                        heads = width // HD1
                        byhead = parting.source(n).rearrange("p (h d) -> p h d", h=heads)
                        e.wait_ge(meant, centred_before(n))
                        e.tensor_tensor(byhead, byhead, spread(head_sum[:, n % NRAW, 0:heads], HD1),
                                        ALU.subtract).then_inc(centred_, 1)
                e.wait_ge(centred_, centred_before(len(work_items)))

            @block.vector
            def _(e):
                chain = Chain(nc, "w1_chain", 15 + centred_before(len(work_items)))
                chain.start(e, 0)
                e.wait_ge(small, 16 * 7)
                chain.link(e.reciprocal(inv_insc[:, :, :], insc[:, :, :]))
                for k in range(KD):
                    e.tensor_scalar(row_w[:, k, :], inv_insc[:, k, :], lnw[:, k:k + 1], None, ALU.mult)
                    e.tensor_scalar(row_b[:, k, :], inv_insc[:, k, :], lnb[:, k:k + 1], None, ALU.mult)
                chain.link(e.reciprocal(inv_smooth[:, :], smooth[:, :]))
                chain.link(e.tensor_scalar(hln[:, 4:8], hln[:, 4:8], HD1**-0.5, None, ALU.mult))
                chain.link(e.tensor_copy(head_eps[:, 0:4], spread(wsc[:, 0:1], 4)))
                chain.link(e.tensor_copy(head_eps[:, 4:8], spread(wsc[:, 1:2], 4)))
                chain.link(e.tensor_copy(head_eps[:, 8:10], spread(wsc[:, 2:3], 2)))
                chain.link(e.memset(head_eps[:, 10:12], 1.0 / CTX_UP))
                chain.link(e.tensor_tensor(head_eps[:, :], head_eps[:, :], head_eps[:, :], ALU.mult))
                chain.link(e.reciprocal(head_eps[:, :], head_eps[:, :]))
                chain.link(e.tensor_scalar(head_eps[:, :], head_eps[:, :], EPS, None, ALU.mult))
                chain.link(e.tensor_scalar(sign[:, :], wsc[:, 0:3], 0.0, 2.0, ALU.is_ge, ALU.mult))
                chain.link(e.tensor_scalar(sign[:, :], sign[:, :], -1.0, None, ALU.add))
                chain.link(e.tensor_tensor(hln[:, 0:6:2], hln[:, 0:6:2], sign[:, :], ALU.mult))
                chain.link(e.tensor_tensor(out_gate[:, :], psc[:, :], wsc[:, 4:5], ALU.mult))
                chain.link(e.tensor_tensor(out_gate[:, :], out_gate[:, :], gates[:, 1:2], ALU.mult))

                def mean(n):
                    heads = work_items[n][1] // HD1
                    parting.wait_load(e, n)
                    m = head_sum[:, n % NRAW, 0:heads]
                    chain.link(e.tensor_reduce(m, parting.source(n).rearrange("p (h d) -> p h d", h=heads), AX, ALU.add))
                    e.tensor_scalar(m, m, 1.0 / HD1, None, ALU.mult).then_inc(meant, 1)

                ahead = 2
                for n in range(-ahead, len(work_items)):
                    if n + ahead < len(work_items) and work_items[n + ahead][4]:
                        mean(n + ahead)
                    if n >= 0:
                        parting.wait_high(e, n)
                        parting.low_part(e, n)
                chain.end()
                parting.wait_low(e, len(work_items) - 1)

    r = Pieces(nc)
    xq = sb("xq", [P, KD, 4, B * P], BF16)
    only_here = ExitStack()

    def rb(name, shape, dt=F32):
        return only_here.enter_context(nc.sbuf_tensor(name, shape, dt))

    stats, mv, rstd, spare = rb("stats_r", [P, 2, 6]), rb("mv_r", [P, 2, 2]), rb("rstd_r", [P, 2]), rb("spare_r", [P, 1])
    rows = rb("rows_n", [P, 2, D])
    wide, total = rb("wide_r", [P, 2, 8, P]), rb("total_r", [P, 2, 8, P])
    yb, ye = rb("yb", [P, 2, 8, P], BF16), rb("ye", [P, 2, 8, P], BF16)
    r_stat, r_rstd, r_n = r.flag("r_stat", "vector"), r.flag("r_rstd", "gpsimd"), r.flag("r_n", "vector")
    r_T, r_u = r.flag("r_T", "tensor", 1, 2), r.flag("r_u", "scalar", 1, 2)
    r_grid, r_add = r.flag("r_grid", "vector", 1, 2), r.flag("r_add", "gpsimd")
    c_r1, c_r1g, c_r3 = Chain(nc, "c_r1", 1), Chain(nc, "c_r1g", 2), Chain(nc, "c_r3", 2)

    def float8_grid(e, chain, y32, b16, e16):
        chain.link(e.tensor_scalar(b16, y32, F8_MAX, -F8_MAX, ALU.min, ALU.max))
        chain.link(e.tensor_scalar(e16.bitcast(U16), b16.bitcast(U16), EXPONENT, None, ALU.bitwise_and))
        return e.tensor_scalar(e16, e16, F8_TINY, F8_SHIFT, ALU.max, ALU.mult)

    @r.piece("1", "vector")
    def _(e, n, b):
        i = 2 * n + b
        c_r1.start(e, i)
        c_r1.link(e.bn_stats(stats[:, b, :], x[:, i, :]))
        e.memset(spare[:, :], 0.0)
        e.bn_aggr(mv[:, b, :], stats[:, b, :]).then_inc(r_stat.sem, 1)
        c_r1.end()

    @r.piece("1", "gpsimd")
    def _(e, n, b):
        i = 2 * n + b
        c_r1g.start(e, i)
        e.wait_ge(r_stat.sem, r_stat.at(i))
        c_r1g.link(e.tensor_tensor(rstd[:, b:b + 1], mv[:, b, 1:2], t["one_eps"][:, 0:1], ALU.mult))
        c_r1g.link(e.tensor_tensor(rstd[:, b:b + 1], rstd[:, b:b + 1], t["eps_eps"][:, 0:1], ALU.add))
        e.tensor_tensor(rstd[:, b:b + 1], rstd[:, b:b + 1], t["half"][:, 0:1], ALU.pow).then_inc(r_rstd.sem, 1)
        c_r1g.end()

    @r.piece("2", "vector")
    def _(e, n, b):
        i = 2 * n + b
        e.wait_ge(r_rstd.sem, r_rstd.at(i))
        e.wait_ge(r_T.sem, r_T.at(i - 2))
        e.tensor_scalar(rows[:, b, :], x[:, i, :], mv[:, b, 0:1], rstd[:, b:b + 1], ALU.subtract,
                        ALU.mult).then_inc(r_n.sem, 1)

    @r.piece("2", "tensor")
    def _(e, n, b):
        i = 2 * n + b
        e.wait_ge(r_n.sem, r_n.at(i))
        e.wait_ge(r_u.sem, r_u.at(i - 2))
        for k in range(KD):
            last = e.transpose(bank[b][:, k * P:(k + 1) * P], rows[:, b, k * P:(k + 1) * P], ident[:, :])
        last.then_inc(r_T.sem, 1)

    @r.piece("2", "scalar")
    def _(e, n, b):
        i = 2 * n + b
        e.wait_ge(r_T.sem, r_T.at(i))
        e.wait_ge(r_grid.sem, r_grid.at(i - 2))
        for k in range(KD):
            for c in range(4):
                last = e.activation(wide[:, b, 4 * k + c, :], bank[b][:, k * P:(k + 1) * P], ACT.Identity,
                                    bias=row_b[:, k, c:c + 1], scale=row_w[:, k, c:c + 1])
        last.then_inc(r_u.sem, 1)

    @r.piece("3", "vector")
    def _(e, n, b):
        i = 2 * n + b
        c_r3.start(e, i)
        e.wait_ge(r_u.sem, r_u.at(i))
        float8_grid(e, c_r3, wide[:, b, :, :], yb[:, b, :, :], ye[:, b, :, :]).then_inc(r_grid.sem, 1)
        c_r3.end()

    @r.piece("3A", "gpsimd")
    def _(e, n, b):
        i = 2 * n + b
        e.wait_ge(r_grid.sem, r_grid.at(i))
        e.tensor_tensor(total[:, b, :, :], yb[:, b, :, :], ye[:, b, :, :], ALU.add).then_inc(r_add.sem, 1)

    @r.piece("3S", "vector")
    def _(e, n, b):
        i = 2 * n + b
        e.wait_ge(r_add.sem, r_add.at(i))
        e.tensor_tensor(xq[:, :, :, bass.ds(i * P, P)].rearrange("p k s t -> p (k s) t"), total[:, b, :, :],
                        ye[:, b, :, :], ALU.subtract)

    rows_order = order("2:1 1:0+ 3:0 3A:0 3S:1- 2:0+ 1:1+ 3:1 3A:1 3S:0")

    def rows_body(owner, n, nxt=True, prev=True):
        return [(name, n + shift, item) for name, shift, item in rows_order
                if shift == 0 or (nxt if shift == 1 else prev)]

    with nc.Block() as block:
        last = B // 2 - 1
        r.run(block, lambda owner: order("1:0 1:1 2:0") + rows_body(owner, 0, prev=False), rows_body,
              lambda owner: rows_body(owner, last, nxt=False) + [("3S", last, 1)], (1, last))
    only_here.close()

    s = Pieces(nc)
    A, S, O = bank[0:4], bank[4:6], bank[6:8]
    squares, hss, hr = sb("squares", [P, 12, HD1], BF16), sb("head_squares", [P, 12]), sb("head_rstd", [P, 12])
    hn = sb("heads_n", [P, 3, 4, HD1])
    hT = sb("headsT", [P, 3, 4, P])
    v = sb("v1", [P, 2, 2, HD1])
    nmax, rowsum, rinv = sb("nmax1", [P, 2, 4]), sb("rowsum1", [P, 2, 4]), sb("rinv1", [P, 2, 4])
    prob, probT = sb("prob1", [P, 2, 4, P]), sb("probT1", [P, 2, 4, P])
    wide2, cb, ce = sb("wide2", [P, 8, P]), sb("cb", [P, 8, P], BF16), sb("ce", [P, 8, P], BF16)
    total2 = sb("total2", [P, 8, P])
    catq = sb("catq", [P, 8, P], BF16)
    sig = s.flag
    pe_A, a_st, g_r = sig("pe_A", "tensor", 4), sig("a_st", "scalar", 3), sig("g_r", "gpsimd", 3)
    v_n, pe_hT = sig("v_n", "vector", 3), sig("pe_headsT", "tensor", 3)
    a_hT, a_v = sig("a_headsT", "scalar", 3), sig("a_v", "scalar")
    pe_S, v_mx, a_ex = sig("pe_S1", "tensor", 2), sig("v_mx1", "vector", 2), sig("a_ex1", "scalar", 2)
    v_iv, g_p = sig("v_iv1", "vector", 2), sig("g_p1", "gpsimd", 2)
    pe_PT, v_PT = sig("pe_PT1", "tensor", 2), sig("v_PT1", "vector", 2)
    v_qm = sig("v_qm", "vector", 2)
    v_grid, g_add = sig("v_grid", "vector"), sig("g_add", "gpsimd")
    pe_O, v_q, pe_out, v_x = sig("pe_O1", "tensor", 2), sig("v_catq", "vector"), sig("pe_out", "tensor"), sig("v_x3", "vector")

    @s.piece("A", "tensor")
    def _(e, i, n):
        rows_at, w_at = bass.ds((i // J) * P, P), (i % J) * W1

        def project(out, which, c0, n):
            for k in range(KD):
                for hl in range(2):
                    last = e.matmul(out, xq[:, k, which, rows_at], wb[:, k, hl, bass.ds(w_at + c0, n)],
                                    start=(k == 0 and hl == 0), stop=(k == KD - 1 and hl == 1))
            return last

        def project_context(out, c0, n):
            for k in range(KD):
                for part, hl in ((0, 0), (0, 1), (1, 0)):
                    last = e.matmul(out, cx[:, k, part, rows_at], wb[:, k, hl, bass.ds(w_at + c0, n)],
                                    start=(k == 0 and part == hl == 0), stop=(k == KD - 1 and part == 1))
            return last

        if n < 3:
            e.wait_ge(a_hT.sem, a_hT.at(i - 1, n + 1))
        else:
            e.wait_ge(a_v.sem, a_v.at(i - 1))
        if n < 2:
            project(A[n][:, :], n, (Q_, QX_)[n], 512).then_inc(pe_A.sem, 1)
        else:
            project(A[n][:, 0:256], n, (K_, V_)[n - 2], 256)
            project_context(A[n][:, 256:512], (KX_, VX_)[n - 2], 256).then_inc(pe_A.sem, 1)

    @s.piece("ST", "scalar")
    def _(e, i, n):
        e.wait_ge(pe_A.sem, pe_A.at(i, n + 1))
        for h in range(4):
            last = e.activation(squares[:, 4 * n + h, :], A[n][:, h * HD1:(h + 1) * HD1], ACT.Square, scale=HD1**-0.5,
                                accum_out=hss[:, 4 * n + h:4 * n + h + 1])
        last.then_inc(a_st.sem, 1)

    c_su = [Chain(nc, f"c_su{n}", 1) for n in range(3)]

    @s.piece("SU", "gpsimd")
    def _(e, i, n):
        c_su[n].start(e, i)
        four = slice(4 * n, 4 * n + 4)
        e.wait_ge(a_st.sem, a_st.at(i, n + 1))
        c_su[n].link(e.tensor_tensor(hr[:, four], hss[:, four], head_eps[:, four], ALU.add))
        e.tensor_tensor(hr[:, four], hr[:, four], t["half"][:, four], ALU.pow).then_inc(g_r.sem, 1)
        c_su[n].end()

    @s.piece("N", "vector")
    def _(e, i, n):
        e.wait_ge(g_r.sem, g_r.at(i, n + 1))
        e.tensor_tensor(hn[:, n, :, :], A[n][:, :].rearrange("p (h d) -> p h d", h=4),
                        spread(hr[:, 4 * n:4 * n + 4], HD1), ALU.mult).then_inc(v_n.sem, 1)

    @s.piece("TQ", "tensor")
    def _(e, i, n):
        e.wait_ge(v_n.sem, v_n.at(i, n + 1))
        for h in range(4):
            last = e.transpose(A[n][:, h * P:(h + 1) * P], hn[:, n, h, :], ident[:, :])
        last.then_inc(pe_hT.sem, 1)

    @s.piece("TQ", "scalar")
    def _(e, i, n):
        e.wait_ge(pe_hT.sem, pe_hT.at(i, n + 1))
        for h0, h1, c in (((0, 4, 0),), ((0, 4, 2),), ((0, 2, 4), (2, 4, 6)))[n]:
            last = e.activation(hT[:, n, h0:h1, :].rearrange("p h t -> p (h t)"), A[n][:, h0 * P:h1 * P],
                                ACT.Identity, bias=hln[:, c + 1:c + 2], scale=hln[:, c:c + 1])
        last.then_inc(a_hT.sem, 1)

    @s.piece("VE", "scalar")
    def _(e, i):
        e.wait_ge(pe_A.sem, pe_A.at(i))
        e.wait_ge(pe_O.sem, pe_O.at(i - 1))
        e.activation(v[:, 0, :, :].rearrange("p h d -> p (h d)"), A[3][:, 0:256], ACT.Copy, scale=wsc[:, 3:4])
        e.activation(v[:, 1, :, :].rearrange("p h d -> p (h d)"), A[3][:, 256:512], ACT.Copy,
                     scale=1.0 / CTX_UP).then_inc(a_v.sem, 1)

    @s.piece("SC", "tensor")
    def _(e, i, kind):
        e.wait_ge(a_hT.sem, a_hT.at(i))
        e.wait_ge(v_PT.sem, v_PT.at(i - 1, kind + 1))
        for h in range(4):
            last = e.matmul(S[kind][:, h * P:(h + 1) * P], hT[:, kind, h, :], hT[:, 2, 2 * kind + h // 2, :],
                            start=True, stop=True)
        last.then_inc(pe_S.sem, 1)

    @s.piece("SC", "vector")
    def _(e, i, kind):
        e.wait_ge(pe_S.sem, pe_S.at(i, kind + 1))
        e.tensor_reduce(nmax[:, kind, :], S[kind][:, :].rearrange("p (h t) -> p h t", h=4), AX, ALU.max,
                        negate=True).then_inc(v_mx.sem, 1)

    @s.piece("SC", "scalar")
    def _(e, i, kind):
        e.wait_ge(v_mx.sem, v_mx.at(i, kind + 1))
        for h in range(4):
            last = e.activation(prob[:, kind, h, :], S[kind][:, h * P:(h + 1) * P], ACT.Exp,
                                bias=nmax[:, kind, h:h + 1], accum_out=rowsum[:, kind, h:h + 1])
        last.then_inc(a_ex.sem, 1)

    @s.piece("R", "vector")
    def _(e, i, kind):
        e.wait_ge(a_ex.sem, a_ex.at(i, kind + 1))
        e.reciprocal(rinv[:, kind, :], rowsum[:, kind, :]).then_inc(v_iv.sem, 1)

    @s.piece("R", "gpsimd")
    def _(e, i, kind):
        e.wait_ge(v_iv.sem, v_iv.at(i, kind + 1))
        e.tensor_tensor(prob[:, kind, :, :], prob[:, kind, :, :], spread(rinv[:, kind, :], P),
                        ALU.mult).then_inc(g_p.sem, 1)

    @s.piece("PT", "tensor")
    def _(e, i, kind):
        e.wait_ge(g_p.sem, g_p.at(i, kind + 1))
        for h in range(4):
            last = e.transpose(S[kind][:, h * P:(h + 1) * P], prob[:, kind, h, :], ident[:, :])
        last.then_inc(pe_PT.sem, 1)

    @s.piece("PT", "vector")
    def _(e, i, kind):
        e.wait_ge(pe_PT.sem, pe_PT.at(i, kind + 1))
        e.tensor_copy(probT[:, kind, :, :].rearrange("p h t -> p (h t)"), S[kind][:, :]).then_inc(v_PT.sem, 1)

    @s.piece("PV", "tensor")
    def _(e, i, kind):
        e.wait_ge(a_v.sem, a_v.at(i))
        if kind == 1:
            e.wait_ge(v_x.sem, v_x.at(i - 1))
        e.wait_ge(v_PT.sem, v_PT.at(i, kind + 1))
        for g in range(2):
            last = e.matmul(O[kind][:, g * 2 * P:(g + 1) * 2 * P], v[:, kind, g, :],
                            probT[:, kind, 2 * g:2 * g + 2, :], start=True, stop=True)
        last.then_inc(pe_O.sem, 1)

    c_q = Chain(nc, "c_q", 2)

    @s.piece("QM", "vector")
    def _(e, i, kind):
        e.wait_ge(pe_O.sem, pe_O.at(i, kind + 1))
        e.tensor_tensor(wide2[:, 4 * kind:4 * kind + 4, :], O[kind][:, :].rearrange("p (h t) -> p h t", h=4),
                        spread(inv_smooth[:, bass.ds((i % J) * 4 + 16 * kind, 4)], P), ALU.mult).then_inc(v_qm.sem, 1)

    @s.piece("Q", "vector")
    def _(e, i):
        c_q.start(e, i)
        e.wait_ge(v_qm.sem, v_qm.at(i))
        float8_grid(e, c_q, wide2[:, :, :], cb[:, :, :], ce[:, :, :]).then_inc(v_grid.sem, 1)
        c_q.end()

    @s.piece("QA", "gpsimd")
    def _(e, i):
        e.wait_ge(v_grid.sem, v_grid.at(i))
        e.tensor_tensor(total2[:, :, :], cb[:, :, :], ce[:, :, :], ALU.add).then_inc(g_add.sem, 1)

    @s.piece("QS", "vector")
    def _(e, i):
        e.wait_ge(g_add.sem, g_add.at(i))
        e.tensor_tensor(catq[:, :, :], total2[:, :, :], ce[:, :, :], ALU.subtract).then_inc(v_q.sem, 1)

    @s.piece("O", "tensor")
    def _(e, i):
        e.wait_ge(v_q.sem, v_q.at(i))
        n = 0
        for kind in range(2):
            for h in range(4):
                for hl in range(2):
                    w = wp[:, hl, bass.ds((i % J) * 4 + 16 * kind + h, 1), :].rearrange("p h o -> p (h o)")
                    last = e.matmul(O[1][:, 0:D], catq[:, 4 * kind + h, :], w, start=(n == 0), stop=(n == 15))
                    n += 1
        last.then_inc(pe_out.sem, 1)

    @s.piece("O", "vector")
    def _(e, i):
        e.wait_ge(pe_out.sem, pe_out.at(i))
        row = x[:, bass.ds(i // J, 1), :].rearrange("p b d -> p (b d)")
        e.scalar_tensor_tensor(row, O[1][:, 0:D], out_gate[:, 0:1], row, ALU.mult, ALU.add).then_inc(v_x.sem, 1)

    N = B * J
    with nc.Block() as block:
        s.run_pipelined(block, lambda owner: order(ORDER1[owner]), N, 1, 2)



NE = 8
W_UP = 64.0
GROUP = 4
GT = GROUP * P


def layer1_experts(nc, a, t, ctx):
    def sb(name, shape, dt=F32):
        return ctx.enter_context(nc.sbuf_tensor(name, shape, dt))

    x, gates, ident = t["x"], t["gates"], t["ident"]
    bank = [ctx.enter_context(nc.psum_tensor(f"ps2_{n}", [P, 512], F32)) for n in range(8)]
    win = sb("w_in", [P, 2, NE, KD, FF], F16)
    wout = sb("w_out", [P, 2, NE, KF, D], F16)
    wr = sb("w_router", [P, KD, NE])
    rT = sb("rowsT", [P, KD, 2, B * P], F16)
    gate = sb("gate", [P, B, NE])

    r = Pieces(nc)
    only_here = ExitStack()

    def rb(name, shape, dt=F32):
        return only_here.enter_context(nc.sbuf_tensor(name, shape, dt))

    NRAW = 4
    raw = rb("raw2", [P, NRAW, 2048])
    items = []
    for name, w in (("winT", win), ("woutT", wout)):
        for n in range(NE // 2):
            for_two = slice(2 * n, 2 * n + 2)
            parts = [w[:, hl, for_two, :, :].rearrange("p e k n -> p (e k n)") for hl in range(2)]
            items.append((a[name].rearrange("e (k p) n -> p e k n", p=P)[:, for_two], 2048, parts, W_UP))
    parting = Parting(nc, "w2", raw, items)
    stats, mv, rstd, spare = rb("stats_m", [P, 2, 6]), rb("mv_m", [P, 2, 2]), rb("rstd_m", [P, 2]), rb("spare_m", [P, 1])
    rows, u = rb("rows_m", [P, 2, D]), rb("rowsT32", [P, 2, KD, P])
    logit = rb("logit", [P, B, NE])
    small, made = nc.alloc_semaphore("w2_small"), nc.alloc_semaphore("w2_made")
    r_stat, r_rstd, r_n = r.flag("m_stat", "vector"), r.flag("m_rstd", "gpsimd"), r.flag("m_n", "vector")
    r_T, r_u, r_hi = r.flag("m_T", "tensor", 1, 2), r.flag("m_u", "scalar"), r.flag("m_hi", "scalar", 1, 2)
    r_lo, r_lg, r_out = r.flag("m_lo", "vector", 1, 2), r.flag("m_lg", "tensor", 1, 2), r.flag("m_out", "vector", 1, 2)
    c_1, c_1g = Chain(nc, "c_m1", 1), Chain(nc, "c_m1g", 1)

    @r.piece("1", "vector")
    def _(e, n, b):
        i = 2 * n + b
        c_1.start(e, i)
        c_1.link(e.bn_stats(stats[:, b, :], x[:, i, :]))
        e.memset(spare[:, :], 0.0)
        e.bn_aggr(mv[:, b, :], stats[:, b, :]).then_inc(r_stat.sem, 1)
        c_1.end()

    @r.piece("1", "gpsimd")
    def _(e, n, b):
        i = 2 * n + b
        c_1g.start(e, i)
        e.wait_ge(r_stat.sem, r_stat.at(i))
        c_1g.link(e.tensor_tensor(rstd[:, b:b + 1], mv[:, b, 1:2], t["eps"][:, 0:1], ALU.add))
        e.tensor_tensor(rstd[:, b:b + 1], rstd[:, b:b + 1], t["half"][:, 0:1], ALU.pow).then_inc(r_rstd.sem, 1)
        c_1g.end()

    @r.piece("2", "vector")
    def _(e, n, b):
        i = 2 * n + b
        e.wait_ge(r_rstd.sem, r_rstd.at(i))
        e.wait_ge(r_T.sem, r_T.at(i - 2))
        e.tensor_scalar(rows[:, b, :], x[:, i, :], mv[:, b, 0:1], rstd[:, b:b + 1], ALU.subtract,
                        ALU.mult).then_inc(r_n.sem, 1)

    @r.piece("2", "tensor")
    def _(e, n, b):
        i = 2 * n + b
        e.wait_ge(r_n.sem, r_n.at(i))
        e.wait_ge(r_hi.sem, r_hi.at(i - 2))
        for k in range(KD):
            last = e.transpose(bank[b][:, k * P:(k + 1) * P], rows[:, b, k * P:(k + 1) * P], ident[:, :])
        last.then_inc(r_T.sem, 1)

    @r.piece("2", "scalar")
    def _(e, n, b):
        i = 2 * n + b
        e.wait_ge(r_T.sem, r_T.at(i))
        e.wait_ge(r_lg.sem, r_lg.at(i - 2))
        e.wait_ge(r_lo.sem, r_lo.at(i - 2))
        at = bass.ds(i * P, P)
        src = bank[b][:, 0:D].rearrange("p (k t) -> p k t", k=KD)
        e.activation(u[:, b, :, :], src, ACT.Copy).then_inc(r_u.sem, 1)
        e.activation(rT[:, :, 0, at], src, ACT.Copy).then_inc(r_hi.sem, 1)

    @r.piece("2L", "vector")
    def _(e, n, b):
        i = 2 * n + b
        e.wait_ge(r_hi.sem, r_hi.at(i))
        at = bass.ds(i * P, P)
        e.tensor_tensor(rT[:, :, 1, at], u[:, b, :, :], rT[:, :, 0, at], ALU.subtract).then_inc(r_lo.sem, 1)

    @r.piece("3", "tensor")
    def _(e, n, b):
        i = 2 * n + b
        e.wait_ge(r_u.sem, r_u.at(i))
        e.wait_ge(r_out.sem, r_out.at(i - 2))
        for k in range(KD):
            last = e.matmul(bank[2 + b][:, 0:NE], u[:, b, k, :], wr[:, k, :], start=(k == 0), stop=(k == KD - 1))
        last.then_inc(r_lg.sem, 1)

    @r.piece("3", "vector")
    def _(e, n, b):
        i = 2 * n + b
        e.wait_ge(r_lg.sem, r_lg.at(i))
        e.tensor_copy(logit[:, i, :], bank[2 + b][:, 0:NE]).then_inc(r_out.sem, 1)

    @r.piece("W", "sync")
    def _(e, n):
        e.dma_start(wr[:, :, :], a["WrT"].rearrange("(k p) n -> p k n", p=P)).then_inc(small, 16)
        parting.load(e)

    @r.piece("W", "scalar")
    def _(e, n):
        for m in range(len(items)):
            parting.wait_load(e, m)
            parting.high_part(e, m)
        parting.wait_high(e, len(items) - 1)

    @r.piece("W", "vector")
    def _(e, n):
        for m in range(len(items)):
            parting.wait_high(e, m)
            parting.low_part(e, m)
        parting.wait_low(e, len(items) - 1)

    @r.piece("start", "tensor")
    def _(e, n):
        e.wait_ge(small, 16)

    number = rb("number", [P, B, NE])
    same, first, second = rb("same", [P, B, NE]), rb("first", [P, B, NE]), rb("second", [P, B, NE])
    hide = rb("hide", [P, B, NE])
    most, place, gap = rb("most", [P, 2, B]), rb("place", [P, 2, B]), rb("gap", [P, 3, B])
    c_g = Chain(nc, "c_gates", 17)
    g_d, g_e = nc.alloc_semaphore("gap_done"), nc.alloc_semaphore("gap_exp")

    @r.piece("start", "gpsimd")
    def _(e, n):
        for m in range(NE):
            e.memset(number[:, :, m:m + 1].rearrange("p b n -> p (b n)"), float(NE - m))
        e.memset(hide[:, :, :], MASKED).then_inc(made, 1)
        e.wait_ge(made, 1)

    @r.piece("G", "vector")
    def _(e, n):
        c_g.start(e, 0)
        e.wait_ge(r_out.sem, r_out.at(B - 1))
        e.wait_ge(made, 1)
        for which, out in ((0, first), (1, second)):
            c_g.link(e.tensor_reduce(most[:, which, :], logit[:, :, :], AX, ALU.max))
            c_g.link(e.tensor_tensor(same[:, :, :], logit[:, :, :], spread(most[:, which, :], NE), ALU.is_equal))
            c_g.link(e.tensor_tensor(same[:, :, :], same[:, :, :], number[:, :, :], ALU.mult))
            c_g.link(e.tensor_reduce(place[:, which, :], same[:, :, :], AX, ALU.max))
            c_g.link(e.tensor_tensor(out[:, :, :], number[:, :, :], spread(place[:, which, :], NE), ALU.is_equal))
            if which == 0:
                c_g.link(e.tensor_tensor(same[:, :, :], out[:, :, :], hide[:, :, :], ALU.mult))
                c_g.link(e.tensor_tensor(logit[:, :, :], logit[:, :, :], same[:, :, :], ALU.add))
        e.tensor_tensor(gap[:, 0, :], most[:, 1, :], most[:, 0, :], ALU.subtract).then_inc(g_d, 1)
        e.wait_ge(g_e, 1)
        c_g.link(e.tensor_scalar(gap[:, 2, :], gap[:, 1, :], 1.0, None, ALU.add))
        c_g.link(e.reciprocal(gap[:, 2, :], gap[:, 2, :]))
        c_g.link(e.tensor_scalar(gap[:, 2, :], gap[:, 2, :], gates[:, 3:4], 1.0 / W_UP, ALU.mult, ALU.mult))
        e.tensor_tensor(first[:, :, :], first[:, :, :], spread(gap[:, 2, :], NE), ALU.mult)
        c_g.link(e.tensor_tensor(second[:, :, :], second[:, :, :], spread(gap[:, 2, :], NE), ALU.mult))
        c_g.link(e.tensor_tensor(second[:, :, :], second[:, :, :], spread(gap[:, 1, :], NE), ALU.mult))
        e.tensor_tensor(gate[:, :, :], first[:, :, :], second[:, :, :], ALU.add)
        c_g.end()

    @r.piece("G", "scalar")
    def _(e, n):
        e.wait_ge(g_d, 1)
        e.activation(gap[:, 1, :], gap[:, 0, :], ACT.Exp).then_inc(g_e, 1)

    rows_order = {"vector": "2L:1- 2:1 1:0+ 3:1- 2L:0 2:0+ 1:1+ 3:0", "tensor": "3:1- 2:1 3:0 2:0+",
                  "scalar": "2:1 2:0+", "gpsimd": "1:0+ 1:1+", "sync": ""}

    def rows_body(owner, n, nxt=True, prev=True):
        return [(name, n + shift, item) for name, shift, item in order(rows_order[owner])
                if shift == 0 or (nxt if shift == 1 else prev)]

    with nc.Block() as block:
        last = B // 2 - 1
        r.run(block, lambda owner: ([("start", 0), ("W", 0)] if owner == "sync" else [("start", 0)]) + order("1:0 1:1 2:0")
              + rows_body(owner, 0, prev=False),
              rows_body, lambda owner: rows_body(owner, last, nxt=False) + [("2L", last, 1), ("3", last, 1), ("G", 0)] + (
                  [] if owner == "sync" else [("W", 0)]), (1, last))
    only_here.close()

    s = Pieces(nc)
    Hb, Y = bank[0:4], bank[4:8]
    h32 = sb("h32", [P, KF, GT])
    hh = sb("hidden", [P, 2, 2, KF, GT], F16)
    pe_H, a_h, v_hi, v_lo = (s.flag("pe_H", "tensor", KF), s.flag("a_h", "scalar", KF),
                             s.flag("v_hi", "vector", KF), s.flag("v_lo", "vector", KF))
    pe_Y, v_Y = s.flag("pe_Y", "tensor", GROUP, 2), s.flag("v_Y", "vector", GROUP)

    @s.piece("H", "tensor")
    def _(e, i, b):
        rows_at = bass.ds((i // NE) * GT, GT)
        for m in range(KF):
            e.wait_ge(a_h.sem, a_h.at(i - 1, m + 1))
            for k in range(KD):
                for part, hl in ((0, 0), (0, 1), (1, 0)):
                    w = win[:, hl, bass.ds(i % NE, 1), k, m * P:(m + 1) * P].rearrange("p e n -> p (e n)")
                    last = e.matmul(Hb[m][:, :], w, rT[:, k, part, rows_at], start=(k == 0 and part == hl == 0),
                                    stop=(k == KD - 1 and part == 1))
            last.then_inc(pe_H.sem, 1)

    @s.piece("H", "scalar")
    def _(e, i, b):
        for m in range(KF):
            e.wait_ge(pe_H.sem, pe_H.at(i, m + 1))
            e.wait_ge(v_lo.sem, v_lo.at(i - 1, m + 1))
            e.activation(h32[:, m, :], Hb[m][:, :], ACT.Silu, scale=1.0 / W_UP).then_inc(a_h.sem, 1)

    @s.piece("H", "vector")
    def _(e, i, b):
        e.wait_ge(pe_Y.sem, pe_Y.at(i - 2))
        for m in range(KF):
            e.wait_ge(a_h.sem, a_h.at(i, m + 1))
            e.tensor_copy(hh[:, b, 0, m, :], h32[:, m, :]).then_inc(v_hi.sem, 1)
            e.wait_ge(v_hi.sem, v_hi.at(i, m + 1))
            e.tensor_tensor(hh[:, b, 1, m, :], h32[:, m, :], hh[:, b, 0, m, :], ALU.subtract).then_inc(v_lo.sem, 1)

    @s.piece("Y", "tensor")
    def _(e, i, b):
        for q in range(GROUP):
            e.wait_ge(v_Y.sem, v_Y.at(i - 1, q + 1))
            for m in range(KF):
                if q == 0:
                    e.wait_ge(v_lo.sem, v_lo.at(i, m + 1))
                for part, hl in ((0, 0), (0, 1), (1, 0)):
                    w = wout[:, hl, bass.ds(i % NE, 1), m, :].rearrange("p e n -> p (e n)")
                    last = e.matmul(Y[q][:, 0:D], hh[:, b, part, m, q * P:(q + 1) * P], w,
                                    start=(m == 0 and part == hl == 0), stop=(m == KF - 1 and part == 1))
            last.then_inc(pe_Y.sem, 1)

    @s.piece("Y", "vector")
    def _(e, i, b):
        for q in range(GROUP):
            e.wait_ge(pe_Y.sem, pe_Y.at(i, q + 1))
            at = (i // NE) * GROUP + q
            row = x[:, bass.ds(at, 1), :].rearrange("p b d -> p (b d)")
            g = gate[:, bass.ds(at, 1), bass.ds(i % NE, 1)].rearrange("p b e -> p (b e)")
            e.scalar_tensor_tensor(row, Y[q][:, 0:D], g, row, ALU.mult, ALU.add).then_inc(v_Y.sem, 1)

    N = NE * B // GROUP

    def pair(n):
        return [("H", 2 * n + 1, 1), ("Y", 2 * n, 0), ("H", 2 * n + 2, 0), ("Y", 2 * n + 1, 1)]

    with nc.Block() as block:
        s.run_alike(block, [("H", 0, 0)], pair, [("H", N - 1, 1), ("Y", N - 2, 0), ("Y", N - 1, 1)], (0, N // 2 - 1))


def store_rows(nc, t, out):
    done = nc.alloc_semaphore("stored")
    with nc.Block() as block:
        @block.sync
        def _(e):
            e.dma_start(out.rearrange("b p d -> p b d"), t["x"][:, :, :]).then_inc(done, 16)
            e.wait_ge(done, 16)


def program(nc, a, out, phases):
    t = prepare_common(nc, a)
    with ExitStack() as ctx:
        if phases[0]:
            layer0(nc, a, t, ctx)
    with ExitStack() as ctx:
        if phases[1]:
            layer1_attention(nc, a, t, ctx)
    with ExitStack() as ctx:
        if phases[2]:
            layer1_experts(nc, a, t, ctx)
    store_rows(nc, t, out)




def hadamard(n):
    h = np.ones((1, 1), np.float32)
    while h.shape[0] < n:
        h = np.block([[h, h], [h, -h]])
    return np.ascontiguousarray(h, np.float32)


def lay_out(v):
    a = {}
    a["x"] = v["x"]
    a["ctxT"] = v["ctx_2048"].reshape(B * P, D).T
    a["g_xattn"], a["g_ffn"] = v["g_xattn"], v["g_ffn"]
    a["causal"] = v["mask_SxS2_bc0"]
    a["padding"] = v["mask_BxS2_bk0"]
    a["WqT"] = v["L0_xattn_Wq"].T
    a["bq"] = v["L0_xattn_bq"].reshape(KD, P).T
    wk = np.broadcast_to(v["L0_xattn_Wk"].reshape(G0, 1, HD0, D), (G0, R0, HD0, D))
    a["WkT"] = wk.reshape(G0 * R0 * HD0, D).T
    bk = np.broadcast_to(v["L0_xattn_bk"].reshape(G0, 1, HD0), (G0, R0, HD0))
    a["bk"] = bk.reshape(KD, P).T
    a["WvT"] = v["L0_xattn_Wv"].T
    a["bv"] = v["L0_xattn_bv"]
    a["bo"] = v["L0_xattn_bo"]
    wo = v["L0_xattn_Wo"].reshape(D, 2, 4, 1, R0, HD0).transpose(1, 2, 3, 5, 4, 0)
    a["WoT"] = np.broadcast_to(wo, (2, 4, 4, HD0, R0, D)).reshape(2, P, R0, D)
    a["w_upT"] = v["L0_ffn_w_up"].T
    a["w_downT"] = v["L0_ffn_w_down"].T
    a["had256"], a["had128"] = hadamard(D), hadamard(P)
    rows = np.arange(P)
    a["low_row"] = -(rows[:, None] % GP >= GP // 2).astype(np.float32)
    a["high_row"] = (rows[:, None] % GP < GP // 2).astype(np.float32)
    a["pick"] = ((rows[:, None] // HD0) % R0 == np.arange(R0)[None, :]).astype(np.float32)
    a["in_scales"] = np.stack([v[f"L1_xattn_{n}_in_scale"] for n in ("q", "qx", "k", "v")], axis=1)
    a["ln_w"], a["ln_b"] = v["L1_xattn_ln_w"].reshape(KD, P).T, v["L1_xattn_ln_b"].reshape(KD, P).T
    a["w_scales"] = np.stack([v[f"L1_xattn_{n}_scale"] for n in ("wq", "wqx", "wk", "wv", "proj_w")])
    a["proj_in_scale"] = v["L1_xattn_proj_in_scale"].reshape(1)
    a["head_ln"] = np.stack([v[f"L1_xattn_{n}ln_{c}"] for n in ("q", "qx", "k", "kx") for c in "wb"], axis=1)
    a["smooth"] = v["L1_xattn_proj_smooth"].reshape(32, P).T
    for n in ("wq", "wqx", "wk", "wv"):
        a[n + "T"] = v["L1_xattn_" + n].T
    a["wkxT"], a["wvxT"] = v["L1_xattn_w_kv_x"][:G1 * HD1].T, v["L1_xattn_w_kv_x"][G1 * HD1:].T
    a["WrT"] = v["L1_ffn_Wr"].T
    a["winT"], a["woutT"] = v["L1_ffn_Win"].transpose(0, 2, 1), v["L1_ffn_Wout"].transpose(0, 2, 1)
    a["wprojT"] = v["L1_xattn_wproj"].T
    return {k: np.ascontiguousarray(x) for k, x in a.items()}


PHASES = (1, 1, 1)


def kernel(**inputs):
    import concourse.bacc as bacc
    from concourse.bass_utils import run_bass_kernel_spmd

    nc = bacc.Bacc("TRN2", target_bir_lowering=False, num_devices=1)
    arrays = {f"in_{k}": x for k, x in lay_out(inputs).items()}
    aps = {k[3:]: nc.dram_tensor(k, x.shape, mybir.dt.from_np(x.dtype), kind="ExternalInput").ap()
           for k, x in arrays.items()}
    out = nc.dram_tensor("out_0", (B, P, D), F32, kind="ExternalOutput").ap()
    program(nc, aps, out, PHASES)
    r = run_bass_kernel_spmd(nc, [arrays], core_ids=[0])
    return r.results[0]["out_0"]
```
